# Optimizing a Trainium2 kernel written in Bass

```python
import numpy as np
import jax
import jax.numpy as jnp

def _softmax(x, axis=-1):
    return jax.nn.softmax(x, axis=axis)

def _gelu(x):
    return jax.nn.gelu(x, approximate=True)

def _silu(x):
    return jax.nn.silu(x)

def _sigmoid(x):
    return jax.nn.sigmoid(x)

def _layernorm(x, axis=-1, eps=1e-05):
    m = jnp.mean(x, axis=axis, keepdims=True)
    v = jnp.var(x, axis=axis, keepdims=True)
    return (x - m) / jnp.sqrt(v + eps)

def _scatter_add(tgt, idx, src, axis=0):
    return tgt.at[idx].add(src)

def _segment_sum(src, seg, n):
    return jax.ops.segment_sum(src, seg, n)
kernel_name = 'mk_prb_d1_jaxref_r4_a9d5df'

def setup_inputs(seed: int=0):
    np.random.seed(seed)
    _w = jnp.asarray

    def _L0_attn_setup():
        import jax, jax.numpy as jnp
        import numpy as np
        B, T, C = (8, 512, 256)
        H = 4 * C
        N_LAYER, LAYER_ID = (12, 2)
        K_CLAMP = 60.0
        LN_EPS = 1e-05

        def _ln(x, g, b):
            m = jnp.mean(x, axis=-1, keepdims=True)
            v = jnp.var(x, axis=-1, keepdims=True)
            return (x - m) * jax.lax.rsqrt(v + LN_EPS) * g + b

        def _mix(x, time_mix, combined_mix):
            c = x.shape[-1]
            xm1 = jnp.pad(x[:, :-1], ((0, 0), (1, 0), (0, 0)))
            xp1 = jnp.pad(x[:, 1:], ((0, 0), (0, 1), (0, 0)))
            xc = jnp.concatenate([xm1[..., :c // 2], xp1[..., c // 2:]], axis=-1)
            return x * time_mix + xm1 * (1.0 - time_mix) + xc * combined_mix

        def _wkv(time_decay, time_first, k, v):
            ed = jnp.exp(-jnp.exp(time_decay))
            eu = jnp.exp(time_first)

            def step(carry, kv_t):
                a, b = carry
                kt, vt = kv_t
                y = (a + eu * kt * vt) / (b + eu * kt)
                return ((ed * a + kt * vt, ed * b + kt), y)
            kT = jnp.swapaxes(k, 0, 1)
            vT = jnp.swapaxes(v, 0, 1)
            z = jnp.zeros_like(kT[0])
            _, y = jax.lax.scan(step, (z, z), (kT, vT))
            return jnp.swapaxes(y, 0, 1)

        def _time_mix_block(x, time_mix, combined_mix, time_decay, time_first, Wk, Wv, Wr, Wo):
            xm = _mix(x, time_mix, combined_mix)
            k = jnp.exp(jnp.minimum(xm @ Wk.T, K_CLAMP))
            v = xm @ Wv.T
            r = xm @ Wr.T
            wkv = _wkv(time_decay, time_first, k, v)
            return jax.nn.sigmoid(r) * wkv @ Wo.T

        def _channel_mix_block(x, time_mix, combined_mix, Fk, Fv, Fr):
            xm = _mix(x, time_mix, combined_mix)
            k = jnp.square(jax.nn.relu(xm @ Fk.T))
            kv = k @ Fv.T
            return jax.nn.sigmoid(xm @ Fr.T) * kv
        key = jax.random.key(seed)
        ks = jax.random.split(key, 9)
        s = 0.02
        x = jax.random.normal(ks[0], (B, T, C), jnp.float32)
        h = np.arange(C, dtype=np.float64)
        frac = (LAYER_ID - 1) / (N_LAYER - 2)
        f1 = 3.0 + frac * (1.2 - 3.0)
        f2 = 0.65 + frac * (0.4 - 0.65)
        decay_speed = np.power(f2, h / (C - 1) * 7.0) * f1
        tm = jnp.concatenate([jnp.zeros(C // 2), jnp.ones(C // 2)]).reshape(1, 1, C).astype(jnp.float32)
        return dict(x=x, ln1_g=jnp.ones((C,), jnp.float32), ln1_b=jnp.zeros((C,), jnp.float32), ln2_g=jnp.ones((C,), jnp.float32), ln2_b=jnp.zeros((C,), jnp.float32), att_time_mix=tm, att_combined_mix=jnp.full((1, 1, C), 0.01, jnp.float32), time_decay=jnp.asarray(np.log(decay_speed), jnp.float32), time_first=jnp.full((C,), float(np.log(0.3)), jnp.float32), Wk=jax.random.normal(ks[1], (C, C), jnp.float32) * s, Wv=jax.random.normal(ks[2], (C, C), jnp.float32) * s, Wr=jax.random.normal(ks[3], (C, C), jnp.float32) * s, Wo=jax.random.normal(ks[4], (C, C), jnp.float32) * s, ffn_time_mix=tm, ffn_combined_mix=jnp.full((1, 1, C), 0.01, jnp.float32), Fk=jax.random.normal(ks[5], (H, C), jnp.float32) * s, Fv=jax.random.normal(ks[6], (C, H), jnp.float32) * s, Fr=jax.random.normal(ks[7], (C, C), jnp.float32) * s)
    _L0_attn_in = _L0_attn_setup()

    def _L0_ffn_setup():
        import jax, jax.numpy as jnp
        import numpy as np
        import math
        B, L, D = (4, 1024, 256)
        F = 1024
        E = 16
        CAP_FACTOR = 1.0
        EPS = 1e-05
        key = jax.random.key(seed)
        ks = jax.random.split(key, 8)
        std = 0.02
        return {'x': jax.random.normal(ks[0], (B, L, D), dtype=jnp.float32), 'norm_weight': jnp.ones((D,), dtype=jnp.float32), 'router_weight': jax.random.normal(ks[1], (E, D), dtype=jnp.float32) * std, 'router_bias': jnp.zeros((E,), dtype=jnp.float32), 'fc1_weight': jax.random.normal(ks[2], (E, F, D), dtype=jnp.float32) * std, 'fc1_bias': jnp.zeros((E, F), dtype=jnp.float32), 'fc2_weight': jax.random.normal(ks[3], (E, D, F), dtype=jnp.float32) * std, 'fc2_bias': jnp.zeros((E, D), dtype=jnp.float32)}
    _L0_ffn_in = _L0_ffn_setup()
    _d = {'L0_attn_x': _L0_attn_in['x'], 'L0_attn_ln1_g': _L0_attn_in['ln1_g'], 'L0_attn_ln1_b': _L0_attn_in['ln1_b'], 'L0_attn_ln2_g': _L0_attn_in['ln2_g'], 'L0_attn_ln2_b': _L0_attn_in['ln2_b'], 'L0_attn_att_time_mix': _L0_attn_in['att_time_mix'], 'L0_attn_att_combined_mix': _L0_attn_in['att_combined_mix'], 'L0_attn_time_decay': _L0_attn_in['time_decay'], 'L0_attn_time_first': _L0_attn_in['time_first'], 'L0_attn_Wk': _L0_attn_in['Wk'], 'L0_attn_Wv': _L0_attn_in['Wv'], 'L0_attn_Wr': _L0_attn_in['Wr'], 'L0_attn_Wo': _L0_attn_in['Wo'], 'L0_attn_ffn_time_mix': _L0_attn_in['ffn_time_mix'], 'L0_attn_ffn_combined_mix': _L0_attn_in['ffn_combined_mix'], 'L0_attn_Fk': _L0_attn_in['Fk'], 'L0_attn_Fv': _L0_attn_in['Fv'], 'L0_attn_Fr': _L0_attn_in['Fr'], 'L0_ffn_norm_weight': _L0_ffn_in['norm_weight'], 'L0_ffn_router_weight': _L0_ffn_in['router_weight'], 'L0_ffn_router_bias': _L0_ffn_in['router_bias'], 'L0_ffn_fc1_weight': _L0_ffn_in['fc1_weight'], 'L0_ffn_fc1_bias': _L0_ffn_in['fc1_bias'], 'L0_ffn_fc2_weight': _L0_ffn_in['fc2_weight'], 'L0_ffn_fc2_bias': _L0_ffn_in['fc2_bias']}
    _x0 = _d['L0_attn_x']
    _d['L0_attn_x'] = jax.random.normal(jax.random.fold_in(jax.random.key(seed), 1), (8, 512, 256), dtype=_x0.dtype)
    del _x0
    return _d

def reference(L0_attn_x, L0_attn_ln1_g, L0_attn_ln1_b, L0_attn_ln2_g, L0_attn_ln2_b, L0_attn_att_time_mix, L0_attn_att_combined_mix, L0_attn_time_decay, L0_attn_time_first, L0_attn_Wk, L0_attn_Wv, L0_attn_Wr, L0_attn_Wo, L0_attn_ffn_time_mix, L0_attn_ffn_combined_mix, L0_attn_Fk, L0_attn_Fv, L0_attn_Fr, L0_ffn_norm_weight, L0_ffn_router_weight, L0_ffn_router_bias, L0_ffn_fc1_weight, L0_ffn_fc1_bias, L0_ffn_fc2_weight, L0_ffn_fc2_bias):

    def _L0_attn_ref(x, ln1_g, ln1_b, ln2_g, ln2_b, att_time_mix, att_combined_mix, time_decay, time_first, Wk, Wv, Wr, Wo, ffn_time_mix, ffn_combined_mix, Fk, Fv, Fr):
        import jax, jax.numpy as jnp
        import numpy as np
        B, T, C = (8, 512, 256)
        H = 4 * C
        N_LAYER, LAYER_ID = (12, 2)
        K_CLAMP = 60.0
        LN_EPS = 1e-05

        def _ln(x, g, b):
            m = jnp.mean(x, axis=-1, keepdims=True)
            v = jnp.var(x, axis=-1, keepdims=True)
            return (x - m) * jax.lax.rsqrt(v + LN_EPS) * g + b

        def _mix(x, time_mix, combined_mix):
            c = x.shape[-1]
            xm1 = jnp.pad(x[:, :-1], ((0, 0), (1, 0), (0, 0)))
            xp1 = jnp.pad(x[:, 1:], ((0, 0), (0, 1), (0, 0)))
            xc = jnp.concatenate([xm1[..., :c // 2], xp1[..., c // 2:]], axis=-1)
            return x * time_mix + xm1 * (1.0 - time_mix) + xc * combined_mix

        def _wkv(time_decay, time_first, k, v):
            ed = jnp.exp(-jnp.exp(time_decay))
            eu = jnp.exp(time_first)

            def step(carry, kv_t):
                a, b = carry
                kt, vt = kv_t
                y = (a + eu * kt * vt) / (b + eu * kt)
                return ((ed * a + kt * vt, ed * b + kt), y)
            kT = jnp.swapaxes(k, 0, 1)
            vT = jnp.swapaxes(v, 0, 1)
            z = jnp.zeros_like(kT[0])
            _, y = jax.lax.scan(step, (z, z), (kT, vT))
            return jnp.swapaxes(y, 0, 1)

        def _time_mix_block(x, time_mix, combined_mix, time_decay, time_first, Wk, Wv, Wr, Wo):
            xm = _mix(x, time_mix, combined_mix)
            k = jnp.exp(jnp.minimum(xm @ Wk.T, K_CLAMP))
            v = xm @ Wv.T
            r = xm @ Wr.T
            wkv = _wkv(time_decay, time_first, k, v)
            return jax.nn.sigmoid(r) * wkv @ Wo.T

        def _channel_mix_block(x, time_mix, combined_mix, Fk, Fv, Fr):
            xm = _mix(x, time_mix, combined_mix)
            k = jnp.square(jax.nn.relu(xm @ Fk.T))
            kv = k @ Fv.T
            return jax.nn.sigmoid(xm @ Fr.T) * kv
        x = _ln(x, ln1_g, ln1_b)
        x = x + _time_mix_block(x, att_time_mix, att_combined_mix, time_decay, time_first, Wk, Wv, Wr, Wo)
        x = _ln(x, ln2_g, ln2_b)
        x = x + _channel_mix_block(x, ffn_time_mix, ffn_combined_mix, Fk, Fv, Fr)
        return x

    def _L0_ffn_ref(x, norm_weight, router_weight, router_bias, fc1_weight, fc1_bias, fc2_weight, fc2_bias):
        import jax, jax.numpy as jnp
        import numpy as np
        import math
        B, L, D = (4, 1024, 256)
        F = 1024
        E = 16
        CAP_FACTOR = 1.0
        EPS = 1e-05
        b, l, d = x.shape
        n_tokens = b * l
        n_experts = router_weight.shape[0]
        capacity = max(1, math.ceil(CAP_FACTOR * n_tokens / n_experts))
        top_k = min(capacity, n_tokens)
        xf = x.reshape(n_tokens, d)
        rms = jnp.sqrt(jnp.mean(xf * xf, axis=-1, keepdims=True) + EPS)
        xn = xf / rms * norm_weight
        logits = xn @ router_weight.T + router_bias
        probs = jax.nn.softmax(logits, axis=-1)
        _, idx = jax.lax.top_k(logits.T, top_k)
        xe = xn[idx]
        h = jnp.einsum('ecd,efd->ecf', xe, fc1_weight) + fc1_bias[:, None, :]
        h = jax.nn.gelu(h, approximate=False)
        y = jnp.einsum('ecf,edf->ecd', h, fc2_weight) + fc2_bias[:, None, :]
        gates = jnp.take_along_axis(probs.T, idx, axis=1)
        flat_idx = idx.reshape(-1)
        contrib = (y * gates[:, :, None]).reshape(-1, d)
        output = jnp.zeros((n_tokens, d), dtype=x.dtype).at[flat_idx].add(contrib)
        gate_sums = jnp.zeros((n_tokens, 1), dtype=x.dtype).at[flat_idx].add(gates.reshape(-1, 1))
        assigned = gate_sums > 0
        output = jnp.where(assigned, output / jnp.where(assigned, gate_sums, 1.0), output)
        return output.reshape(b, l, d)
    x = L0_attn_x
    xn = _layernorm(x, axis=-1)
    x = x + _L0_attn_ref(xn, L0_attn_ln1_g, L0_attn_ln1_b, L0_attn_ln2_g, L0_attn_ln2_b, L0_attn_att_time_mix, L0_attn_att_combined_mix, L0_attn_time_decay, L0_attn_time_first, L0_attn_Wk, L0_attn_Wv, L0_attn_Wr, L0_attn_Wo, L0_attn_ffn_time_mix, L0_attn_ffn_combined_mix, L0_attn_Fk, L0_attn_Fv, L0_attn_Fr) + _L0_ffn_ref(xn, L0_ffn_norm_weight, L0_ffn_router_weight, L0_ffn_router_bias, L0_ffn_fc1_weight, L0_ffn_fc1_bias, L0_ffn_fc2_weight, L0_ffn_fc2_bias)
    return x

_drawn_inputs = setup_inputs


def setup_inputs(seed=0):
    import zlib

    import numpy as np

    out = dict(_drawn_inputs(seed))
    spreads = {'L0_attn_ln1_g': (1.0, 0.2),
     'L0_attn_ln1_b': (0.0, 0.1),
     'L0_attn_ln2_g': (1.0, 0.2),
     'L0_attn_ln2_b': (0.0, 0.1),
     'L0_attn_att_combined_mix': (0.009999999776482582, 0.6),
     'L0_attn_time_first': (-1.2039728164672852, 0.6),
     'L0_attn_ffn_combined_mix': (0.009999999776482582, 0.6),
     'L0_ffn_norm_weight': (1.0, 0.2),
     'L0_ffn_router_bias': (0.0, 2.0),
     'L0_ffn_fc1_bias': (0.0, 0.643),
     'L0_ffn_fc2_bias': (0.0, 0.34)}
    factors = {'L0_attn_att_time_mix': 7.018,
     'L0_attn_time_decay': 7.518,
     'L0_attn_Wk': 8.0,
     'L0_attn_Wv': 3.934,
     'L0_attn_Wr': 8.0,
     'L0_attn_Wo': 3.948,
     'L0_attn_ffn_time_mix': 3.169,
     'L0_attn_Fk': 2.783,
     'L0_attn_Fr': 8.0}
    for name, (base, spread) in spreads.items():
        noise = np.random.default_rng([zlib.crc32(name.encode()), seed]).standard_normal(out[name].shape)
        drawn = base * np.exp(spread * noise) if base else spread * noise
        out[name] = jnp.asarray(drawn.astype(out[name].dtype))
    for name, factor in factors.items():
        out[name] = (out[name] * factor).astype(out[name].dtype)
    return out
```

```python
import numpy as np
import concourse.bass as bass
from concourse import mybir
from contextlib import ExitStack

F32, F32R, BF16, I32 = mybir.dt.float32, mybir.dt.float32r, mybir.dt.bfloat16, mybir.dt.int32
U32 = mybir.dt.uint32
ALU, ACT, AX = mybir.AluOpType, mybir.ActivationFunctionType, mybir.AxisListType

P = 128
NSEQ, T, C = 8, 512, 256
N = NSEQ * T
CC = C // P
TT = T // P
NT = N // P
H = 4 * C
HF = H // P
E, F, CAP = 16, 1024, N // 16
FF = F // P
HALVES = CAP // P
SEG = P // E
ROW = C + E
EPS = 1e-5
K_CLAMP = 60.0
MAG_BITS = 31
STEPS = 5
DVE_PASS = 39

(LN1_G, LN1_B, LN2_G, LN2_B, TM1, CM1, TM2, CM2, DECAY, FIRST, NORM_W) = range(11)
IDENT, BLOCK, TRI = 0, P, 2 * P
IOTA16 = 3 * P
PCOL = IOTA16 + 16
TILE = PCOL + 1
DIAG = TILE + NT
NCONST = DIAG + 8


def build(nc, x, params, w_proj, w_fk, w_fv, router_w, router_b, fc1, fc1_b, fc2, fc2_b, const, bits_i, bits_f, out):
    rows = nc.dram_tensor("token_rows", (N, ROW), F32).ap()
    logit_rows = nc.dram_tensor("logit_rows", (NSEQ, E, T), F32).ap()
    index_rows = nc.dram_tensor("index_rows", (E, CAP), F32).ap()

    ctx = ExitStack()
    with ctx:
        def sb(name, shape, dt=F32):
            return ctx.enter_context(nc.sbuf_tensor(name, shape, dt))

        def sem(name):
            return ctx.enter_context(nc.semaphore(name))

        prm = sb("prm", [P, 11, CC])
        cst = sb("cst", [P, NCONST])
        bit_i = sb("bit_i", [P, 48], I32)
        bit_f = sb("bit_f", [P, 48])
        ident = cst[:, IDENT:IDENT + P]
        shift1 = sb("shift1", [P, CC])
        shift2 = sb("shift2", [P, CC])
        decay = sb("decay", [P, CC])
        first = sb("first", [P, CC])
        rw = sb("rw", [P, CC, E])
        rwn = sb("rwn", [P, CC, E])
        rb = sb("rb", [E, 1])
        gates = sb("gates", [P, NT * E])
        xsel = sb("xsel", [P, T])
        xs = sb("xs", [P, T])
        sgn = sb("sgn", [P, 8])
        cand = sb("cand", [P, 2], I32)
        rej = sb("rej", [P, 1], I32)
        cnt = sb("cnt", [P, 2])
        idx = sb("idx", [P, 2 * E], U32)
        stat = sb("stat", [P, 10, NT])
        st = sb("st", [P, NT, 6])
        st2 = sb("st2", [P, TT, 6])
        sm = sb("sm", [P, 8, TT])
        negh = sb("negh", [P, NT])
        junk = sb("junk", [P, T], BF16)
        hr = [sb(f"hr{i}", [P, T]) for i in range(2)]

        wproj_h = sb("wproj_h", [P, 5, CC, C], F32R)
        wproj_l = sb("wproj_l", [P, 5, CC, C], F32R)
        wfk_h = sb("wfk_h", [P, CC, H], F32R)
        wfk_l = sb("wfk_l", [P, CC, H], F32R)
        xm1_h = sb("xm1_h", [P, CC, T], F32R)
        xm1_l = sb("xm1_l", [P, CC, T], F32R)
        xm2_h = sb("xm2_h", [P, CC, T], F32R)
        xm2_l = sb("xm2_l", [P, CC, T], F32R)
        y_h = sb("y_h", [P, CC, T], F32R)
        y_l = sb("y_l", [P, CC, T], F32R)
        wfv = sb("wfv", [P, HF, C])
        zT = sb("zT", [P, CC * N])
        zT_c = zT[:, :].rearrange("p (c n) -> p c n", c=CC)
        hid = sb("hid", [P, HF, T])

        ARENA = 19340
        arena = sb("arena", [P, ARENA])
        at = [0]

        def take(n):
            at[0] += n
            assert at[0] <= ARENA, at[0]
            return arena[:, at[0] - n:at[0]]

        x1p = [take(CC * (T + 2)).rearrange("p (c t) -> p c t", c=CC) for _ in range(2)]
        def chunks():
            return take(CC * T).rearrange("p (c t) -> p c t", c=CC)
        u1, u2, xm, ek, th, kv, num, den, x2T, thf, x4T = (chunks() for _ in range(11))
        ap = take(CC * (T + 1)).rearrange("p (c t) -> p c t", c=CC)
        bp = take(CC * (T + 1)).rearrange("p (c t) -> p c t", c=CC)
        x3p = take(CC * (T + 2)).rearrange("p (c t) -> p c t", c=CC)
        xres, obuf = (take(TT * C).rearrange("p (j c) -> p j c", j=TT) for _ in range(2))
        z2 = x4T.rearrange("p c t -> p (c t)").rearrange("p (j c) -> p j c", j=TT)
        at[0] = 0
        xall = take(NT * C)
        zst = [take(TT * C).rearrange("p (j c) -> p j c", j=TT) for _ in range(2)]
        raw_proj = take(5 * CC * C).rearrange("p (w c o) -> p w c o", w=5, c=CC)
        raw_fk = take(CC * H).rearrange("p (c o) -> p c o", c=CC)
        lgs = [take(T)[0:E] for _ in range(2)]
        at[0] = 0
        gt, eq, eqpre, mask, pre, pos = (take(T) for _ in range(6))
        ones = take(T)
        lt, ex, pt, pm, mt = (take(NT * E) for _ in range(5))
        ph_i, pl_i = (take(NT * E).bitcast(I32) for _ in range(2))
        ph, pl = (take(NT * E // 2).bitcast(BF16) for _ in range(2))
        smx = take(4 * NT).rearrange("p (k n) -> p k n", k=4)
        iota_b = take(8).bitcast(BF16)
        tile_b = take(NT // 2).bitcast(BF16)
        onehot = hid[:, :, :].rearrange("p f t -> p (f t)").bitcast(BF16)
        place = take(NT * E * 16).bitcast(BF16)
        diag = take(2 * P).rearrange("p (e k) -> p e k", e=8)
        ids = take(2 * 32).rearrange("p (g k) -> p g k", g=2)
        idf = take(32).rearrange("p (g k) -> p g k", g=2)
        idr = take(P)[0:2 * E]
        at[0] = 0
        w1 = [zT[:, 0:2048].rearrange("p (c f) -> p c f", c=CC), zT[:, 4096:6144].rearrange("p (c f) -> p c f", c=CC)]
        w2 = [zT[:, 2048:4096].rearrange("p (f d) -> p f d", f=FF), zT[:, 6144:8192].rearrange("p (f d) -> p f d", f=FF)]
        xe = [take(HALVES * ROW).rearrange("p (h r) -> p h r", h=HALVES) for _ in range(2)]
        xeT = [take(CC * CAP).rearrange("p (c n) -> p c n", c=CC) for _ in range(2)]
        he = [take(FF * CAP).rearrange("p (f n) -> p f n", f=FF) for _ in range(2)]
        ye = [take(HALVES * C).rearrange("p (h d) -> p h d", h=HALVES) for _ in range(2)]
        yg = [take(HALVES * C).rearrange("p (h d) -> p h d", h=HALVES) for _ in range(2)]
        b2 = [take(C) for _ in range(2)]
        b1f = take(E * FF)
        b1 = b1f.rearrange("p (e f) -> p e f", e=E)
        idx2 = sb("idx2", [P, 2, 2], U32)

        ps = [ctx.enter_context(nc.psum_tensor(f"pair{i}", [P, 2, T], F32)) for i in range(4)]
        K_, V_, R_, O_ = ps

        const_in, proj_in, fk_in, fv_in, router_in, b1_in = (sem(n) for n in (
            "const_in", "proj_in", "fk_in", "fv_in", "router_in", "b1_in"))
        x_in = [sem(f"x_in{g}") for g in range(4)]
        dve_done, act_done, pool_done = sem("dve_done"), sem("act_done"), sem("pool_done")
        zero_done, var_ready, rstd_ready, var2_ready, rstd2_ready = (sem(n) for n in (
            "zero_done", "var_ready", "rstd_ready", "var2_ready", "rstd2_ready"))
        arena_b, mixing_ready = sem("arena_b"), sem("mixing_ready")
        z_ready, zT_psum, zT_ready = sem("z_ready"), sem("zT_psum"), sem("zT_ready")
        lg_psum, lg_ready = sem("lg_psum"), sem("lg_ready")
        z_stored = [sem("z_stored0"), sem("z_stored1")]
        lg_stored = [sem("lg_stored0"), sem("lg_stored1")]
        xsel_in = sem("xsel_in")
        x1_ready, u1_ready, xm1_ready, u1_used = sem("x1_ready"), sem("u1_ready"), sem("xm1_ready"), sem("u1_used")
        k_done, r_done, v_done = sem("k_done"), sem("r_done"), sem("v_done")
        ek_ready, th_ready, v_used, th_used = sem("ek_ready"), sem("th_ready"), sem("v_used"), sem("th_used")
        y_ready, wo_done, x2_ready, x2tok = sem("y_ready"), sem("wo_done"), sem("x2_ready"), sem("x2tok")
        v2_ready, r2_ready, ln2_ready = sem("v2_ready"), sem("r2_ready"), sem("ln2_ready")
        z2_ready, z2T_done, u2_ready, xm2_ready = sem("z2_ready"), sem("z2T_done"), sem("u2_ready"), sem("xm2_ready")
        fr_done, thf_ready, fk_done, relu_done, h_ready, fv_done = (sem(n) for n in (
            "fr_done", "thf_ready", "fk_done", "relu_done", "h_ready", "fv_done"))
        clamp_ready = sem("clamp_ready")
        x3_ready, rwn_ready = sem("x3_ready"), sem("rwn_ready")
        x4_ready, x4tok, out_ready = sem("x4_ready"), sem("x4tok"), sem("out_ready")
        xres_in, out_stored = sem("xres_in"), sem("out_stored")
        cnt_ready, total_done = sem("cnt_ready"), sem("total_done")
        tok_psum, exp_ready, gates_ready, gates_stored = (sem(n) for n in (
            "tok_psum", "exp_ready", "gates_ready", "gates_stored"))
        sub_ready = sem("sub_ready")
        tail_cnt, tail_psum, onehots_ready, ids_psum = (sem(n) for n in (
            "tail_cnt", "tail_psum", "onehots_ready", "ids_psum"))
        ids_ready, ids_stored, idr_in, idT_psum, idx_ready = (sem(n) for n in (
            "ids_ready", "ids_stored", "idr_in", "idT_psum", "idx_ready"))
        w1_in, w2_in, b2_in = ([sem(f"{n}_in{i}") for i in range(2)] for n in ("w1", "w2", "b2"))
        idx2_early, idx2_ready = sem("idx2_early"), sem("idx2_ready")
        rows_in = [sem("rows_in0"), sem("rows_in1")]
        xeT_psum, xeT_ready, fc1_done, he_ready, fc2_done, ye_ready, yg_ready = (sem(n) for n in (
            "xeT_psum", "xeT_ready", "fc1_done", "he_ready", "fc2_done", "ye_ready", "yg_ready"))
        added = sem("added")

        def product3(o, wh, wl, xh, xl, start, stop):
            nc.tensor.matmul(o, wh, xh, start=start, stop=False)
            nc.tensor.matmul(o, wh, xl, start=False, stop=False)
            return nc.tensor.matmul(o, wl, xh, start=False, stop=stop)

        class Chain:
            def __init__(self, eng, s, per_round=()):
                self.eng, self.s, self.base, self.n = eng, s, 0, 0
                self.per_round = list(per_round)

            def step(self, ins):
                self.n += 1
                return ins.then_inc(self.s, 1)

            def join(self, behind=0):
                self.eng.wait_ge(self.s, self.base + (self.n - behind))

            def link(self, ins):
                self.step(ins)
                self.join()
                return ins

            def begin(self):
                self.start, self.base, self.n = self.base + self.n, 0, 0
                self.per, self.i = self.per_round.pop(0), 0

            def round(self, i):
                assert self.i == 0 or self.n == self.per, (self.n, self.per)
                self.base, self.n, self.i = self.start + i * self.per, 0, 1

            def end(self, rounds):
                assert self.n == self.per, (self.n, self.per)
                self.base, self.n = self.start + rounds * self.per, 0

        def after(eng, signal, value):
            if not (isinstance(value, int) and value <= 0):
                eng.wait_ge(signal, value)

        def tell(eng, ins, signal, value):
            ins.then_inc(signal, 1)
            eng.wait_ge(signal, value)

        def passes(eng, chain, body):
            chain.begin()
            with eng.Fori(0, (NSEQ - 2) // 2) as j:
                for k in range(2):
                    chain.round(2 * j + k)
                    body(1 + 2 * j + k, (1 + k) % 2)
            chain.round(NSEQ - 2)
            body(NSEQ - 1, (NSEQ - 1) % 2)

        def pairs(eng, chain, n, body):
            chain.begin()
            for k in range(2):
                chain.round(k)
                body(k, k, True)
            with eng.Fori(1, n // 2) as j:
                for k in range(2):
                    chain.round(2 * j + k)
                    body(2 * j + k, k, False)
            chain.end(n)

        block = ctx.enter_context(nc.Block())

        @block.sync
        def _(sp):
            x_t = x.rearrange("(g t p) c -> g p t c", g=4, p=P)
            sp.dma_start(cst[:, :], const).then_inc(const_in, 16)
            sp.dma_start(prm[:, :, :], params).then_inc(const_in, 16)
            for g in range(4):
                sp.dma_start(xall[:, g * 2048:(g + 1) * 2048].rearrange("p (t c) -> p t c", c=C), x_t[g]).then_inc(x_in[g], 16)
            sp.dma_start(rw[:, :, :], router_w).then_inc(router_in, 16)
            sp.dma_start(rb[:, :], router_b).then_inc(router_in, 16)
            sp.dma_start(bit_i[:, :], bits_i).then_inc(router_in, 16)
            sp.dma_start(bit_f[:, :], bits_f).then_inc(router_in, 16)
            sp.dma_start(raw_proj, w_proj).then_inc(proj_in, 16)
            sp.dma_start(raw_fk, w_fk).then_inc(fk_in, 16)
            sp.dma_start(wfv[:, :, :], w_fv).then_inc(fv_in, 16)
            z_rows = rows.rearrange("(b j p) r -> b p j r", b=NSEQ, p=P)
            with sp.Fori(0, NSEQ // 2) as j:
                for k in range(2):
                    sp.wait_ge(z_ready, 2 * j + k + 1)
                    sp.dma_start(z_rows[bass.ds(2 * j + k, 1), :, :, 0:C].rearrange("b p j r -> (b p) j r"), zst[k]).then_inc(z_stored[k], 16)
                    sp.wait_ge(lg_ready, 2 * j + k + 1)
                    sp.dma_start(logit_rows[bass.ds(2 * j + k, 1), :, :].rearrange("b e t -> (b e) t"), lgs[k]).then_inc(lg_stored[k], 16)
            for k in range(2):
                sp.wait_ge(lg_stored[k], 16 * NSEQ // 2)
                sp.wait_ge(z_stored[k], 16 * NSEQ // 2)
            sp.dma_start(xsel[:, :], logit_rows.rearrange("b e t -> (b e) t")).then_inc(xsel_in, 16)
            x_b = x.rearrange("(b j p) c -> b p j c", b=NSEQ, p=P)
            out_b = out.rearrange("(b j p) c -> b p j c", b=NSEQ, p=P)
            sp.wait_ge(arena_b, 1)
            sp.dma_start(xres, x_b[0]).then_inc(xres_in, 16)
            with sp.Fori(0, NSEQ - 1) as b:
                sp.wait_ge(out_ready, b + 1)
                sp.dma_start(out_b[bass.ds(b, 1), :, :, :].rearrange("b p j c -> (b p) j c"), obuf).then_inc(out_stored, 16)
                sp.wait_ge(out_stored, 16 * (b + 1))
                sp.dma_start(xres, x_b[bass.ds(b + 1, 1), :, :, :].rearrange("b p j c -> (b p) j c")).then_inc(xres_in, 16)
            sp.wait_ge(out_ready, NSEQ)
            sp.dma_start(out_b[NSEQ - 1], obuf).then_inc(out_stored, 16)
            sp.wait_ge(u1_ready, NSEQ)
            for k in range(2):
                sp.dma_start(w1[k], fc1[k]).then_inc(w1_in[k], 16)
                sp.dma_start(w2[k], fc2[k]).then_inc(w2_in[k], 16)
            sp.wait_ge(out_stored, 16 * NSEQ)
            sp.wait_ge(gates_ready, 1)
            gate_rows = rows.rearrange("(s q p) r -> p q s r", s=SEG, p=P)
            for q in range(TT):
                sp.dma_start(gate_rows[:, q, :, C:ROW],
                             gates[:, q * SEG * E:(q + 1) * SEG * E].rearrange("p (s e) -> p s e", e=E)).then_inc(gates_stored, 16)
            sp.wait_ge(ids_ready, 1)
            ids_v = index_rows.rearrange("(g e) (h l) -> (e h) g l", g=2, l=16)
            for g in range(2):
                sp.dma_start(ids_v[:, g, :], idf[:, g, :]).then_inc(ids_stored, 16)
            sp.wait_ge(ids_stored, 32)
            sp.dma_start(idr, index_rows.rearrange("e (h n) -> (e h) n", n=P)).then_inc(idr_in, 16)
            sp.wait_ge(idx_ready, 1)
            sp.dma_start(b1, fc1_b).then_inc(b1_in, 16)
            for k in range(2):
                sp.dma_start(b2[k], fc2_b[k:k + 1, :].to_broadcast([P, C])).then_inc(b2_in[k], 16)
            with sp.Fori(1, E // 2) as j:
                for k in range(2):
                    e = 2 * j + k
                    sp.wait_ge(fc2_done, e - 1)
                    sp.dma_start(w1[k], fc1[bass.ds(e, 1), :, :, :].rearrange("e p c f -> (e p) c f")).then_inc(w1_in[k], 16)
                    sp.dma_start(w2[k], fc2[bass.ds(e, 1), :, :, :].rearrange("e p f d -> (e p) f d")).then_inc(w2_in[k], 16)
                    sp.wait_ge(ye_ready, e - 1)
                    sp.dma_start(b2[k], fc2_b[bass.ds(e, 1), :].to_broadcast([P, C])).then_inc(b2_in[k], 16)

        @block.gpsimd
        def _(pool):
            ch = Chain(pool, pool_done, [0])
            G = nc.gpsimd
            pool.wait_ge(zero_done, 1)
            pool.wait_ge(var_ready, 1)
            G.tensor_tensor(stat[:, 4, :], stat[:, 3, :], negh[:, :], ALU.pow).then_inc(rstd_ready, 1)
            pool.wait_ge(var2_ready, 1)
            G.tensor_tensor(stat[:, 6, :], stat[:, 5, :], negh[:, :], ALU.pow).then_inc(rstd2_ready, 1)
            with pool.Fori(0, NSEQ) as b:
                pool.wait_ge(v2_ready, b + 1)
                G.tensor_tensor(sm[:, 5, :], sm[:, 4, :], negh[:, 0:TT], ALU.pow).then_inc(r2_ready, 1)
            for q in range(1):
                pool.wait_ge(gates_stored, 16 * TT)
                pool.wait_ge(idx_ready, 1)
                pool.wait_ge(out_stored, 16 * NSEQ)

            def scatter(e, k):
                pool.wait_ge(idx_ready, 1)
                pool.wait_ge(yg_ready, e + 1)
                after(pool, added, 2 * 16 * e)
                for h in range(HALVES):
                    G.indirect_dma_start(out=out, out_offset=bass.IndirectOffsetOnAxis(ap=idx2[:, k, h:h + 1], axis=0),
                                         in_=yg[k][:, h, :], in_offset=None, compute_op=ALU.add).then_inc(added, 16)

            def slot(e, k, early):
                if not early:
                    pool.wait_ge(yg_ready, e - 1)
                    pool.wait_ge(added, 2 * 16 * (e - 1))
                G.tensor_copy(idx2[:, k, :], idx[:, bass.ds(2 * e, 2)]).then_inc(idx2_early if early else idx2_ready, 1)
                pool.wait_ge(idx_ready, 1)
                pool.wait_ge(*((idx2_early, e + 1) if early else (idx2_ready, e - 1)))
                for h in range(HALVES):
                    G.indirect_dma_start(out=xe[k][:, h, :], out_offset=None, in_=rows,
                                         in_offset=bass.IndirectOffsetOnAxis(ap=idx2[:, k, h:h + 1], axis=0)).then_inc(rows_in[k], 16)
                if not (early and k == 0):
                    scatter(e - 1, 1 - k)

            pairs(pool, ch, E, slot)
            scatter(E - 1, 1)
            pool.wait_ge(added, 2 * 16 * E)

        @block.scalar
        def _(act):
            ch = Chain(act, act_done, [0, 2, 0])
            A = nc.scalar
            act.wait_ge(const_in, 32)
            ch.link(A.activation(decay[:, :], prm[:, DECAY, :], ACT.Exp))
            ch.link(A.activation(decay[:, :], decay[:, :], ACT.Exp, scale=-1.0))
            A.activation(first[:, :], prm[:, FIRST, :], ACT.Exp).then_inc(mixing_ready, 1)
            act.wait_ge(router_in, 64)

            def stage_a(b, k, early):
                pair = (K_, V_)[k]
                act.wait_ge(zT_psum, b + 1)
                A.activation(zT_c[:, :, bass.ds(b * T, T)], pair[:, :, :], ACT.Copy).then_inc(zT_ready, 1)
                act.wait_ge(lg_psum, b + 1)
                if not early:
                    act.wait_ge(lg_stored[k], 8 * (b - k))
                A.activation(lgs[k], R_[0:E, k, :], ACT.Identity, bias=rb[:, 0:1]).then_inc(lg_ready, 1)

            pairs(act, ch, NSEQ, stage_a)

            def mix_in(b, k):
                for c in range(CC):
                    ch.step(A.activation(x1p[k][:, c, 1:T + 1], zT_c[:, c, bass.ds(b * T, T)], ACT.Identity,
                                         scale=prm[:, LN1_G, c:c + 1], bias=prm[:, LN1_B, c:c + 1]))
                ch.join()
                for c in range(CC):
                    last = A.activation(u1[:, c, :], x1p[k][:, c, 1:T + 1], ACT.Copy, scale=prm[:, TM1, c:c + 1])
                last.then_inc(u1_ready, 1)

            def attention(b):
                act.wait_ge(clamp_ready, b + 1)
                A.activation(ek, ek, ACT.Exp).then_inc(ek_ready, 1)
                act.wait_ge(r_done, b + 1)
                after(act, y_ready, b)
                A.activation(th, R_[:, :, :], ACT.Tanh, scale=0.5).then_inc(th_ready, 1)

            def ffn(b):
                act.wait_ge(fr_done, b + 1)
                A.activation(thf, R_[:, :, :], ACT.Tanh, scale=0.5).then_inc(thf_ready, 1)
                for f in range(HF + 1):
                    if f < HF:
                        if f >= 2:
                            act.wait_ge(h_ready, b * HF + f - 1)
                        act.wait_ge(fk_done, b * HF + f + 1)
                        A.activation(hr[f % 2][:, :], K_[:, f % 2, :], ACT.Relu).then_inc(relu_done, 1)
                    if f > 0:
                        act.wait_ge(relu_done, b * HF + f)
                        A.activation(hid[:, f - 1, :], hr[(f - 1) % 2][:, :], ACT.Square).then_inc(h_ready, 1)

            def norm2(b):
                act.wait_ge(ln2_ready, b + 1)
                after(act, z2T_done, b)
                for j in range(TT):
                    last = A.activation(z2[:, j, :], K_[:, j // 2, (j % 2) * C:(j % 2 + 1) * C], ACT.Identity,
                                        scale=sm[:, 5, j:j + 1], bias=sm[:, 6, j:j + 1])
                last.then_inc(z2_ready, 1)
                act.wait_ge(z2T_done, b + 1)
                after(act, x4_ready, b)
                for c in range(CC):
                    last = A.activation(x3p[:, c, 1:T + 1], V_[:, c, :], ACT.Identity,
                                        scale=prm[:, LN2_G, c:c + 1], bias=prm[:, LN2_B, c:c + 1])
                last.then_inc(x3_ready, 1)
                act.wait_ge(x3_ready, b + 1)
                after(act, xm2_ready, b)
                for c in range(CC):
                    last = A.activation(u2[:, c, :], x3p[:, c, 1:T + 1], ACT.Copy, scale=prm[:, TM2, c:c + 1])
                last.then_inc(u2_ready, 1)

            act.wait_ge(arena_b, 1)
            mix_in(0, 0)
            attention(0)
            mix_in(1, 1)
            norm2(0)

            def one(b, k):
                attention(b)
                last_one = isinstance(b, int)
                if not last_one:
                    act.wait_ge(x2_ready, b)
                    act.wait_ge(xm1_ready, b + 1)
                    mix_in(b + 1, 1 - k)
                ffn(b - 1)
                norm2(b)

            passes(act, ch, one)
            ffn(NSEQ - 1)
            act.wait_ge(sub_ready, 1)
            A.activation(ex, lt, ACT.Exp).then_inc(exp_ready, 1)
            act.wait_ge(b1_in, 16)

            def slot(e, k, early):
                act.wait_ge(xeT_psum, e + 1)
                if not early:
                    act.wait_ge(fc1_done, 4 * (e - 1))
                for c in range(CC):
                    last = A.activation(xeT[k][:, c, :], K_[:, k, c * CAP:(c + 1) * CAP], ACT.Copy,
                                        scale=prm[:, NORM_W, c:c + 1])
                last.then_inc(xeT_ready, 1)
                if not early:
                    act.wait_ge(fc2_done, e - 1)
                for fp in range(FF // 2):
                    act.wait_ge(fc1_done, 4 * e + fp + 1)
                    bank = (V_, R_)[fp // 2]
                    for i in range(2):
                        last = A.activation(he[k][:, 2 * fp + i, :], bank[:, fp % 2, i * CAP:(i + 1) * CAP], ACT.Gelu,
                                            bias=b1f[:, bass.ds(e * FF + 2 * fp + i, 1)])
                    last.then_inc(he_ready, 1)

            pairs(act, ch, E, slot)

        @block.tensor
        def _(pe):
            ch = Chain(pe, act_done, [0, 0, 0])
            M = nc.tensor
            pe.wait_ge(const_in, 32)

            def stage_a(b, k, early):
                pair = (K_, V_)[k]
                pe.wait_ge(z_ready, b + 1)
                if not early:
                    pe.wait_ge(zT_ready, b - 1)
                for j in range(TT):
                    for c in range(CC):
                        last = M.transpose(pair[:, c, j * P:(j + 1) * P], zst[k][:, j, c * P:(c + 1) * P], ident)
                last.then_inc(zT_psum, 1)
                pe.wait_ge(zT_ready, b + 1)
                if early and k == 0:
                    pe.wait_ge(rwn_ready, 1)
                if not early:
                    pe.wait_ge(lg_ready, b - 1)
                for c in range(CC):
                    last = M.matmul(R_[0:E, k, :], rwn[:, c, :], zT_c[:, c, bass.ds(b * T, T)], start=(c == 0), stop=(c == CC - 1))
                last.then_inc(lg_psum, 1)

            pairs(pe, ch, NSEQ, stage_a)

            def total():
                return M.matmul(V_[:, 0, 0:1], cst[:, BLOCK:BLOCK + P], cnt[:, 0:1], start=True, stop=True)

            pe.wait_ge(cnt_ready, 1)
            total().then_inc(total_done, 1)

            def project(w, out_pair, sig):
                for m in range(CC):
                    for c in range(CC):
                        o = slice(m * P, (m + 1) * P)
                        last = product3(out_pair[:, m, :], wproj_h[:, w, c, o], wproj_l[:, w, c, o],
                                        *(v[:, c, :] for v in ((y_h, y_l) if w == 3 else (xm2_h, xm2_l) if w == 4 else (xm1_h, xm1_l))),
                                        start=(c == 0), stop=(c == CC - 1))
                last.then_inc(sig, 1)

            def kvr(b):
                pe.wait_ge(xm1_ready, b + 1)
                after(pe, z2_ready, b)
                project(0, K_, k_done)
                project(2, R_, r_done)
                after(pe, u2_ready, b)
                project(1, V_, v_done)

            def hidden_out(b, f):
                pe.wait_ge(h_ready, b * HF + f + 1)
                for m in range(CC):
                    last = M.matmul(O_[:, m, :], wfv[:, f, m * P:(m + 1) * P], hid[:, f, :], start=(f == 0), stop=(f == HF - 1))
                return last

            def ffn(b, search):
                pe.wait_ge(xm2_ready, b + 1)
                if search:
                    pe.wait_ge(th_ready, b + 2)
                project(4, R_, fr_done)
                for f in range(HF):
                    if f >= 2:
                        pe.wait_ge(relu_done, b * HF + f - 1)
                    elif search and f == 0:
                        pe.wait_ge(ek_ready, b + 2)
                    for c in range(CC):
                        o = slice(f * P, (f + 1) * P)
                        last = product3(K_[:, f % 2, :], wfk_h[:, c, o], wfk_l[:, c, o], xm2_h[:, c, :], xm2_l[:, c, :],
                                        start=(c == 0), stop=(c == CC - 1))
                    last.then_inc(fk_done, 1)
                    if search and f % 2 == 0:
                        step_total(b, f // 2)
                    if f >= 2:
                        hidden_out(b, f - 2)
                if search:
                    step_total(b, 4)
                hidden_out(b, HF - 2)
                hidden_out(b, HF - 1).then_inc(fv_done, 1)

            def step_total(b, i):
                if i < STEPS:
                    pe.wait_ge(cnt_ready, b * STEPS + i + 2)
                    total().then_inc(total_done, 1)

            def attention_out(b):
                pe.wait_ge(y_ready, b + 1)
                project(3, V_, wo_done)

            def to_tokens(pair, src, sig):
                for j in range(TT):
                    for c in range(CC):
                        last = M.transpose(pair[:, j // 2, (j % 2) * C + c * P:(j % 2) * C + (c + 1) * P],
                                           src[:, c, j * P:(j + 1) * P], ident)
                last.then_inc(sig, 1)

            def x4_tokens(b):
                pe.wait_ge(x4_ready, b + 1)
                pe.wait_ge(thf_ready, b + 1)
                to_tokens(R_, x4T, x4tok)

            def norm2(b):
                pe.wait_ge(x2_ready, b + 1)
                after(pe, relu_done, HF * b)
                to_tokens(K_, x2T, x2tok)
                pe.wait_ge(z2_ready, b + 1)
                for c in range(CC):
                    for j in range(TT):
                        last = M.transpose(V_[:, c, j * P:(j + 1) * P], z2[:, j, c * P:(c + 1) * P], ident)
                last.then_inc(z2T_done, 1)

            kvr(0)
            pe.wait_ge(ek_ready, 1)
            attention_out(0)
            norm2(0)

            def one(b, k):
                kvr(b)
                ffn(b - 1, True)
                attention_out(b)
                x4_tokens(b - 1)
                norm2(b)

            passes(pe, ch, one)
            ffn(NSEQ - 1, False)
            x4_tokens(NSEQ - 1)

            for q in range(TT):
                last = M.transpose(K_[:, 0, q * P:(q + 1) * P], xsel[:, q * P:(q + 1) * P], ident)
            last.then_inc(tok_psum, 1)
            pe.wait_ge(tail_cnt, 1)
            M.matmul(V_[:, 0, 0:2], cst[:, BLOCK:BLOCK + P], cnt[:, 0:2], start=True, stop=True)
            M.matmul(V_[:, 0, 4:6], cst[:, TRI:TRI + P], cnt[:, 0:2], start=True, stop=True).then_inc(tail_psum, 1)
            pe.wait_ge(tail_cnt, 2)
            M.matmul(V_[:, 0, 0:1], cst[:, TRI:TRI + P], cnt[:, 0:1], start=True, stop=True).then_inc(tail_psum, 1)
            pe.wait_ge(tail_cnt, 3)
            for q in range(TT):
                last = M.transpose(V_[:, 1, q * P:(q + 1) * P], pos[:, q * P:(q + 1) * P], ident)
            last.then_inc(tail_psum, 1)
            pe.wait_ge(onehots_ready, 1)
            for n in range(NT):
                for g in range(2):
                    lo, hi = (n * E + g * 8) * 16, (n * E + g * 8 + 8) * 16
                    last = M.matmul(O_[:, g, 0:256], onehot[:, lo:hi], place[:, 2 * lo:2 * hi], start=(n == 0), stop=(n == NT - 1))
            last.then_inc(ids_psum, 1)
            pe.wait_ge(idr_in, 16)
            M.transpose(K_[:, 1, 0:2 * E], idr, cst[0:2 * E, IDENT:IDENT + 2 * E]).then_inc(idT_psum, 1)

            pe.wait_ge(idx_ready, 1)

            def back(e, k):
                pe.wait_ge(he_ready, 4 * (e + 1))
                pe.wait_ge(w2_in[k], 8 * (e - k) + 16)
                for h in range(HALVES):
                    for f in range(FF):
                        last = M.matmul(O_[:, k, h * C:(h + 1) * C], he[k][:, f, h * P:(h + 1) * P], w2[k][:, f, :],
                                        start=(f == 0), stop=(f == FF - 1))
                last.then_inc(fc2_done, 1)

            def slot(e, k, early):
                pe.wait_ge(rows_in[k], 16 * (e - k) + 32)
                if not early:
                    pe.wait_ge(xeT_ready, e - 1)
                for c in range(CC):
                    for h in range(HALVES):
                        last = M.transpose(K_[:, k, c * CAP + h * P:c * CAP + (h + 1) * P], xe[k][:, h, c * P:(c + 1) * P], ident)
                last.then_inc(xeT_psum, 1)
                pe.wait_ge(xeT_ready, e + 1)
                pe.wait_ge(w1_in[k], 8 * (e - k) + 16)
                for fp in range(FF // 2):
                    bank = (V_, R_)[fp // 2]
                    if not (early and k == 0):
                        pe.wait_ge(he_ready, 4 * (e - 1) + fp + 1)
                    for i in range(2):
                        f = 2 * fp + i
                        for c in range(CC):
                            last = M.matmul(bank[:, fp % 2, i * CAP:(i + 1) * CAP], w1[k][:, c, f * P:(f + 1) * P], xeT[k][:, c, :],
                                            start=(c == 0), stop=(c == CC - 1))
                    last.then_inc(fc1_done, 1)
                if not (early and k == 0):
                    back(e - 1, 1 - k)

            pairs(pe, ch, E, slot)
            back(E - 1, 1)

        @block.vector
        def _(dve):
            ch = Chain(dve, dve_done, [0, DVE_PASS, 0])
            V = nc.vector
            V.memset(negh[:, :], -0.5).then_inc(zero_done, 1)
            for g in range(4):
                dve.wait_ge(x_in[g], 16)
                for t in range(8 * g, 8 * g + 8):
                    ins = V.bn_stats(st[:, t, :], xall[:, t * C:(t + 1) * C])
            ch.link(ins)

            def moments(s, mean, dif, m2, var, tmp):
                ch.step(V.tensor_tensor(mean, s[:, :, 1], s[:, :, 4], ALU.add))
                ch.step(V.tensor_tensor(dif, s[:, :, 1], s[:, :, 4], ALU.subtract))
                ch.link(V.tensor_tensor(m2, s[:, :, 2], s[:, :, 5], ALU.add))
                ch.step(V.tensor_scalar(mean, mean, 0.5, None, ALU.mult))
                ch.link(V.scalar_tensor_tensor(tmp, dif, 0.25, dif, ALU.mult, ALU.mult))
                ch.link(V.scalar_tensor_tensor(var, m2, 1.0 / C, tmp, ALU.mult, ALU.add))

            moments(st, stat[:, 0, :], stat[:, 1, :], stat[:, 2, :], stat[:, 7, :], stat[:, 8, :])
            V.tensor_scalar(stat[:, 3, :], stat[:, 7, :], EPS, None, ALU.add).then_inc(var_ready, 1)
            dve.wait_ge(rstd_ready, 1)
            ch.link(V.tensor_tensor(stat[:, 8, :], stat[:, 7, :], stat[:, 4, :], ALU.mult))
            ch.link(V.tensor_tensor(stat[:, 8, :], stat[:, 8, :], stat[:, 4, :], ALU.mult))
            V.tensor_scalar(stat[:, 5, :], stat[:, 8, :], EPS, None, ALU.add).then_inc(var2_ready, 1)
            dve.wait_ge(const_in, 32)
            for sh, tm, cm in ((shift1, TM1, CM1), (shift2, TM2, CM2)):
                ch.link(V.tensor_scalar(sh[:, :], prm[:, tm, :], -1.0, 1.0, ALU.mult, ALU.add))
                ch.link(V.tensor_tensor(sh[:, 0:1], sh[:, 0:1], prm[:, cm, 0:1], ALU.add))
            dve.wait_ge(router_in, 64)
            for c in range(CC):
                ins = V.tensor_scalar(rwn[:, c, :], rw[:, c, :], prm[:, NORM_W, c:c + 1], None, ALU.mult)
            ins.then_inc(rwn_ready, 1)
            dve.wait_ge(rstd2_ready, 1)
            ch.link(V.tensor_tensor(stat[:, 8, :], stat[:, 4, :], stat[:, 6, :], ALU.mult))
            ch.link(V.scalar_tensor_tensor(stat[:, 9, :], stat[:, 0, :], -1.0, stat[:, 8, :], ALU.mult, ALU.mult))

            def stage_a(b, k, early):
                if not early:
                    dve.wait_ge(z_stored[k], 8 * (b - k))
                    dve.wait_ge(zT_psum, b - 1)
                for j in range(TT):
                    t = b * TT + j
                    ins = V.tensor_scalar(zst[k][:, j, :], xall[:, bass.ds(t * C, C)], stat[:, 8, bass.ds(t, 1)],
                                          stat[:, 9, bass.ds(t, 1)], ALU.mult, ALU.add)
                ins.then_inc(z_ready, 1)

            pairs(dve, ch, NSEQ, stage_a)

            dve.wait_ge(proj_in, 16)
            ch.link(V.tensor_scalar(raw_proj[:, 3, :, :], raw_proj[:, 3, :, :], 0.5, None, ALU.mult))
            ch.link(V.tensor_copy(wproj_h[:, :, :, :], raw_proj))
            ch.step(V.tensor_tensor(wproj_l[:, :, :, :], raw_proj, wproj_h[:, :, :, :].bitcast(F32), ALU.subtract))
            dve.wait_ge(fk_in, 16)
            ch.link(V.tensor_copy(wfk_h[:, :, :], raw_fk))
            ch.step(V.tensor_tensor(wfk_l[:, :, :], raw_fk, wfk_h[:, :, :].bitcast(F32), ALU.subtract))
            dve.wait_ge(fv_in, 16)
            ch.link(V.tensor_scalar(wfv[:, :, :], wfv[:, :, :], 0.5, None, ALU.mult))
            dve.wait_ge(zT_psum, NSEQ)
            for k in range(2):
                dve.wait_ge(z_stored[k], 8 * NSEQ)
                dve.wait_ge(lg_stored[k], 8 * NSEQ)
            for v in (*x1p, x3p):
                V.memset(v[:, :, 0:1], 0.0)
                V.memset(v[:, :, T + 1:T + 2], 0.0)
            V.memset(ap[:, :, 0:1], 0.0)
            tell(dve, V.memset(bp[:, :, 0:1], 0.0), arena_b, 1)

            dve.wait_ge(xsel_in, 16)
            V.tensor_scalar(junk[:, :], xsel[:, :], 0.0, None, ALU.is_ge, ALU.add, accum_out=cnt[:, 0:1]).then_inc(cnt_ready, 1)
            dve.wait_ge(total_done, 1)
            ch.link(V.tensor_scalar(sgn[:, 0:1], V_[:, 0, 0:1], float(CAP), None, ALU.is_ge))
            ch.step(V.tensor_scalar(sgn[:, 1:2], sgn[:, 0:1], 2.0, -1.0, ALU.mult, ALU.add))
            ch.link(V.tensor_scalar(sgn[:, 2:3], sgn[:, 0:1], float(CAP - (N - CAP + 1)), float(N - CAP + 1), ALU.mult, ALU.add))
            ch.step(V.tensor_scalar(xs[:, :], xsel[:, :], sgn[:, 1:2], None, ALU.mult))
            ch.link(V.tensor_copy(cand[:, 0:1], bit_i[:, 0:1]))

            def count():
                V.tensor_scalar(junk[:, :], xs[:, :], cand[:, 0:1].bitcast(F32), None, ALU.is_ge, ALU.add,
                                accum_out=cnt[:, 0:1]).then_inc(cnt_ready, 1)

            def decide(b, i):
                s = (b - 1) * STEPS + i
                dve.wait_ge(total_done, s + 2)
                ch.link(V.tensor_scalar(rej[:, :], V_[:, 0, 0:1], sgn[:, 2:3], bit_f[:, bass.ds(s, 1)], ALU.is_lt, ALU.mult))
                ch.link(V.scalar_tensor_tensor(cand[:, 0:1], rej[:, :], bit_i[:, bass.ds(s + 1, 1)], cand[:, 0:1],
                                               ALU.bitwise_xor, ALU.bitwise_xor))

            def mix(b, src, u, shift, cm, hi, lo, ready):
                ch.step(V.scalar_tensor_tensor(xm[:, 0, :], src[:, 0, 0:T], shift[:, 0:1], u[:, 0, :], ALU.mult, ALU.add))
                ch.link(V.scalar_tensor_tensor(xm[:, 1, :], src[:, 1, 0:T], shift[:, 1:2], u[:, 1, :], ALU.mult, ALU.add))
                ch.link(V.scalar_tensor_tensor(xm[:, 1, :], src[:, 1, 2:T + 2], prm[:, cm, 1:2], xm[:, 1, :], ALU.mult, ALU.add))
                ch.link(V.tensor_copy(hi[:, :, :], xm))
                tell(dve, V.tensor_tensor(lo[:, :, :], xm, hi[:, :, :].bitcast(F32), ALU.subtract), ready, b + 1)

            def wkv(b, search):
                dve.wait_ge(k_done, b + 1)
                V.tensor_scalar(ek, K_[:, :, :], K_CLAMP, None, ALU.min).then_inc(clamp_ready, 1)
                dve.wait_ge(ek_ready, b + 1)
                dve.wait_ge(v_done, b + 1)
                ch.link(V.tensor_tensor(kv, ek, V_[:, :, :], ALU.mult))
                if search:
                    count()
                for c in range(CC):
                    ch.step(V.tensor_tensor_scan(ap[:, c, 1:T + 1], decay[:, c:c + 1].to_broadcast([P, T]), kv[:, c, :], 0.0, ALU.mult, ALU.add))
                    ch.step(V.tensor_tensor_scan(bp[:, c, 1:T + 1], decay[:, c:c + 1].to_broadcast([P, T]), ek[:, c, :], 0.0, ALU.mult, ALU.add))
                if search:
                    decide(b, 0)
                    count()
                ch.join()
                for c in range(CC):
                    ch.step(V.scalar_tensor_tensor(num[:, c, :], kv[:, c, :], first[:, c:c + 1], ap[:, c, 0:T], ALU.mult, ALU.add))
                    ch.step(V.scalar_tensor_tensor(den[:, c, :], ek[:, c, :], first[:, c:c + 1], bp[:, c, 0:T], ALU.mult, ALU.add))
                if search:
                    decide(b, 1)
                    count()
                ch.join()
                dve.wait_ge(th_ready, b + 1)
                ch.step(V.scalar_tensor_tensor(num, th, 1.0, num, ALU.add, ALU.mult))
                ch.step(V.reciprocal(den, den))
                if search:
                    decide(b, 2)
                    count()
                ch.join()
                ch.link(V.tensor_tensor(kv, num, den, ALU.mult))
                if search:
                    decide(b, 3)
                    count()
                after(dve, wo_done, b)
                ch.link(V.tensor_copy(y_h[:, :, :], kv))
                if search:
                    decide(b, 4)
                tell(dve, V.tensor_tensor(y_l[:, :, :], kv, y_h[:, :, :].bitcast(F32), ALU.subtract), y_ready, b + 1)

            def mix1(b, k):
                dve.wait_ge(u1_ready, b + 1)
                mix(b, x1p[k], u1, shift1, CM1, xm1_h, xm1_l, xm1_ready)

            def ffn_end(b):
                dve.wait_ge(fv_done, b + 1)
                dve.wait_ge(thf_ready, b + 1)
                ch.link(V.scalar_tensor_tensor(x4T, thf, 1.0, O_[:, :, :], ALU.add, ALU.mult))
                tell(dve, V.tensor_tensor(x4T, x4T, x3p[:, :, 1:T + 1], ALU.add), x4_ready, b + 1)

            def ffn_out(b):
                dve.wait_ge(x4tok, b + 1)
                dve.wait_ge(xres_in, 16 * b + 16)
                tell(dve, V.tensor_tensor(obuf.rearrange("p (a j) c -> p a (j c)", a=2), R_[:, :, :],
                                        xres.rearrange("p (a j) c -> p a (j c)", a=2), ALU.add), out_ready, b + 1)

            def residual1(b, k):
                dve.wait_ge(wo_done, b + 1)
                tell(dve, V.tensor_tensor(x2T, V_[:, :, :], x1p[k][:, :, 1:T + 1], ALU.add), x2_ready, b + 1)

            def norm2(b):
                dve.wait_ge(x2tok, b + 1)
                after(dve, z2_ready, b)
                for j in range(TT):
                    ins = V.bn_stats(st2[:, j, :], K_[:, j // 2, (j % 2) * C:(j % 2 + 1) * C])
                ch.link(ins)
                moments(st2, sm[:, 0, :], sm[:, 1, :], sm[:, 2, :], sm[:, 3, :], sm[:, 7, :])
                V.tensor_scalar(sm[:, 4, :], sm[:, 3, :], EPS, None, ALU.add).then_inc(v2_ready, 1)
                dve.wait_ge(r2_ready, b + 1)
                tell(dve, V.scalar_tensor_tensor(sm[:, 6, :], sm[:, 0, :], -1.0, sm[:, 5, :], ALU.mult, ALU.mult), ln2_ready, b + 1)

            def mix2(b):
                dve.wait_ge(u2_ready, b + 1)
                mix(b, x3p, u2, shift2, CM2, xm2_h, xm2_l, xm2_ready)

            dve.wait_ge(mixing_ready, 1)
            mix1(0, 0)
            wkv(0, False)
            mix1(1, 1)
            residual1(0, 0)
            norm2(0)
            mix2(0)

            def one(b, k):
                wkv(b, True)
                if not isinstance(b, int):
                    mix1(b + 1, 1 - k)
                ffn_end(b - 1)
                residual1(b, k)
                ffn_out(b - 1)
                norm2(b)
                mix2(b)

            passes(dve, ch, one)
            ffn_end(NSEQ - 1)
            ffn_out(NSEQ - 1)

            def per_token(v):
                return v.rearrange("p (n e) -> p n e", e=E)

            def over_experts(v):
                return v.unsqueeze(2).to_broadcast([P, NT, E])

            dve.wait_ge(out_stored, 16 * NSEQ)
            dve.wait_ge(tok_psum, 1)
            ch.step(V.memset(ones, 1.0))
            logits = K_[:, 0, :].rearrange("p (n e) -> p n e", e=E)
            ch.link(V.tensor_reduce(smx[:, 0, :], logits, AX.X, ALU.max))
            tell(dve, V.tensor_tensor(per_token(lt), logits, over_experts(smx[:, 0, :]), ALU.subtract), sub_ready, 1)
            ch.link(V.tensor_scalar(sgn[:, 3:4], cand[:, 0:1].bitcast(F32), sgn[:, 1:2], None, ALU.mult))
            ch.step(V.tensor_scalar(gt, xsel[:, :], sgn[:, 3:4], None, ALU.is_gt, ALU.add, accum_out=cnt[:, 0:1]))
            tell(dve, V.tensor_scalar(eq, xsel[:, :], sgn[:, 3:4], None, ALU.is_equal, ALU.add, accum_out=cnt[:, 1:2]), tail_cnt, 1)
            dve.wait_ge(exp_ready, 1)
            ch.link(V.tensor_reduce(smx[:, 1, :], per_token(ex), AX.X, ALU.add))
            ch.link(V.reciprocal(smx[:, 1, :], smx[:, 1, :]))
            ch.link(V.tensor_tensor(per_token(pt), per_token(ex), over_experts(smx[:, 1, :]), ALU.mult))
            dve.wait_ge(tail_psum, 1)
            ch.step(V.tensor_scalar(sgn[:, 4:5], V_[:, 0, 0:1], -1.0, float(CAP), ALU.mult, ALU.add))
            ch.link(V.tensor_copy(sgn[:, 5:6], V_[:, 0, 5:6]))
            ch.link(V.tensor_tensor_scan(eqpre, ones, eq, sgn[:, 5:6], ALU.mult, ALU.add))
            ch.link(V.scalar_tensor_tensor(mt, eqpre, sgn[:, 4:5], eq, ALU.is_le, ALU.mult))
            ch.link(V.tensor_tensor(mask, mt, gt, ALU.add))
            tell(dve, V.tensor_scalar(pre, mask, 1.0, None, ALU.mult, ALU.add, accum_out=cnt[:, 0:1]), tail_cnt, 2)
            dve.wait_ge(tail_psum, 2)
            ch.link(V.tensor_copy(sgn[:, 6:7], V_[:, 0, 0:1]))
            ch.link(V.tensor_tensor_scan(pre, ones, mask, sgn[:, 6:7], ALU.mult, ALU.add))
            ch.link(V.tensor_tensor(pos, pre, mask, ALU.mult))
            tell(dve, V.tensor_scalar(pos, pos, -1.0, None, ALU.add), tail_cnt, 3)
            dve.wait_ge(tail_psum, 3)
            ch.step(V.tensor_scalar(mt, V_[:, 1, :], 0.0, None, ALU.is_ge))
            ch.link(V.tensor_copy(ph_i, V_[:, 1, :]))
            ch.step(V.tensor_scalar(pl_i, ph_i, 15, None, ALU.bitwise_and))
            ch.link(V.tensor_tensor(pm, pt, mt, ALU.mult))
            ch.step(V.tensor_scalar(ph_i, ph_i, 4, None, ALU.arith_shift_right))
            ch.step(V.tensor_copy(pl, pl_i))
            ch.link(V.tensor_reduce(smx[:, 2, :], per_token(pm), AX.X, ALU.add))
            ch.step(V.tensor_copy(ph, ph_i))
            ch.step(V.tensor_copy(iota_b, cst[:, IOTA16:IOTA16 + 16]))
            ch.step(V.tensor_copy(tile_b, cst[:, TILE:TILE + NT]))
            ch.link(V.scalar_tensor_tensor(smx[:, 3, :], smx[:, 2, :], 0.0, smx[:, 2, :], ALU.is_equal, ALU.add))
            ch.link(V.reciprocal(smx[:, 3, :], smx[:, 3, :]))
            tell(dve, V.tensor_tensor(per_token(gates[:, :]), per_token(pm), over_experts(smx[:, 3, :]), ALU.mult), gates_ready, 1)

            def sixteen(v):
                return v.unsqueeze(2).to_broadcast([P, NT * E, 16])

            iota_all = iota_b.unsqueeze(1).to_broadcast([P, NT * E, 16])
            place_v = place.rearrange("p (n k l) -> p n k l", k=2, l=16)
            ch.step(V.tensor_tensor(onehot.rearrange("p (n l) -> p n l", l=16), sixteen(ph), iota_all, ALU.is_equal))
            ch.link(V.tensor_tensor(place_v[:, :, 0, :], sixteen(pl), iota_all, ALU.is_equal))
            p5 = place.rearrange("p (n e k l) -> p n e k l", e=E, k=2, l=16)
            tiles = tile_b.unsqueeze(2).unsqueeze(3).to_broadcast([P, NT, E, 16])
            ch.link(V.tensor_tensor(p5[:, :, :, 1, :], p5[:, :, :, 0, :], tiles, ALU.mult))
            tell(dve, V.tensor_scalar(place_v[:, :, 0, :], place_v[:, :, 0, :], cst[:, PCOL:PCOL + 1], None, ALU.mult), onehots_ready, 1)
            dve.wait_ge(ids_psum, 1)
            for g in range(2):
                ch.link(V.tensor_tensor(diag, O_[:, g, 0:256].rearrange("p (e k) -> p e k", e=8),
                                        cst[:, DIAG:DIAG + 8].unsqueeze(2).to_broadcast([P, 8, 32]), ALU.mult))
                ch.link(V.tensor_reduce(ids[:, g, :], diag.rearrange("p e k -> p k e"), AX.X, ALU.add))
            tell(dve, V.scalar_tensor_tensor(idf, ids[:, :, 16:32], float(P), ids[:, :, 0:16], ALU.mult, ALU.add), ids_ready, 1)
            dve.wait_ge(idT_psum, 1)
            V.tensor_copy(idx[:, :], K_[:, 1, 0:2 * E]).then_inc(idx_ready, 1)

            def slot(e, k, early):
                dve.wait_ge(fc2_done, e + 1)
                dve.wait_ge(b2_in[k], 8 * (e - k) + 16)
                if not early:
                    dve.wait_ge(added, 2 * 16 * (e - 1))
                tell(dve, V.tensor_tensor(ye[k], O_[:, k, :].rearrange("p (h d) -> p h d", h=HALVES),
                                        b2[k].unsqueeze(1).to_broadcast([P, HALVES, C]), ALU.add), ye_ready, e + 1)
                for h in range(HALVES):
                    ins = V.tensor_scalar(yg[k][:, h, :], ye[k][:, h, :], xe[k][:, h, bass.ds(e + C, 1)], None, ALU.mult)
                ins.then_inc(yg_ready, 1)

            pairs(dve, ch, E, slot)


def kernel(**inputs):
    import concourse.bacc as bacc
    from concourse.bass_utils import run_bass_kernel_spmd
    A = {k: np.asarray(v) for k, v in inputs.items()}
    a = {k[len("L0_attn_"):]: v for k, v in A.items() if k.startswith("L0_attn_")}
    m = {k[len("L0_ffn_"):]: v for k, v in A.items() if k.startswith("L0_ffn_")}

    def chans(v):
        return v.reshape(CC, P).T

    def stationary(w):
        return w.T.reshape(w.shape[1] // P, P, w.shape[0]).transpose(1, 0, 2)

    params = np.stack([chans(v) for v in (
        a["ln1_g"], a["ln1_b"], a["ln2_g"], a["ln2_b"], a["att_time_mix"], a["att_combined_mix"], a["ffn_time_mix"],
        a["ffn_combined_mix"], a["time_decay"], a["time_first"], m["norm_weight"])], axis=1)
    const = np.zeros((P, NCONST), np.float32)
    r = np.arange(P)
    const[:, IDENT:IDENT + P] = np.eye(P)
    const[:, BLOCK:BLOCK + P] = r[:, None] % E == r[None, :] % E
    const[:, TRI:TRI + P] = (r[:, None] % E == r[None, :] % E) & (r[:, None] // E < r[None, :] // E)
    const[:, IOTA16:IOTA16 + 16] = np.arange(16)
    const[:, PCOL] = r
    n = np.arange(NT)
    const[:, TILE:TILE + NT] = (n % SEG) * TT + n // SEG
    const[:, DIAG:DIAG + 8] = r[:, None] // 16 == np.arange(8)[None, :]
    bits = np.zeros(48, np.int64)
    bits[:MAG_BITS] = 1 << (MAG_BITS - 1 - np.arange(MAG_BITS))
    arrays = {
        "x": A["L0_attn_x"].reshape(N, C),
        "params": params,
        "w_proj": np.stack([stationary(a[k]) for k in ("Wk", "Wv", "Wr", "Wo", "Fr")], axis=1),
        "w_fk": stationary(a["Fk"]),
        "w_fv": stationary(a["Fv"]),
        "router_w": stationary(m["router_weight"]),
        "router_b": m["router_bias"].reshape(E, 1),
        "fc1": m["fc1_weight"].transpose(0, 2, 1).reshape(E, CC, P, F).transpose(0, 2, 1, 3),
        "fc1_b": m["fc1_bias"].reshape(E, FF, P).transpose(2, 0, 1),
        "fc2": m["fc2_weight"].transpose(0, 2, 1).reshape(E, FF, P, C).transpose(0, 2, 1, 3),
        "fc2_b": m["fc2_bias"],
        "const": const,
        "bits_i": np.broadcast_to(bits.astype(np.int32), (P, 48)),
        "bits_f": np.broadcast_to(bits.astype(np.float32), (P, 48)),
    }
    nc = bacc.Bacc("TRN2", target_bir_lowering=False, num_devices=1)
    given, aps = {}, []
    for name, v in arrays.items():
        given[f"in_{name}"] = np.ascontiguousarray(v)
        aps.append(nc.dram_tensor(f"in_{name}", v.shape, mybir.dt.from_np(v.dtype), kind="ExternalInput").ap())
    aps.append(nc.dram_tensor("y", (N, C), F32, kind="ExternalOutput").ap())
    build(nc, *aps)
    got = run_bass_kernel_spmd(nc, [given], core_ids=[0])
    return got.results[0]["y"].reshape(NSEQ, T, C)
```

```python
import numpy as np
import concourse.bass as bass
from concourse import mybir
from contextlib import ExitStack

F32, F32R, BF16, I32 = mybir.dt.float32, mybir.dt.float32r, mybir.dt.bfloat16, mybir.dt.int32
U32 = mybir.dt.uint32
ALU, ACT, AX = mybir.AluOpType, mybir.ActivationFunctionType, mybir.AxisListType

P = 128
NSEQ, T, C = 8, 512, 256
N = NSEQ * T
CC = C // P
TT = T // P
NT = N // P
H = 4 * C
HF = H // P
E, F, CAP = 16, 1024, N // 16
FF = F // P
HALVES = CAP // P
SEG = P // E
ROW = C + E
EPS = 1e-5
K_CLAMP = 60.0
MAG_BITS = 31
STEPS = 5
DVE_PASS = 39

(LN1_G, LN1_B, LN2_G, LN2_B, TM1, CM1, TM2, CM2, DECAY, FIRST, NORM_W) = range(11)
IDENT, BLOCK, TRI = 0, P, 2 * P
IOTA16 = 3 * P
PCOL = IOTA16 + 16
TILE = PCOL + 1
DIAG = TILE + NT
NCONST = DIAG + 8


def build(nc, x, params, w_proj, w_fk, w_fv, router_w, router_b, fc1, fc1_b, fc2, fc2_b, const, bits_i, bits_f, out):
    rows = nc.dram_tensor("token_rows", (N, ROW), F32).ap()
    logit_rows = nc.dram_tensor("logit_rows", (NSEQ, E, T), F32).ap()
    index_rows = nc.dram_tensor("index_rows", (E, CAP), F32).ap()

    ctx = ExitStack()
    with ctx:
        def sb(name, shape, dt=F32):
            return ctx.enter_context(nc.sbuf_tensor(name, shape, dt))

        def sem(name):
            return ctx.enter_context(nc.semaphore(name))

        prm = sb("prm", [P, 11, CC])
        cst = sb("cst", [P, NCONST])
        bit_i = sb("bit_i", [P, 48], I32)
        bit_f = sb("bit_f", [P, 48])
        ident = cst[:, IDENT:IDENT + P]
        shift1 = sb("shift1", [P, CC])
        shift2 = sb("shift2", [P, CC])
        decay = sb("decay", [P, CC])
        first = sb("first", [P, CC])
        rw = sb("rw", [P, CC, E])
        rwn = sb("rwn", [P, CC, E])
        rb = sb("rb", [E, 1])
        gates = sb("gates", [P, NT * E])
        xsel = sb("xsel", [P, T])
        xs = sb("xs", [P, T])
        sgn = sb("sgn", [P, 8])
        cand = sb("cand", [P, 2], I32)
        rej = sb("rej", [P, 1], I32)
        cnt = sb("cnt", [P, 2])
        idx = sb("idx", [P, 2 * E], U32)
        stat = sb("stat", [P, 10, NT])
        st = sb("st", [P, NT, 6])
        st2 = sb("st2", [P, TT, 6])
        sm = sb("sm", [P, 8, TT])
        negh = sb("negh", [P, NT])
        junk = sb("junk", [P, T], BF16)
        hr, h32 = ([sb(f"{n}{i}", [P, T]) for i in range(2)] for n in ("hr", "h"))

        ROUNDED = 22528
        rounded = sb("rounded", [P, ROUNDED], F32R)
        taken = [0]

        def round_take(n):
            taken[0] += n
            assert taken[0] <= ROUNDED, taken[0]
            return rounded[:, taken[0] - n:taken[0]]

        wproj_h, wproj_l = (round_take(5 * CC * C).rearrange("p (w c o) -> p w c o", w=5, c=CC) for _ in range(2))
        wfk_h, wfk_l = (round_take(CC * H).rearrange("p (c o) -> p c o", c=CC) for _ in range(2))
        wfv_h, wfv_l = (round_take(HF * C).rearrange("p (f o) -> p f o", f=HF) for _ in range(2))
        xm1_h, xm1_l, xm2_h, xm2_l, y_h, y_l = (round_take(CC * T).rearrange("p (c t) -> p c t", c=CC) for _ in range(6))
        h_h, h_l = ([round_take(T) for _ in range(3)] for _ in range(2))
        taken[0] = 0
        w1_h, w1_l = ([round_take(CC * F).rearrange("p (c f) -> p c f", c=CC) for _ in range(2)] for _ in range(2))
        w2_h, w2_l = ([round_take(FF * C).rearrange("p (f d) -> p f d", f=FF) for _ in range(2)] for _ in range(2))
        xe_h, xe_l = ([round_take(CC * CAP).rearrange("p (c n) -> p c n", c=CC) for _ in range(2)] for _ in range(2))
        he_h, he_l = ([round_take(2 * CAP).rearrange("p (i n) -> p i n", i=2) for _ in range(FF // 2)] for _ in range(2))

        zT = sb("zT", [P, CC * N])
        zT_c = zT[:, :].rearrange("p (c n) -> p c n", c=CC)

        ARENA = 17200
        arena = sb("arena", [P, ARENA])
        at = [0]

        def take(n):
            at[0] += n
            assert at[0] <= ARENA, at[0]
            return arena[:, at[0] - n:at[0]]

        x1p = [take(CC * (T + 2)).rearrange("p (c t) -> p c t", c=CC) for _ in range(2)]
        def chunks():
            return take(CC * T).rearrange("p (c t) -> p c t", c=CC)
        u, xm, ek, th, kv, num, den, thf, x4T = (chunks() for _ in range(9))
        x2T = kv
        ap = take(CC * (T + 1)).rearrange("p (c t) -> p c t", c=CC)
        bp = take(CC * (T + 1)).rearrange("p (c t) -> p c t", c=CC)
        x3p = take(CC * (T + 2)).rearrange("p (c t) -> p c t", c=CC)
        xres, obuf = (take(TT * C).rearrange("p (j c) -> p j c", j=TT) for _ in range(2))
        z2 = x4T.rearrange("p c t -> p (c t)").rearrange("p (j c) -> p j c", j=TT)
        at[0] = 0
        xall = take(NT * C)
        zst = [take(TT * C).rearrange("p (j c) -> p j c", j=TT) for _ in range(2)]
        raw_proj = take(5 * CC * C).rearrange("p (w c o) -> p w c o", w=5, c=CC)
        raw_fk = take(CC * H).rearrange("p (c o) -> p c o", c=CC)
        raw_fv = take(HF * C).rearrange("p (f o) -> p f o", f=HF)
        lgs = [hr[k][0:E, :] for k in range(2)]
        at[0] = 0
        gt, eq, eqpre, mask, pre, pos = (take(T) for _ in range(6))
        ones = take(T)
        lt, ex, pt, pm, mt = (take(NT * E) for _ in range(5))
        ph_i, pl_i = (take(NT * E).bitcast(I32) for _ in range(2))
        ph, pl = (take(NT * E // 2).bitcast(BF16) for _ in range(2))
        smx = take(4 * NT).rearrange("p (k n) -> p k n", k=4)
        iota_b = take(8).bitcast(BF16)
        tile_b = take(NT // 2).bitcast(BF16)
        onehot = zT[:, 4096:8192].bitcast(BF16)
        place = take(NT * E * 16).bitcast(BF16)
        diag = take(2 * P).rearrange("p (e k) -> p e k", e=8)
        ids = take(2 * 32).rearrange("p (g k) -> p g k", g=2)
        idf = take(32).rearrange("p (g k) -> p g k", g=2)
        idr = take(P)[0:2 * E]
        at[0] = 0
        w1 = [zT[:, 0:2048].rearrange("p (c f) -> p c f", c=CC), zT[:, 4096:6144].rearrange("p (c f) -> p c f", c=CC)]
        w2 = [zT[:, 2048:4096].rearrange("p (f d) -> p f d", f=FF), zT[:, 6144:8192].rearrange("p (f d) -> p f d", f=FF)]
        xe = [take(HALVES * ROW).rearrange("p (h r) -> p h r", h=HALVES) for _ in range(2)]
        xeT = [take(CC * CAP).rearrange("p (c n) -> p c n", c=CC) for _ in range(2)]
        he = [take(2 * CAP).rearrange("p (i n) -> p i n", i=2) for _ in range(2)]
        ye = take(HALVES * C).rearrange("p (h d) -> p h d", h=HALVES)
        yg = [take(HALVES * C).rearrange("p (h d) -> p h d", h=HALVES) for _ in range(2)]
        b2 = [take(C) for _ in range(2)]
        b1f = take(E * FF)
        b1 = b1f.rearrange("p (e f) -> p e f", e=E)
        gate = take(2 * HALVES).rearrange("p (k h) -> p k h", k=2)
        idx_g = sb("idx_g", [P, 2, HALVES], U32)
        idx_s = sb("idx_s", [P, 2, HALVES], U32)

        ps = [ctx.enter_context(nc.psum_tensor(f"pair{i}", [P, 2, T], F32)) for i in range(4)]
        K_, V_, R_, O_ = ps

        const_in, proj_in, fk_in, fv_in, router_in, b1_in = (sem(n) for n in (
            "const_in", "proj_in", "fk_in", "fv_in", "router_in", "b1_in"))
        x_in = [sem(f"x_in{g}") for g in range(4)]
        dve_done, act_done = sem("dve_done"), sem("act_done")
        zero_done, var_ready, rstd_ready, var2_ready, rstd2_ready = (sem(n) for n in (
            "zero_done", "var_ready", "rstd_ready", "var2_ready", "rstd2_ready"))
        arena_b, mixing_ready = sem("arena_b"), sem("mixing_ready")
        z_ready, zT_psum, zT_ready = sem("z_ready"), sem("zT_psum"), sem("zT_ready")
        lg_psum, lg_ready = sem("lg_psum"), sem("lg_ready")
        z_stored = [sem("z_stored0"), sem("z_stored1")]
        lg_stored = [sem("lg_stored0"), sem("lg_stored1")]
        xsel_in = sem("xsel_in")
        x1_ready, u1_ready, xm1_ready, u1_used = sem("x1_ready"), sem("u1_ready"), sem("xm1_ready"), sem("u1_used")
        k_done, r_done, v_done = sem("k_done"), sem("r_done"), sem("v_done")
        ek_ready, th_ready, v_used, th_used = sem("ek_ready"), sem("th_ready"), sem("v_used"), sem("th_used")
        y_ready, wo_done, x2_ready, x2tok = sem("y_ready"), sem("wo_done"), sem("x2_ready"), sem("x2tok")
        v2_ready, r2_ready, ln2_ready = sem("v2_ready"), sem("r2_ready"), sem("ln2_ready")
        z2_ready, z2T_done, u2_ready, xm2_ready = sem("z2_ready"), sem("z2T_done"), sem("u2_ready"), sem("xm2_ready")
        fr_done, thf_ready, fk_done, relu_done, hh_ready = (sem(n) for n in (
            "fr_done", "thf_ready", "fk_done", "relu_done", "hh_ready"))
        hl_ready, h_used = sem("hl_ready"), sem("h_used")
        clamp_ready = sem("clamp_ready")
        x3_ready, rwn_ready = sem("x3_ready"), sem("rwn_ready")
        x4_ready, x4tok, out_ready = sem("x4_ready"), sem("x4tok"), sem("out_ready")
        xres_in, out_stored = sem("xres_in"), sem("out_stored")
        cnt_ready, total_done = sem("cnt_ready"), sem("total_done")
        tok_psum, exp_ready, gates_ready, gates_stored = (sem(n) for n in (
            "tok_psum", "exp_ready", "gates_ready", "gates_stored"))
        sub_ready = sem("sub_ready")
        tail_cnt, tail_psum, onehots_ready, ids_psum = (sem(n) for n in (
            "tail_cnt", "tail_psum", "onehots_ready", "ids_psum"))
        ids_ready, ids_stored, idr_in, idT_psum, idx_ready = (sem(n) for n in (
            "ids_ready", "ids_stored", "idr_in", "idT_psum", "idx_ready"))
        w1_in, w2_in, b2_in = ([sem(f"{n}_in{i}") for i in range(2)] for n in ("w1", "w2", "b2"))
        idx_g_early, idx_g_ready, idx_s_ready = sem("idx_g_early"), sem("idx_g_ready"), sem("idx_s_ready")
        rows_in = [sem("rows_in0"), sem("rows_in1")]
        w1h_ready, w1l_ready, w2h_ready, w2l_ready = (sem(n) for n in ("w1h_ready", "w1l_ready", "w2h_ready", "w2l_ready"))
        xeT_psum, xeT_ready, xeh_ready, xel_ready = (sem(n) for n in ("xeT_psum", "xeT_ready", "xeh_ready", "xel_ready"))
        fc1_done, gelu_done, heh_ready, hel_ready, fc2_done, ye_ready, yg_ready = (sem(n) for n in (
            "fc1_done", "gelu_done", "heh_ready", "hel_ready", "fc2_done", "ye_ready", "yg_ready"))
        added = sem("added")

        def product3(o, wh, wl, xh, xl, start, stop):
            nc.tensor.matmul(o, wh, xh, start=start, stop=False)
            nc.tensor.matmul(o, wh, xl, start=False, stop=False)
            return nc.tensor.matmul(o, wl, xh, start=False, stop=stop)

        class Chain:
            def __init__(self, eng, s, per_round=()):
                self.eng, self.s, self.base, self.n = eng, s, 0, 0
                self.per_round = list(per_round)

            def step(self, ins):
                self.n += 1
                return ins.then_inc(self.s, 1)

            def join(self, behind=0):
                self.eng.wait_ge(self.s, self.base + (self.n - behind))

            def link(self, ins):
                self.step(ins)
                self.join()
                return ins

            def begin(self):
                self.start, self.base, self.n = self.base + self.n, 0, 0
                self.per, self.i = self.per_round.pop(0), 0

            def round(self, i):
                assert self.i == 0 or self.n == self.per, (self.n, self.per)
                self.base, self.n, self.i = self.start + i * self.per, 0, 1

            def end(self, rounds):
                assert self.n == self.per, (self.n, self.per)
                self.base, self.n = self.start + rounds * self.per, 0

        def after(eng, signal, value):
            if not (isinstance(value, int) and value <= 0):
                eng.wait_ge(signal, value)

        def tell(eng, ins, signal, value):
            ins.then_inc(signal, 1)
            eng.wait_ge(signal, value)

        def passes(eng, chain, body):
            chain.begin()
            with eng.Fori(0, (NSEQ - 2) // 2) as j:
                for k in range(2):
                    chain.round(2 * j + k)
                    body(1 + 2 * j + k, (1 + k) % 2)
            chain.round(NSEQ - 2)
            body(NSEQ - 1, (NSEQ - 1) % 2)

        def pairs(eng, chain, n, body):
            chain.begin()
            for k in range(2):
                chain.round(k)
                body(k, k, True)
            with eng.Fori(1, n // 2) as j:
                for k in range(2):
                    chain.round(2 * j + k)
                    body(2 * j + k, k, False)
            chain.end(n)

        def first_of(i):
            return isinstance(i, int) and i == 0

        def last_of(i, n):
            return isinstance(i, int) and i == n - 1

        def experts(eng, body):
            body(0, 0)
            with eng.Fori(0, (E - 2) // 2) as j:
                for k in range(2):
                    body(1 + 2 * j + k, (1 + k) % 2)
            body(E - 1, (E - 1) % 2)

        block = ctx.enter_context(nc.Block())

        @block.sync
        def _(sp):
            x_t = x.rearrange("(g t p) c -> g p t c", g=4, p=P)
            sp.dma_start(cst[:, :], const).then_inc(const_in, 16)
            sp.dma_start(prm[:, :, :], params).then_inc(const_in, 16)
            for g in range(4):
                sp.dma_start(xall[:, g * 2048:(g + 1) * 2048].rearrange("p (t c) -> p t c", c=C), x_t[g]).then_inc(x_in[g], 16)
            sp.dma_start(rw[:, :, :], router_w).then_inc(router_in, 16)
            sp.dma_start(rb[:, :], router_b).then_inc(router_in, 16)
            sp.dma_start(bit_i[:, :], bits_i).then_inc(router_in, 16)
            sp.dma_start(bit_f[:, :], bits_f).then_inc(router_in, 16)
            sp.dma_start(raw_proj, w_proj).then_inc(proj_in, 16)
            sp.dma_start(raw_fk, w_fk).then_inc(fk_in, 16)
            sp.dma_start(raw_fv, w_fv).then_inc(fv_in, 16)
            z_rows = rows.rearrange("(b j p) r -> b p j r", b=NSEQ, p=P)
            with sp.Fori(0, NSEQ // 2) as j:
                for k in range(2):
                    sp.wait_ge(z_ready, 2 * j + k + 1)
                    sp.dma_start(z_rows[bass.ds(2 * j + k, 1), :, :, 0:C].rearrange("b p j r -> (b p) j r"), zst[k]).then_inc(z_stored[k], 16)
                    sp.wait_ge(lg_ready, 2 * j + k + 1)
                    sp.dma_start(logit_rows[bass.ds(2 * j + k, 1), :, :].rearrange("b e t -> (b e) t"), lgs[k]).then_inc(lg_stored[k], 16)
            for k in range(2):
                sp.wait_ge(lg_stored[k], 16 * NSEQ // 2)
                sp.wait_ge(z_stored[k], 16 * NSEQ // 2)
            sp.dma_start(xsel[:, :], logit_rows.rearrange("b e t -> (b e) t")).then_inc(xsel_in, 16)
            x_b = x.rearrange("(b j p) c -> b p j c", b=NSEQ, p=P)
            out_b = out.rearrange("(b j p) c -> b p j c", b=NSEQ, p=P)
            sp.wait_ge(arena_b, 1)
            sp.dma_start(xres, x_b[0]).then_inc(xres_in, 16)
            with sp.Fori(0, NSEQ - 1) as b:
                sp.wait_ge(out_ready, b + 1)
                sp.dma_start(out_b[bass.ds(b, 1), :, :, :].rearrange("b p j c -> (b p) j c"), obuf).then_inc(out_stored, 16)
                sp.wait_ge(out_stored, 16 * (b + 1))
                sp.dma_start(xres, x_b[bass.ds(b + 1, 1), :, :, :].rearrange("b p j c -> (b p) j c")).then_inc(xres_in, 16)
            sp.wait_ge(out_ready, NSEQ)
            sp.dma_start(out_b[NSEQ - 1], obuf).then_inc(out_stored, 16)
            sp.wait_ge(u1_ready, NSEQ)
            sp.dma_start(w1[0], fc1[0]).then_inc(w1_in[0], 16)
            sp.dma_start(w2[0], fc2[0]).then_inc(w2_in[0], 16)
            sp.wait_ge(out_stored, 16 * NSEQ)
            sp.wait_ge(gates_ready, 1)
            gate_rows = rows.rearrange("(s q p) r -> p q s r", s=SEG, p=P)
            for q in range(TT):
                sp.dma_start(gate_rows[:, q, :, C:ROW],
                             gates[:, q * SEG * E:(q + 1) * SEG * E].rearrange("p (s e) -> p s e", e=E)).then_inc(gates_stored, 16)
            sp.wait_ge(ids_ready, 1)
            ids_v = index_rows.rearrange("(g e) (h l) -> (e h) g l", g=2, l=16)
            for g in range(2):
                sp.dma_start(ids_v[:, g, :], idf[:, g, :]).then_inc(ids_stored, 16)
            sp.wait_ge(ids_stored, 32)
            sp.dma_start(idr, index_rows.rearrange("e (h n) -> (e h) n", n=P)).then_inc(idr_in, 16)
            sp.wait_ge(idx_ready, 1)
            sp.dma_start(w1[1], fc1[1]).then_inc(w1_in[1], 16)
            sp.dma_start(b1, fc1_b).then_inc(b1_in, 16)
            sp.dma_start(w2[1], fc2[1]).then_inc(w2_in[1], 16)
            for k in range(2):
                sp.dma_start(b2[k], fc2_b[k:k + 1, :].to_broadcast([P, C])).then_inc(b2_in[k], 16)
            with sp.Fori(1, E // 2) as j:
                for k in range(2):
                    e = 2 * j + k
                    sp.wait_ge(w1l_ready, e - 1)
                    sp.dma_start(w1[k], fc1[bass.ds(e, 1), :, :, :].rearrange("e p c f -> (e p) c f")).then_inc(w1_in[k], 16)
                    sp.wait_ge(w2l_ready, e - 1)
                    sp.dma_start(w2[k], fc2[bass.ds(e, 1), :, :, :].rearrange("e p f d -> (e p) f d")).then_inc(w2_in[k], 16)
                    sp.wait_ge(ye_ready, e - 1)
                    sp.dma_start(b2[k], fc2_b[bass.ds(e, 1), :].to_broadcast([P, C])).then_inc(b2_in[k], 16)

        @block.gpsimd
        def _(pool):
            G = nc.gpsimd
            pool.wait_ge(zero_done, 1)
            pool.wait_ge(var_ready, 1)
            G.tensor_tensor(stat[:, 4, :], stat[:, 3, :], negh[:, :], ALU.pow).then_inc(rstd_ready, 1)
            pool.wait_ge(var2_ready, 1)
            G.tensor_tensor(stat[:, 6, :], stat[:, 5, :], negh[:, :], ALU.pow).then_inc(rstd2_ready, 1)

            def rstd2(b):
                pool.wait_ge(v2_ready, b + 1)
                G.tensor_tensor(sm[:, 5, :], sm[:, 4, :], negh[:, 0:TT], ALU.pow).then_inc(r2_ready, 1)

            def hidden_low(b):
                for f in range(HF):
                    pool.wait_ge(hh_ready, b * HF + f + 1)
                    G.tensor_tensor(h_l[f % 3], h32[f % 2][:, :], h_h[f % 3].bitcast(F32), ALU.subtract).then_inc(hl_ready, 1)

            rstd2(0)
            with pool.Fori(1, NSEQ) as b:
                hidden_low(b - 1)
                rstd2(b)
            hidden_low(NSEQ - 1)
            pool.wait_ge(gates_stored, 16 * TT)
            pool.wait_ge(idx_ready, 1)
            pool.wait_ge(out_stored, 16 * NSEQ)

            def gather(e, k):
                early = isinstance(e, int) and e < 2
                after(pool, xel_ready, 0 if early else e - 1)
                G.tensor_copy(idx_g[:, k, :], idx[:, bass.ds(2 * e, 2)]).then_inc(idx_g_early if early else idx_g_ready, 1)
                pool.wait_ge(idx_ready, 1)
                pool.wait_ge(*((idx_g_early, e + 1) if early else (idx_g_ready, e - 1)))
                for h in range(HALVES):
                    G.indirect_dma_start(out=xe[k][:, h, :], out_offset=None, in_=rows,
                                         in_offset=bass.IndirectOffsetOnAxis(ap=idx_g[:, k, h:h + 1], axis=0)).then_inc(rows_in[k], 16)

            def scatter(e, k):
                pool.wait_ge(yg_ready, e + 1)
                after(pool, added, 2 * 16 * e)
                G.tensor_copy(idx_s[:, k, :], idx[:, bass.ds(2 * e, 2)]).then_inc(idx_s_ready, 1)
                pool.wait_ge(idx_ready, 1)
                pool.wait_ge(idx_s_ready, e + 2)
                for h in range(HALVES):
                    G.indirect_dma_start(out=out, out_offset=bass.IndirectOffsetOnAxis(ap=idx_s[:, k, h:h + 1], axis=0),
                                         in_=yg[k][:, h, :], in_offset=None, compute_op=ALU.add).then_inc(added, 16)

            def w1_low(e, k):
                pool.wait_ge(w1h_ready, e + 1)
                G.tensor_tensor(w1_l[k], w1[k], w1_h[k].bitcast(F32), ALU.subtract).then_inc(w1l_ready, 1)

            def slot(e, k):
                if not last_of(e, E):
                    gather(e + 1, 1 - k)
                    w1_low(e + 1, 1 - k)
                if not first_of(e):
                    scatter(e - 1, 1 - k)

            G.tensor_copy(idx_s[:, 0, :], idx[:, 0:2]).then_inc(idx_s_ready, 1)
            gather(0, 0)
            w1_low(0, 0)
            experts(pool, slot)
            scatter(E - 1, 1)
            pool.wait_ge(added, 2 * 16 * E)

        @block.scalar
        def _(act):
            ch = Chain(act, act_done, [0, 2])
            A = nc.scalar
            act.wait_ge(const_in, 32)
            ch.link(A.activation(decay[:, :], prm[:, DECAY, :], ACT.Exp))
            ch.link(A.activation(decay[:, :], decay[:, :], ACT.Exp, scale=-1.0))
            A.activation(first[:, :], prm[:, FIRST, :], ACT.Exp).then_inc(mixing_ready, 1)
            act.wait_ge(router_in, 64)

            def stage_a(b, k, early):
                pair = (K_, V_)[k]
                act.wait_ge(zT_psum, b + 1)
                A.activation(zT_c[:, :, bass.ds(b * T, T)], pair[:, :, :], ACT.Copy).then_inc(zT_ready, 1)
                act.wait_ge(lg_psum, b + 1)
                if not early:
                    act.wait_ge(lg_stored[k], 8 * (b - k))
                A.activation(lgs[k], R_[0:E, k, :], ACT.Identity, bias=rb[:, 0:1]).then_inc(lg_ready, 1)

            pairs(act, ch, NSEQ, stage_a)

            def mix_in(b, k):
                for c in range(CC):
                    ch.step(A.activation(x1p[k][:, c, 1:T + 1], zT_c[:, c, bass.ds(b * T, T)], ACT.Identity,
                                         scale=prm[:, LN1_G, c:c + 1], bias=prm[:, LN1_B, c:c + 1]))
                ch.join()
                for c in range(CC):
                    last = A.activation(u[:, c, :], x1p[k][:, c, 1:T + 1], ACT.Copy, scale=prm[:, TM1, c:c + 1])
                last.then_inc(u1_ready, 1)

            def attention(b):
                act.wait_ge(clamp_ready, b + 1)
                A.activation(ek, ek, ACT.Exp).then_inc(ek_ready, 1)
                act.wait_ge(r_done, b + 1)
                after(act, y_ready, b)
                A.activation(th, R_[:, :, :], ACT.Tanh, scale=0.5).then_inc(th_ready, 1)

            def ffn(b):
                act.wait_ge(fr_done, b + 1)
                A.activation(thf, R_[:, :, :], ACT.Tanh, scale=0.5).then_inc(thf_ready, 1)
                for f in range(HF + 1):
                    if f < HF:
                        if f >= 2:
                            act.wait_ge(hh_ready, b * HF + f - 1)
                        act.wait_ge(fk_done, b * HF + f + 1)
                        A.activation(hr[f % 2][:, :], K_[:, f % 2, :], ACT.Relu).then_inc(relu_done, 1)
                    if f > 0:
                        act.wait_ge(relu_done, b * HF + f)
                        g = f - 1
                        if g >= 2:
                            act.wait_ge(hl_ready, b * HF + g - 1)
                        if g >= 3:
                            act.wait_ge(h_used, b * HF + g - 2)
                        A.activation(h32[g % 2][:, :], hr[g % 2][:, :], ACT.Square)
                        A.activation(h_h[g % 3], hr[g % 2][:, :], ACT.Square).then_inc(hh_ready, 1)

            def norm2(b):
                act.wait_ge(ln2_ready, b + 1)
                after(act, z2T_done, b)
                for j in range(TT):
                    last = A.activation(z2[:, j, :], K_[:, j // 2, (j % 2) * C:(j % 2 + 1) * C], ACT.Identity,
                                        scale=sm[:, 5, j:j + 1], bias=sm[:, 6, j:j + 1])
                last.then_inc(z2_ready, 1)
                act.wait_ge(z2T_done, b + 1)
                after(act, x4_ready, b)
                for c in range(CC):
                    last = A.activation(x3p[:, c, 1:T + 1], V_[:, c, :], ACT.Identity,
                                        scale=prm[:, LN2_G, c:c + 1], bias=prm[:, LN2_B, c:c + 1])
                last.then_inc(x3_ready, 1)
                act.wait_ge(x3_ready, b + 1)
                after(act, xm2_ready, b)
                for c in range(CC):
                    last = A.activation(u[:, c, :], x3p[:, c, 1:T + 1], ACT.Copy, scale=prm[:, TM2, c:c + 1])
                last.then_inc(u2_ready, 1)

            act.wait_ge(arena_b, 1)
            mix_in(0, 0)
            attention(0)
            mix_in(1, 1)
            norm2(0)

            def one(b, k):
                attention(b)
                last_one = isinstance(b, int)
                if not last_one:
                    act.wait_ge(x2_ready, b)
                    act.wait_ge(xm1_ready, b + 1)
                    mix_in(b + 1, 1 - k)
                ffn(b - 1)
                norm2(b)

            passes(act, ch, one)
            ffn(NSEQ - 1)
            act.wait_ge(sub_ready, 1)
            A.activation(ex, lt, ACT.Exp).then_inc(exp_ready, 1)
            def w_high(e, k, w, w_h, w_in, used, ready):
                act.wait_ge(w_in[k], 8 * (e - k) + 16)
                after(act, used, 4 * (e - 1))
                A.activation(w_h[k], w[k], ACT.Copy).then_inc(ready, 1)

            def w1_high(e, k):
                w_high(e, k, w1, w1_h, w1_in, fc1_done, w1h_ready)

            def w2_high(e, k):
                w_high(e, k, w2, w2_h, w2_in, fc2_done, w2h_ready)

            def rows_to_channels(e, k):
                act.wait_ge(xeT_psum, e + 1)
                after(act, xel_ready, e - 1)
                for c in range(CC):
                    last = A.activation(xeT[k][:, c, :], K_[:, k, c * CAP:(c + 1) * CAP], ACT.Copy,
                                        scale=prm[:, NORM_W, c:c + 1])
                last.then_inc(xeT_ready, 1)

            def gelu(e, fp):
                act.wait_ge(fc1_done, 4 * e + fp + 1)
                if not (first_of(e) and fp < 2):
                    act.wait_ge(hel_ready, 4 * e + fp - 1)
                for i in range(2):
                    last = A.activation(he[fp % 2][:, i, :], V_[:, fp % 2, i * CAP:(i + 1) * CAP], ACT.Gelu,
                                        bias=b1f[:, bass.ds(e * FF + 2 * fp + i, 1)])
                last.then_inc(gelu_done, 1)

            def slot(e, k):
                more = not last_of(e, E)
                gelu(e, 0)
                if more:
                    w1_high(e + 1, 1 - k)
                gelu(e, 1)
                if more:
                    rows_to_channels(e + 1, 1 - k)
                gelu(e, 2)
                if more:
                    w2_high(e + 1, 1 - k)
                gelu(e, 3)

            act.wait_ge(idx_ready, 1)
            w1_high(0, 0)
            w2_high(0, 0)
            rows_to_channels(0, 0)
            act.wait_ge(b1_in, 16)
            experts(act, slot)

        @block.tensor
        def _(pe):
            ch = Chain(pe, act_done, [0, 0, 0])
            M = nc.tensor
            pe.wait_ge(const_in, 32)

            def stage_a(b, k, early):
                pair = (K_, V_)[k]
                pe.wait_ge(z_ready, b + 1)
                if not early:
                    pe.wait_ge(zT_ready, b - 1)
                for j in range(TT):
                    for c in range(CC):
                        last = M.transpose(pair[:, c, j * P:(j + 1) * P], zst[k][:, j, c * P:(c + 1) * P], ident)
                last.then_inc(zT_psum, 1)
                pe.wait_ge(zT_ready, b + 1)
                if early and k == 0:
                    pe.wait_ge(rwn_ready, 1)
                if not early:
                    pe.wait_ge(lg_ready, b - 1)
                for c in range(CC):
                    last = M.matmul(R_[0:E, k, :], rwn[:, c, :], zT_c[:, c, bass.ds(b * T, T)], start=(c == 0), stop=(c == CC - 1))
                last.then_inc(lg_psum, 1)

            pairs(pe, ch, NSEQ, stage_a)

            def total():
                return M.matmul(V_[:, 0, 0:1], cst[:, BLOCK:BLOCK + P], cnt[:, 0:1], start=True, stop=True)

            pe.wait_ge(cnt_ready, 1)
            total().then_inc(total_done, 1)

            def project(w, out_pair, sig):
                for m in range(CC):
                    for c in range(CC):
                        o = slice(m * P, (m + 1) * P)
                        last = product3(out_pair[:, m, :], wproj_h[:, w, c, o], wproj_l[:, w, c, o],
                                        *(v[:, c, :] for v in ((y_h, y_l) if w == 3 else (xm2_h, xm2_l) if w == 4 else (xm1_h, xm1_l))),
                                        start=(c == 0), stop=(c == CC - 1))
                last.then_inc(sig, 1)

            def kvr(b):
                pe.wait_ge(xm1_ready, b + 1)
                after(pe, z2_ready, b)
                project(0, K_, k_done)
                project(2, R_, r_done)
                after(pe, u2_ready, b)
                project(1, V_, v_done)

            def hidden_out(b, f):
                pe.wait_ge(hl_ready, b * HF + f + 1)
                for m in range(CC):
                    o = slice(m * P, (m + 1) * P)
                    last = product3(O_[:, m, :], wfv_h[:, f, o], wfv_l[:, f, o], h_h[f % 3], h_l[f % 3],
                                    start=(f == 0), stop=(f == HF - 1))
                last.then_inc(h_used, 1)

            def ffn(b, search):
                pe.wait_ge(xm2_ready, b + 1)
                if search:
                    pe.wait_ge(th_ready, b + 2)
                project(4, R_, fr_done)
                for f in range(HF):
                    if f >= 2:
                        pe.wait_ge(relu_done, b * HF + f - 1)
                    elif search and f == 0:
                        pe.wait_ge(ek_ready, b + 2)
                    for c in range(CC):
                        o = slice(f * P, (f + 1) * P)
                        last = product3(K_[:, f % 2, :], wfk_h[:, c, o], wfk_l[:, c, o], xm2_h[:, c, :], xm2_l[:, c, :],
                                        start=(c == 0), stop=(c == CC - 1))
                    last.then_inc(fk_done, 1)
                    if search and f % 2 == 0:
                        step_total(b, f // 2)
                    if f >= 2:
                        hidden_out(b, f - 2)
                if search:
                    step_total(b, 4)
                hidden_out(b, HF - 2)
                hidden_out(b, HF - 1)

            def step_total(b, i):
                if i < STEPS:
                    pe.wait_ge(cnt_ready, b * STEPS + i + 2)
                    total().then_inc(total_done, 1)

            def attention_out(b):
                pe.wait_ge(y_ready, b + 1)
                project(3, V_, wo_done)

            def to_tokens(pair, src, sig):
                for j in range(TT):
                    for c in range(CC):
                        last = M.transpose(pair[:, j // 2, (j % 2) * C + c * P:(j % 2) * C + (c + 1) * P],
                                           src[:, c, j * P:(j + 1) * P], ident)
                last.then_inc(sig, 1)

            def x4_tokens(b):
                pe.wait_ge(x4_ready, b + 1)
                pe.wait_ge(thf_ready, b + 1)
                to_tokens(R_, x4T, x4tok)

            def norm2(b):
                pe.wait_ge(x2_ready, b + 1)
                after(pe, relu_done, HF * b)
                to_tokens(K_, x2T, x2tok)
                pe.wait_ge(z2_ready, b + 1)
                for c in range(CC):
                    for j in range(TT):
                        last = M.transpose(V_[:, c, j * P:(j + 1) * P], z2[:, j, c * P:(c + 1) * P], ident)
                last.then_inc(z2T_done, 1)

            kvr(0)
            pe.wait_ge(ek_ready, 1)
            attention_out(0)
            norm2(0)

            def one(b, k):
                kvr(b)
                ffn(b - 1, True)
                attention_out(b)
                x4_tokens(b - 1)
                norm2(b)

            passes(pe, ch, one)
            ffn(NSEQ - 1, False)
            x4_tokens(NSEQ - 1)

            for q in range(TT):
                last = M.transpose(K_[:, 0, q * P:(q + 1) * P], xsel[:, q * P:(q + 1) * P], ident)
            last.then_inc(tok_psum, 1)
            pe.wait_ge(tail_cnt, 1)
            M.matmul(V_[:, 0, 0:2], cst[:, BLOCK:BLOCK + P], cnt[:, 0:2], start=True, stop=True)
            M.matmul(V_[:, 0, 4:6], cst[:, TRI:TRI + P], cnt[:, 0:2], start=True, stop=True).then_inc(tail_psum, 1)
            pe.wait_ge(tail_cnt, 2)
            M.matmul(V_[:, 0, 0:1], cst[:, TRI:TRI + P], cnt[:, 0:1], start=True, stop=True).then_inc(tail_psum, 1)
            pe.wait_ge(tail_cnt, 3)
            for q in range(TT):
                last = M.transpose(V_[:, 1, q * P:(q + 1) * P], pos[:, q * P:(q + 1) * P], ident)
            last.then_inc(tail_psum, 1)
            pe.wait_ge(onehots_ready, 1)
            for n in range(NT):
                for g in range(2):
                    lo, hi = (n * E + g * 8) * 16, (n * E + g * 8 + 8) * 16
                    last = M.matmul(O_[:, g, 0:256], onehot[:, lo:hi], place[:, 2 * lo:2 * hi], start=(n == 0), stop=(n == NT - 1))
            last.then_inc(ids_psum, 1)
            pe.wait_ge(idr_in, 16)
            M.transpose(K_[:, 1, 0:2 * E], idr, cst[0:2 * E, IDENT:IDENT + 2 * E]).then_inc(idT_psum, 1)

            def rows_to_channels(e, k):
                pe.wait_ge(rows_in[k], 16 * (e - k) + 32)
                after(pe, xeT_ready, e - 1)
                for c in range(CC):
                    for h in range(HALVES):
                        last = M.transpose(K_[:, k, c * CAP + h * P:c * CAP + (h + 1) * P], xe[k][:, h, c * P:(c + 1) * P], ident)
                last.then_inc(xeT_psum, 1)

            def fc1_pair(e, k, fp):
                if fp == 0:
                    pe.wait_ge(w1l_ready, e + 1)
                    pe.wait_ge(xel_ready, e + 1)
                if not (first_of(e) and fp < 2):
                    pe.wait_ge(gelu_done, 4 * e + fp - 1)
                for i in range(2):
                    f = slice((2 * fp + i) * P, (2 * fp + i + 1) * P)
                    for c in range(CC):
                        last = product3(V_[:, fp % 2, i * CAP:(i + 1) * CAP], w1_h[k][:, c, f], w1_l[k][:, c, f],
                                        xe_h[k][:, c, :], xe_l[k][:, c, :], start=(c == 0), stop=(c == CC - 1))
                last.then_inc(fc1_done, 1)

            def fc2_pair(e, k, fp):
                if fp == 0:
                    pe.wait_ge(w2l_ready, e + 1)
                pe.wait_ge(hel_ready, 4 * e + fp + 1)
                for i in range(2):
                    for h in range(HALVES):
                        t = slice(h * P, (h + 1) * P)
                        last = product3((R_, O_)[k][:, h, 0:C], he_h[fp][:, i, t], he_l[fp][:, i, t],
                                        w2_h[k][:, 2 * fp + i, :], w2_l[k][:, 2 * fp + i, :],
                                        start=(fp == 0 and i == 0), stop=(fp == 3 and i == 1))
                last.then_inc(fc2_done, 1)

            def slot(e, k):
                fc1_pair(e, k, 0)
                if not first_of(e):
                    fc2_pair(e - 1, 1 - k, 2)
                fc1_pair(e, k, 1)
                if not first_of(e):
                    fc2_pair(e - 1, 1 - k, 3)
                if not last_of(e, E):
                    rows_to_channels(e + 1, 1 - k)
                fc1_pair(e, k, 2)
                fc2_pair(e, k, 0)
                fc1_pair(e, k, 3)
                fc2_pair(e, k, 1)

            pe.wait_ge(idx_ready, 1)
            rows_to_channels(0, 0)
            experts(pe, slot)
            fc2_pair(E - 1, 1, 2)
            fc2_pair(E - 1, 1, 3)

        @block.vector
        def _(dve):
            ch = Chain(dve, dve_done, [0, DVE_PASS])
            V = nc.vector
            V.memset(negh[:, :], -0.5).then_inc(zero_done, 1)
            for g in range(4):
                dve.wait_ge(x_in[g], 16)
                for t in range(8 * g, 8 * g + 8):
                    ins = V.bn_stats(st[:, t, :], xall[:, t * C:(t + 1) * C])
            ch.link(ins)

            def moments(s, mean, dif, m2, var, tmp):
                ch.step(V.tensor_tensor(mean, s[:, :, 1], s[:, :, 4], ALU.add))
                ch.step(V.tensor_tensor(dif, s[:, :, 1], s[:, :, 4], ALU.subtract))
                ch.link(V.tensor_tensor(m2, s[:, :, 2], s[:, :, 5], ALU.add))
                ch.step(V.tensor_scalar(mean, mean, 0.5, None, ALU.mult))
                ch.link(V.scalar_tensor_tensor(tmp, dif, 0.25, dif, ALU.mult, ALU.mult))
                ch.link(V.scalar_tensor_tensor(var, m2, 1.0 / C, tmp, ALU.mult, ALU.add))

            moments(st, stat[:, 0, :], stat[:, 1, :], stat[:, 2, :], stat[:, 7, :], stat[:, 8, :])
            V.tensor_scalar(stat[:, 3, :], stat[:, 7, :], EPS, None, ALU.add).then_inc(var_ready, 1)
            dve.wait_ge(rstd_ready, 1)
            ch.link(V.tensor_tensor(stat[:, 8, :], stat[:, 7, :], stat[:, 4, :], ALU.mult))
            ch.link(V.tensor_tensor(stat[:, 8, :], stat[:, 8, :], stat[:, 4, :], ALU.mult))
            V.tensor_scalar(stat[:, 5, :], stat[:, 8, :], EPS, None, ALU.add).then_inc(var2_ready, 1)
            dve.wait_ge(const_in, 32)
            for sh, tm, cm in ((shift1, TM1, CM1), (shift2, TM2, CM2)):
                ch.link(V.tensor_scalar(sh[:, :], prm[:, tm, :], -1.0, 1.0, ALU.mult, ALU.add))
                ch.link(V.tensor_tensor(sh[:, 0:1], sh[:, 0:1], prm[:, cm, 0:1], ALU.add))
            dve.wait_ge(router_in, 64)
            for c in range(CC):
                ins = V.tensor_scalar(rwn[:, c, :], rw[:, c, :], prm[:, NORM_W, c:c + 1], None, ALU.mult)
            ins.then_inc(rwn_ready, 1)
            dve.wait_ge(rstd2_ready, 1)
            ch.link(V.tensor_tensor(stat[:, 8, :], stat[:, 4, :], stat[:, 6, :], ALU.mult))
            ch.link(V.scalar_tensor_tensor(stat[:, 9, :], stat[:, 0, :], -1.0, stat[:, 8, :], ALU.mult, ALU.mult))

            def stage_a(b, k, early):
                if not early:
                    dve.wait_ge(z_stored[k], 8 * (b - k))
                    dve.wait_ge(zT_psum, b - 1)
                for j in range(TT):
                    t = b * TT + j
                    ins = V.tensor_scalar(zst[k][:, j, :], xall[:, bass.ds(t * C, C)], stat[:, 8, bass.ds(t, 1)],
                                          stat[:, 9, bass.ds(t, 1)], ALU.mult, ALU.add)
                ins.then_inc(z_ready, 1)

            pairs(dve, ch, NSEQ, stage_a)

            dve.wait_ge(proj_in, 16)
            ch.link(V.tensor_scalar(raw_proj[:, 3, :, :], raw_proj[:, 3, :, :], 0.5, None, ALU.mult))
            ch.link(V.tensor_copy(wproj_h[:, :, :, :], raw_proj))
            ch.step(V.tensor_tensor(wproj_l[:, :, :, :], raw_proj, wproj_h[:, :, :, :].bitcast(F32), ALU.subtract))
            dve.wait_ge(fk_in, 16)
            ch.link(V.tensor_copy(wfk_h[:, :, :], raw_fk))
            ch.step(V.tensor_tensor(wfk_l[:, :, :], raw_fk, wfk_h[:, :, :].bitcast(F32), ALU.subtract))
            dve.wait_ge(fv_in, 16)
            ch.link(V.tensor_scalar(raw_fv, raw_fv, 0.5, None, ALU.mult))
            ch.link(V.tensor_copy(wfv_h[:, :, :], raw_fv))
            ch.step(V.tensor_tensor(wfv_l[:, :, :], raw_fv, wfv_h[:, :, :].bitcast(F32), ALU.subtract))
            dve.wait_ge(zT_psum, NSEQ)
            for k in range(2):
                dve.wait_ge(z_stored[k], 8 * NSEQ)
                dve.wait_ge(lg_stored[k], 8 * NSEQ)
            for v in (*x1p, x3p):
                V.memset(v[:, :, 0:1], 0.0)
                V.memset(v[:, :, T + 1:T + 2], 0.0)
            V.memset(ap[:, :, 0:1], 0.0)
            tell(dve, V.memset(bp[:, :, 0:1], 0.0), arena_b, 1)

            dve.wait_ge(xsel_in, 16)
            V.tensor_scalar(junk[:, :], xsel[:, :], 0.0, None, ALU.is_ge, ALU.add, accum_out=cnt[:, 0:1]).then_inc(cnt_ready, 1)
            dve.wait_ge(total_done, 1)
            ch.link(V.tensor_scalar(sgn[:, 0:1], V_[:, 0, 0:1], float(CAP), None, ALU.is_ge))
            ch.step(V.tensor_scalar(sgn[:, 1:2], sgn[:, 0:1], 2.0, -1.0, ALU.mult, ALU.add))
            ch.link(V.tensor_scalar(sgn[:, 2:3], sgn[:, 0:1], float(CAP - (N - CAP + 1)), float(N - CAP + 1), ALU.mult, ALU.add))
            ch.step(V.tensor_scalar(xs[:, :], xsel[:, :], sgn[:, 1:2], None, ALU.mult))
            ch.link(V.tensor_copy(cand[:, 0:1], bit_i[:, 0:1]))

            def count():
                V.tensor_scalar(junk[:, :], xs[:, :], cand[:, 0:1].bitcast(F32), None, ALU.is_ge, ALU.add,
                                accum_out=cnt[:, 0:1]).then_inc(cnt_ready, 1)

            def decide(b, i):
                s = (b - 1) * STEPS + i
                dve.wait_ge(total_done, s + 2)
                ch.link(V.tensor_scalar(rej[:, :], V_[:, 0, 0:1], sgn[:, 2:3], bit_f[:, bass.ds(s, 1)], ALU.is_lt, ALU.mult))
                ch.link(V.scalar_tensor_tensor(cand[:, 0:1], rej[:, :], bit_i[:, bass.ds(s + 1, 1)], cand[:, 0:1],
                                               ALU.bitwise_xor, ALU.bitwise_xor))

            def mix(b, src, u, shift, cm, hi, lo, ready):
                ch.step(V.scalar_tensor_tensor(xm[:, 0, :], src[:, 0, 0:T], shift[:, 0:1], u[:, 0, :], ALU.mult, ALU.add))
                ch.link(V.scalar_tensor_tensor(xm[:, 1, :], src[:, 1, 0:T], shift[:, 1:2], u[:, 1, :], ALU.mult, ALU.add))
                ch.link(V.scalar_tensor_tensor(xm[:, 1, :], src[:, 1, 2:T + 2], prm[:, cm, 1:2], xm[:, 1, :], ALU.mult, ALU.add))
                ch.link(V.tensor_copy(hi[:, :, :], xm))
                tell(dve, V.tensor_tensor(lo[:, :, :], xm, hi[:, :, :].bitcast(F32), ALU.subtract), ready, b + 1)

            def wkv(b, search):
                dve.wait_ge(k_done, b + 1)
                V.tensor_scalar(ek, K_[:, :, :], K_CLAMP, None, ALU.min).then_inc(clamp_ready, 1)
                dve.wait_ge(ek_ready, b + 1)
                dve.wait_ge(v_done, b + 1)
                ch.link(V.tensor_tensor(kv, ek, V_[:, :, :], ALU.mult))
                if search:
                    count()
                for c in range(CC):
                    ch.step(V.tensor_tensor_scan(ap[:, c, 1:T + 1], decay[:, c:c + 1].to_broadcast([P, T]), kv[:, c, :], 0.0, ALU.mult, ALU.add))
                    ch.step(V.tensor_tensor_scan(bp[:, c, 1:T + 1], decay[:, c:c + 1].to_broadcast([P, T]), ek[:, c, :], 0.0, ALU.mult, ALU.add))
                if search:
                    decide(b, 0)
                    count()
                ch.join()
                for c in range(CC):
                    ch.step(V.scalar_tensor_tensor(num[:, c, :], kv[:, c, :], first[:, c:c + 1], ap[:, c, 0:T], ALU.mult, ALU.add))
                    ch.step(V.scalar_tensor_tensor(den[:, c, :], ek[:, c, :], first[:, c:c + 1], bp[:, c, 0:T], ALU.mult, ALU.add))
                if search:
                    decide(b, 1)
                    count()
                ch.join()
                dve.wait_ge(th_ready, b + 1)
                ch.step(V.scalar_tensor_tensor(num, th, 1.0, num, ALU.add, ALU.mult))
                ch.step(V.reciprocal(den, den))
                if search:
                    decide(b, 2)
                    count()
                ch.join()
                ch.link(V.tensor_tensor(kv, num, den, ALU.mult))
                if search:
                    decide(b, 3)
                    count()
                after(dve, wo_done, b)
                ch.link(V.tensor_copy(y_h[:, :, :], kv))
                if search:
                    decide(b, 4)
                tell(dve, V.tensor_tensor(y_l[:, :, :], kv, y_h[:, :, :].bitcast(F32), ALU.subtract), y_ready, b + 1)

            def mix1(b, k):
                dve.wait_ge(u1_ready, b + 1)
                mix(b, x1p[k], u, shift1, CM1, xm1_h, xm1_l, xm1_ready)

            def ffn_end(b):
                dve.wait_ge(h_used, HF * (b + 1))
                dve.wait_ge(thf_ready, b + 1)
                ch.link(V.scalar_tensor_tensor(x4T, thf, 1.0, O_[:, :, :], ALU.add, ALU.mult))
                tell(dve, V.tensor_tensor(x4T, x4T, x3p[:, :, 1:T + 1], ALU.add), x4_ready, b + 1)

            def ffn_out(b):
                dve.wait_ge(x4tok, b + 1)
                dve.wait_ge(xres_in, 16 * b + 16)
                tell(dve, V.tensor_tensor(obuf.rearrange("p (a j) c -> p a (j c)", a=2), R_[:, :, :],
                                        xres.rearrange("p (a j) c -> p a (j c)", a=2), ALU.add), out_ready, b + 1)

            def residual1(b, k):
                dve.wait_ge(wo_done, b + 1)
                tell(dve, V.tensor_tensor(x2T, V_[:, :, :], x1p[k][:, :, 1:T + 1], ALU.add), x2_ready, b + 1)

            def norm2(b):
                dve.wait_ge(x2tok, b + 1)
                after(dve, z2_ready, b)
                for j in range(TT):
                    ins = V.bn_stats(st2[:, j, :], K_[:, j // 2, (j % 2) * C:(j % 2 + 1) * C])
                ch.link(ins)
                moments(st2, sm[:, 0, :], sm[:, 1, :], sm[:, 2, :], sm[:, 3, :], sm[:, 7, :])
                V.tensor_scalar(sm[:, 4, :], sm[:, 3, :], EPS, None, ALU.add).then_inc(v2_ready, 1)
                dve.wait_ge(r2_ready, b + 1)
                tell(dve, V.scalar_tensor_tensor(sm[:, 6, :], sm[:, 0, :], -1.0, sm[:, 5, :], ALU.mult, ALU.mult), ln2_ready, b + 1)

            def mix2(b):
                dve.wait_ge(u2_ready, b + 1)
                mix(b, x3p, u, shift2, CM2, xm2_h, xm2_l, xm2_ready)

            dve.wait_ge(mixing_ready, 1)
            mix1(0, 0)
            wkv(0, False)
            mix1(1, 1)
            residual1(0, 0)
            norm2(0)
            mix2(0)

            def one(b, k):
                wkv(b, True)
                if not isinstance(b, int):
                    mix1(b + 1, 1 - k)
                ffn_end(b - 1)
                residual1(b, k)
                ffn_out(b - 1)
                norm2(b)
                mix2(b)

            passes(dve, ch, one)
            ffn_end(NSEQ - 1)
            ffn_out(NSEQ - 1)

            def per_token(v):
                return v.rearrange("p (n e) -> p n e", e=E)

            def over_experts(v):
                return v.unsqueeze(2).to_broadcast([P, NT, E])

            dve.wait_ge(out_stored, 16 * NSEQ)
            dve.wait_ge(tok_psum, 1)
            ch.step(V.memset(ones, 1.0))
            logits = K_[:, 0, :].rearrange("p (n e) -> p n e", e=E)
            ch.link(V.tensor_reduce(smx[:, 0, :], logits, AX.X, ALU.max))
            tell(dve, V.tensor_tensor(per_token(lt), logits, over_experts(smx[:, 0, :]), ALU.subtract), sub_ready, 1)
            ch.link(V.tensor_scalar(sgn[:, 3:4], cand[:, 0:1].bitcast(F32), sgn[:, 1:2], None, ALU.mult))
            ch.step(V.tensor_scalar(gt, xsel[:, :], sgn[:, 3:4], None, ALU.is_gt, ALU.add, accum_out=cnt[:, 0:1]))
            tell(dve, V.tensor_scalar(eq, xsel[:, :], sgn[:, 3:4], None, ALU.is_equal, ALU.add, accum_out=cnt[:, 1:2]), tail_cnt, 1)
            dve.wait_ge(exp_ready, 1)
            ch.link(V.tensor_reduce(smx[:, 1, :], per_token(ex), AX.X, ALU.add))
            ch.link(V.reciprocal(smx[:, 1, :], smx[:, 1, :]))
            ch.link(V.tensor_tensor(per_token(pt), per_token(ex), over_experts(smx[:, 1, :]), ALU.mult))
            dve.wait_ge(tail_psum, 1)
            ch.step(V.tensor_scalar(sgn[:, 4:5], V_[:, 0, 0:1], -1.0, float(CAP), ALU.mult, ALU.add))
            ch.link(V.tensor_copy(sgn[:, 5:6], V_[:, 0, 5:6]))
            ch.link(V.tensor_tensor_scan(eqpre, ones, eq, sgn[:, 5:6], ALU.mult, ALU.add))
            ch.link(V.scalar_tensor_tensor(mt, eqpre, sgn[:, 4:5], eq, ALU.is_le, ALU.mult))
            ch.link(V.tensor_tensor(mask, mt, gt, ALU.add))
            tell(dve, V.tensor_scalar(pre, mask, 1.0, None, ALU.mult, ALU.add, accum_out=cnt[:, 0:1]), tail_cnt, 2)
            dve.wait_ge(tail_psum, 2)
            ch.link(V.tensor_copy(sgn[:, 6:7], V_[:, 0, 0:1]))
            ch.link(V.tensor_tensor_scan(pre, ones, mask, sgn[:, 6:7], ALU.mult, ALU.add))
            ch.link(V.tensor_tensor(pos, pre, mask, ALU.mult))
            tell(dve, V.tensor_scalar(pos, pos, -1.0, None, ALU.add), tail_cnt, 3)
            dve.wait_ge(tail_psum, 3)
            ch.step(V.tensor_scalar(mt, V_[:, 1, :], 0.0, None, ALU.is_ge))
            ch.link(V.tensor_copy(ph_i, V_[:, 1, :]))
            ch.step(V.tensor_scalar(pl_i, ph_i, 15, None, ALU.bitwise_and))
            ch.link(V.tensor_tensor(pm, pt, mt, ALU.mult))
            ch.step(V.tensor_scalar(ph_i, ph_i, 4, None, ALU.arith_shift_right))
            ch.step(V.tensor_copy(pl, pl_i))
            ch.link(V.tensor_reduce(smx[:, 2, :], per_token(pm), AX.X, ALU.add))
            ch.step(V.tensor_copy(ph, ph_i))
            ch.step(V.tensor_copy(iota_b, cst[:, IOTA16:IOTA16 + 16]))
            ch.step(V.tensor_copy(tile_b, cst[:, TILE:TILE + NT]))
            ch.link(V.scalar_tensor_tensor(smx[:, 3, :], smx[:, 2, :], 0.0, smx[:, 2, :], ALU.is_equal, ALU.add))
            ch.link(V.reciprocal(smx[:, 3, :], smx[:, 3, :]))
            tell(dve, V.tensor_tensor(per_token(gates[:, :]), per_token(pm), over_experts(smx[:, 3, :]), ALU.mult), gates_ready, 1)

            def sixteen(v):
                return v.unsqueeze(2).to_broadcast([P, NT * E, 16])

            iota_all = iota_b.unsqueeze(1).to_broadcast([P, NT * E, 16])
            place_v = place.rearrange("p (n k l) -> p n k l", k=2, l=16)
            ch.step(V.tensor_tensor(onehot.rearrange("p (n l) -> p n l", l=16), sixteen(ph), iota_all, ALU.is_equal))
            ch.link(V.tensor_tensor(place_v[:, :, 0, :], sixteen(pl), iota_all, ALU.is_equal))
            p5 = place.rearrange("p (n e k l) -> p n e k l", e=E, k=2, l=16)
            tiles = tile_b.unsqueeze(2).unsqueeze(3).to_broadcast([P, NT, E, 16])
            ch.link(V.tensor_tensor(p5[:, :, :, 1, :], p5[:, :, :, 0, :], tiles, ALU.mult))
            tell(dve, V.tensor_scalar(place_v[:, :, 0, :], place_v[:, :, 0, :], cst[:, PCOL:PCOL + 1], None, ALU.mult), onehots_ready, 1)
            dve.wait_ge(ids_psum, 1)
            for g in range(2):
                ch.link(V.tensor_tensor(diag, O_[:, g, 0:256].rearrange("p (e k) -> p e k", e=8),
                                        cst[:, DIAG:DIAG + 8].unsqueeze(2).to_broadcast([P, 8, 32]), ALU.mult))
                ch.link(V.tensor_reduce(ids[:, g, :], diag.rearrange("p e k -> p k e"), AX.X, ALU.add))
            tell(dve, V.scalar_tensor_tensor(idf, ids[:, :, 16:32], float(P), ids[:, :, 0:16], ALU.mult, ALU.add), ids_ready, 1)
            dve.wait_ge(idT_psum, 1)
            V.tensor_copy(idx[:, :], K_[:, 1, 0:2 * E]).then_inc(idx_ready, 1)

            def split_rows(e, k):
                dve.wait_ge(xeT_ready, e + 1)
                V.tensor_copy(gate[:, k, :], xe[k][:, :, bass.ds(e + C, 1)].rearrange("p h o -> p (h o)"))
                after(dve, fc1_done, 4 * (e - 1))
                tell(dve, V.tensor_copy(xe_h[k], xeT[k]), xeh_ready, e + 1)
                V.tensor_tensor(xe_l[k], xeT[k], xe_h[k].bitcast(F32), ALU.subtract).then_inc(xel_ready, 1)

            def split_hidden(e, fp):
                dve.wait_ge(gelu_done, 4 * e + fp + 1)
                if not first_of(e):
                    dve.wait_ge(fc2_done, 4 * e + fp - 3)
                tell(dve, V.tensor_copy(he_h[fp], he[fp % 2]), heh_ready, 4 * e + fp + 1)
                V.tensor_tensor(he_l[fp], he[fp % 2], he_h[fp].bitcast(F32), ALU.subtract).then_inc(hel_ready, 1)

            def w2_low(e, k):
                dve.wait_ge(w2h_ready, e + 1)
                V.tensor_tensor(w2_l[k], w2[k], w2_h[k].bitcast(F32), ALU.subtract).then_inc(w2l_ready, 1)

            def result(e, k):
                dve.wait_ge(fc2_done, 4 * e + 4)
                dve.wait_ge(b2_in[k], 8 * (e - k) + 16)
                dve.wait_ge(idx_s_ready, e + 1)
                tell(dve, V.tensor_tensor(ye, (R_, O_)[k][:, :, 0:C], b2[k].unsqueeze(1).to_broadcast([P, HALVES, C]), ALU.add),
                     ye_ready, e + 1)
                for h in range(HALVES):
                    ins = V.tensor_scalar(yg[k][:, h, :], ye[:, h, :], gate[:, k, h:h + 1], None, ALU.mult)
                tell(dve, ins, yg_ready, e + 1)

            def slot(e, k):
                more = not last_of(e, E)
                split_hidden(e, 0)
                split_hidden(e, 1)
                if not first_of(e):
                    result(e - 1, 1 - k)
                if more:
                    split_rows(e + 1, 1 - k)
                split_hidden(e, 2)
                if more:
                    w2_low(e + 1, 1 - k)
                split_hidden(e, 3)

            split_rows(0, 0)
            w2_low(0, 0)
            experts(dve, slot)
            result(E - 1, 1)


def kernel(**inputs):
    import concourse.bacc as bacc
    from concourse.bass_utils import run_bass_kernel_spmd
    A = {k: np.asarray(v) for k, v in inputs.items()}
    a = {k[len("L0_attn_"):]: v for k, v in A.items() if k.startswith("L0_attn_")}
    m = {k[len("L0_ffn_"):]: v for k, v in A.items() if k.startswith("L0_ffn_")}

    def chans(v):
        return v.reshape(CC, P).T

    def stationary(w):
        return w.T.reshape(w.shape[1] // P, P, w.shape[0]).transpose(1, 0, 2)

    params = np.stack([chans(v) for v in (
        a["ln1_g"], a["ln1_b"], a["ln2_g"], a["ln2_b"], a["att_time_mix"], a["att_combined_mix"], a["ffn_time_mix"],
        a["ffn_combined_mix"], a["time_decay"], a["time_first"], m["norm_weight"])], axis=1)
    const = np.zeros((P, NCONST), np.float32)
    r = np.arange(P)
    const[:, IDENT:IDENT + P] = np.eye(P)
    const[:, BLOCK:BLOCK + P] = r[:, None] % E == r[None, :] % E
    const[:, TRI:TRI + P] = (r[:, None] % E == r[None, :] % E) & (r[:, None] // E < r[None, :] // E)
    const[:, IOTA16:IOTA16 + 16] = np.arange(16)
    const[:, PCOL] = r
    n = np.arange(NT)
    const[:, TILE:TILE + NT] = (n % SEG) * TT + n // SEG
    const[:, DIAG:DIAG + 8] = r[:, None] // 16 == np.arange(8)[None, :]
    bits = np.zeros(48, np.int64)
    bits[:MAG_BITS] = 1 << (MAG_BITS - 1 - np.arange(MAG_BITS))
    arrays = {
        "x": A["L0_attn_x"].reshape(N, C),
        "params": params,
        "w_proj": np.stack([stationary(a[k]) for k in ("Wk", "Wv", "Wr", "Wo", "Fr")], axis=1),
        "w_fk": stationary(a["Fk"]),
        "w_fv": stationary(a["Fv"]),
        "router_w": stationary(m["router_weight"]),
        "router_b": m["router_bias"].reshape(E, 1),
        "fc1": m["fc1_weight"].transpose(0, 2, 1).reshape(E, CC, P, F).transpose(0, 2, 1, 3),
        "fc1_b": m["fc1_bias"].reshape(E, FF, P).transpose(2, 0, 1),
        "fc2": m["fc2_weight"].transpose(0, 2, 1).reshape(E, FF, P, C).transpose(0, 2, 1, 3),
        "fc2_b": m["fc2_bias"],
        "const": const,
        "bits_i": np.broadcast_to(bits.astype(np.int32), (P, 48)),
        "bits_f": np.broadcast_to(bits.astype(np.float32), (P, 48)),
    }
    nc = bacc.Bacc("TRN2", target_bir_lowering=False, num_devices=1)
    given, aps = {}, []
    for name, v in arrays.items():
        given[f"in_{name}"] = np.ascontiguousarray(v)
        aps.append(nc.dram_tensor(f"in_{name}", v.shape, mybir.dt.from_np(v.dtype), kind="ExternalInput").ap())
    aps.append(nc.dram_tensor("y", (N, C), F32, kind="ExternalOutput").ap())
    build(nc, *aps)
    got = run_bass_kernel_spmd(nc, [given], core_ids=[0])
    return got.results[0]["y"].reshape(NSEQ, T, C)
```

```python
import numpy as np
import concourse.bass as bass
from concourse import mybir
from contextlib import ExitStack

F32, F32R, BF16, I32 = mybir.dt.float32, mybir.dt.float32r, mybir.dt.bfloat16, mybir.dt.int32
U32 = mybir.dt.uint32
ALU, ACT, AX = mybir.AluOpType, mybir.ActivationFunctionType, mybir.AxisListType

P = 128
NSEQ, T, C = 8, 512, 256
N = NSEQ * T
CC = C // P
TT = T // P
NT = N // P
H = 4 * C
HF = H // P
E, F, CAP = 16, 1024, N // 16
FF = F // P
HALVES = CAP // P
SEG = P // E
ROW = C + E
EPS = 1e-5
K_CLAMP = 60.0
GROUPS = 4
MAG_BITS = 31
TOTALS = (1, 2, 4, 6)
STEPS = 5
DVE_PASS = 33

(LN1_G, LN1_B, LN2_G, LN2_B, TM1, CM1, TM2, CM2, DECAY, FIRST, NORM_W) = range(11)
IDENT, BLOCK, TRI = 0, P, 2 * P
PCOL = 3 * P
TILE = PCOL + 1
DIAG = TILE + NT
NCONST = DIAG + 8


def build(nc, x, params, w_proj, w_fk, w_fv, router_w, router_b, fc1, fc1_b, fc2, fc2_b, const, bits_i, bits_f, out):
    rows = nc.dram_tensor("token_rows", (N, ROW), F32).ap()
    logit_rows = nc.dram_tensor("logit_rows", (NSEQ, E, T), F32).ap()
    index_rows = nc.dram_tensor("index_rows", (E, CAP), F32).ap()

    ctx = ExitStack()
    with ctx:
        def sb(name, shape, dt=F32):
            return ctx.enter_context(nc.sbuf_tensor(name, shape, dt))

        def sem(name):
            return ctx.enter_context(nc.semaphore(name))

        prm = sb("prm", [P, 11, CC])
        cst = sb("cst", [P, NCONST])
        bit_i = sb("bit_i", [P, 48], I32)
        bit_f = sb("bit_f", [P, 48])
        ident = cst[:, IDENT:IDENT + P]
        shift1 = sb("shift1", [P, CC])
        shift2 = sb("shift2", [P, CC])
        gain1, bias1, gain2, bias2 = (sb(n, [P, CC]) for n in ("gain1", "bias1", "gain2", "bias2"))
        decay = sb("decay", [P, CC])
        first = sb("first", [P, CC])
        rw = sb("rw", [P, CC, E])
        rwn = sb("rwn", [P, CC, E])
        rb = sb("rb", [E, 1])
        gates = sb("gates", [P, NT * E])
        st = gates[:, 0:6 * NT].rearrange("p (t s) -> p t s", s=6)
        xsel = sb("xsel", [P, T])
        xs = sb("xs", [P, T])
        sgn = sb("sgn", [P, 8])
        cand = sb("cand", [P, 2], I32)
        rej = sb("rej", [P, 1], I32)
        cnt = sb("cnt", [P, 2])
        idx = sb("idx", [P, 2 * E], U32)
        stat = sb("stat", [P, 10, NT])
        st2 = sb("st2", [P, TT, 6])
        sm = sb("sm", [P, 8, TT])
        negh = sb("negh", [P, NT])
        junk = sb("junk", [P, T], BF16)
        hr, h32 = ([sb(f"{n}{i}", [P, T]) for i in range(2)] for n in ("hr", "h"))

        ROUNDED = 4 * (CC * F + FF * C) + 4 * CC * CAP + FF * 2 * CAP
        rounded = sb("rounded", [P, ROUNDED], F32R)
        taken = [0]

        def round_take(n):
            taken[0] += n
            assert taken[0] <= ROUNDED, taken[0]
            return rounded[:, taken[0] - n:taken[0]]

        wproj_h, wproj_l = (round_take(5 * CC * C).rearrange("p (w c o) -> p w c o", w=5, c=CC) for _ in range(2))
        wfk_h, wfk_l = (round_take(CC * H).rearrange("p (c o) -> p c o", c=CC) for _ in range(2))
        wfv_h, wfv_l = (round_take(HF * C).rearrange("p (f o) -> p f o", f=HF) for _ in range(2))
        xm1_h, xm1_l, xm2_h, xm2_l, y_h, y_l = (round_take(CC * T).rearrange("p (c t) -> p c t", c=CC) for _ in range(6))
        h_h, h_l = ([round_take(T) for _ in range(3)] for _ in range(2))
        taken[0] = 0
        w1_h, w1_l = ([round_take(CC * F).rearrange("p (c f) -> p c f", c=CC) for _ in range(2)] for _ in range(2))
        w2_h, w2_l = ([round_take(FF * C).rearrange("p (f d) -> p f d", f=FF) for _ in range(2)] for _ in range(2))
        xe_h, xe_l = ([round_take(CC * CAP).rearrange("p (c n) -> p c n", c=CC) for _ in range(2)] for _ in range(2))
        he_h, he_l = ([round_take(2 * CAP).rearrange("p (i n) -> p i n", i=2) for _ in range(FF // 2)] for _ in range(2))

        zT = sb("zT", [P, CC * N])
        zT_c = zT[:, :].rearrange("p (c n) -> p c n", c=CC)

        FFN_END = CC * (T + 2) + 2 * TT * C + 2 * CC * T
        ARENA = FFN_END + 3 * NT * E * 8
        arena = sb("arena", [P, ARENA])
        at = [0]

        def take(n):
            at[0] += n
            assert at[0] <= ARENA, at[0]
            return arena[:, at[0] - n:at[0]]

        x3p = take(CC * (T + 2)).rearrange("p (c t) -> p c t", c=CC)
        xres, obuf = (take(TT * C).rearrange("p (j c) -> p j c", j=TT) for _ in range(2))
        def chunks():
            return take(CC * T).rearrange("p (c t) -> p c t", c=CC)
        thf, x4T = chunks(), chunks()
        assert at[0] == FFN_END
        u, xm, ek, th, kv, num, den = (chunks() for _ in range(7))
        x1p = [take(CC * (T + 2)).rearrange("p (c t) -> p c t", c=CC) for _ in range(2)]
        x2T = kv
        ap = take(CC * (T + 1)).rearrange("p (c t) -> p c t", c=CC)
        bp = take(CC * (T + 1)).rearrange("p (c t) -> p c t", c=CC)
        z2 = num.rearrange("p c t -> p (c t)").rearrange("p (j c) -> p j c", j=TT)
        at[0] = 0
        xall = take(NT * C)
        zst = [take(TT * C).rearrange("p (j c) -> p j c", j=TT) for _ in range(2)]
        raw_proj = take(5 * CC * C).rearrange("p (w c o) -> p w c o", w=5, c=CC)
        raw_fk = take(CC * H).rearrange("p (c o) -> p c o", c=CC)
        raw_fv = take(HF * C).rearrange("p (f o) -> p f o", f=HF)
        lgs = [hr[k][0:E, :] for k in range(2)]
        at[0] = FFN_END
        onehot = take(NT * E * 8).bitcast(BF16).rearrange("p (n g k e) -> p n g k e", g=2, k=16, e=8)
        place = take(2 * NT * E * 8).bitcast(BF16).rearrange("p (k n e) -> p k n e", k=32, e=E)
        area = [0]

        def zt_take(n):
            area[0] += n
            assert area[0] <= CC * N
            return zT[:, area[0] - n:area[0]]

        gt, eq, eqpre, mask, pre, pos = (zt_take(T) for _ in range(6))
        lt, ex, pt, mt = (zt_take(NT * E) for _ in range(4))
        pm = lt
        ph_i, pl_i = (zt_take(NT * E).bitcast(I32) for _ in range(2))
        ph, pl = (zt_take(NT * E // 2).bitcast(BF16) for _ in range(2))
        smx = zt_take(4 * NT).rearrange("p (k n) -> p k n", k=4)
        tile_b = zt_take(NT * E // 2).bitcast(BF16)
        diag = zt_take(2 * P).rearrange("p (k e) -> p k e", e=8)
        ids = zt_take(2 * 32).rearrange("p (g k) -> p g k", g=2)
        idf = zt_take(32).rearrange("p (g k) -> p g k", g=2)
        idr = zt_take(P)[0:2 * E]
        at[0] = FFN_END
        w1 = [zT[:, 0:2048].rearrange("p (c f) -> p c f", c=CC), zT[:, 4096:6144].rearrange("p (c f) -> p c f", c=CC)]
        w2 = [zT[:, 2048:4096].rearrange("p (f d) -> p f d", f=FF), zT[:, 6144:8192].rearrange("p (f d) -> p f d", f=FF)]
        xe = [take(HALVES * ROW).rearrange("p (h r) -> p h r", h=HALVES) for _ in range(2)]
        xeT = [take(CC * CAP).rearrange("p (c n) -> p c n", c=CC) for _ in range(2)]
        he = [take(2 * CAP).rearrange("p (i n) -> p i n", i=2) for _ in range(2)]
        ye = take(HALVES * C).rearrange("p (h d) -> p h d", h=HALVES)
        yg = [take(HALVES * C).rearrange("p (h d) -> p h d", h=HALVES) for _ in range(2)]
        b2 = [take(C) for _ in range(2)]
        b1f = take(E * FF)
        b1 = b1f.rearrange("p (e f) -> p e f", e=E)
        gate = take(2 * HALVES).rearrange("p (k h) -> p k h", k=2)
        warm = sb("warm", [P, 1])
        idx_g = sb("idx_g", [P, 2, HALVES], U32)
        idx_s = sb("idx_s", [P, 2, HALVES], U32)

        ps = [ctx.enter_context(nc.psum_tensor(f"pair{i}", [P, 2, T], F32)) for i in range(4)]
        K_, V_, R_, O_ = ps

        const_in, proj_in, fk_in, fv_in, router_in, b1_in = (sem(n) for n in (
            "const_in", "proj_in", "fk_in", "fv_in", "router_in", "b1_in"))
        proj_high, fk_high, fv_high, weights_low = (sem(n) for n in ("proj_high", "fk_high", "fv_high", "weights_low"))
        fv_halved = sem("fv_halved")
        x_in = [sem(f"x_in{g}") for g in range(GROUPS)]
        dve_done, act_done = sem("dve_done"), sem("act_done")
        zero_done, var_ready, rstd_ready, var2_ready, rstd2_ready = (sem(n) for n in (
            "zero_done", "var_ready", "rstd_ready", "var2_ready", "rstd2_ready"))
        arena_b, mixing_ready = sem("arena_b"), sem("mixing_ready")
        zT_psum, zT_ready, scales_ready = sem("zT_psum"), sem("zT_ready"), sem("scales_ready")
        z_ready = [sem("z_ready0"), sem("z_ready1")]
        lg_psum, lg_ready = sem("lg_psum"), sem("lg_ready")
        z_stored = [sem("z_stored0"), sem("z_stored1")]
        lg_stored = [sem("lg_stored0"), sem("lg_stored1")]
        xsel_in = sem("xsel_in")
        u1_ready, xm1_ready = sem("u1_ready"), sem("xm1_ready")
        k_done, r_done, v_done = sem("k_done"), sem("r_done"), sem("v_done")
        ek_ready, th_ready = sem("ek_ready"), sem("th_ready")
        y_ready, wo_done, x2_ready, x2tok = sem("y_ready"), sem("wo_done"), sem("x2_ready"), sem("x2tok")
        u2_high, x3_ready = sem("u2_high"), sem("x3_ready")
        v2_ready, r2_ready, ln2_ready = sem("v2_ready"), sem("r2_ready"), sem("ln2_ready")
        z2_ready, z2T_done, xm2_ready = sem("z2_ready"), sem("z2T_done"), sem("xm2_ready")
        fr_done, thf_ready, fk_done, relu_done, hh_ready = (sem(n) for n in (
            "fr_done", "thf_ready", "fk_done", "relu_done", "hh_ready"))
        hl_ready, h_used = sem("hl_ready"), sem("h_used")
        clamp_ready = sem("clamp_ready")
        rwn_ready, x4_part = sem("rwn_ready"), sem("x4_part")
        xm1_lo, xm2_lo, y_lo = sem("xm1_lo"), sem("xm2_lo"), sem("y_lo")
        x4_ready, x4tok, out_ready = sem("x4_ready"), sem("x4tok"), sem("out_ready")
        xres_in, out_stored = sem("xres_in"), sem("out_stored")
        cnt_ready, total_done, total_read = sem("cnt_ready"), sem("total_done"), sem("total_read")
        tok_psum, exp_ready, gates_ready, gates_stored = (sem(n) for n in (
            "tok_psum", "exp_ready", "gates_ready", "gates_stored"))
        sub_ready, tail_read = sem("sub_ready"), sem("tail_read")
        tail_cnt, tail_psum, onehots_ready, ids_psum = (sem(n) for n in (
            "tail_cnt", "tail_psum", "onehots_ready", "ids_psum"))
        ids_ready, ids_stored, idr_in, idT_psum, idx_ready = (sem(n) for n in (
            "ids_ready", "ids_stored", "idr_in", "idT_psum", "idx_ready"))
        w1_in, w2_in, b2_in = ([sem(f"{n}_in{i}") for i in range(2)] for n in ("w1", "w2", "b2"))
        idx_g_early, idx_g_ready, idx_s_ready = sem("idx_g_early"), sem("idx_g_ready"), sem("idx_s_ready")
        rows_in = [sem("rows_in0"), sem("rows_in1")]
        w1h_ready, w1l_ready, w2h_ready, w2l_ready = (sem(n) for n in ("w1h_ready", "w1l_ready", "w2h_ready", "w2l_ready"))
        xeT_psum, xeT_ready, xeh_ready, xel_ready = (sem(n) for n in ("xeT_psum", "xeT_ready", "xeh_ready", "xel_ready"))
        fc1_done, gelu_done, heh_ready, hel_ready, fc2_done, ye_ready, yg_ready = (sem(n) for n in (
            "fc1_done", "gelu_done", "heh_ready", "hel_ready", "fc2_done", "ye_ready", "yg_ready"))
        added = sem("added")

        def product3(o, wh, wl, xh, xl, start, stop):
            nc.tensor.matmul(o, wh, xh, start=start, stop=False)
            nc.tensor.matmul(o, wh, xl, start=False, stop=False)
            return nc.tensor.matmul(o, wl, xh, start=False, stop=stop)

        class Chain:
            def __init__(self, eng, s, per_round=0):
                self.eng, self.s, self.base, self.n, self.per = eng, s, 0, 0, per_round

            def step(self, ins):
                self.n += 1
                return ins.then_inc(self.s, 1)

            def join(self):
                self.eng.wait_ge(self.s, self.base + self.n)

            def link(self, ins):
                self.step(ins)
                self.join()
                return ins

            def begin(self):
                self.start, self.base, self.n = self.base + self.n, 0, self.per

            def round(self, i):
                assert self.n == self.per, (self.n, self.per)
                self.base, self.n = self.start + i * self.per, 0

        def after(eng, signal, value):
            if not (isinstance(value, int) and value <= 0):
                eng.wait_ge(signal, value)

        def tell(eng, ins, signal, value):
            ins.then_inc(signal, 1)
            eng.wait_ge(signal, value)

        def passes(eng, body, chain=None):
            if chain:
                chain.begin()
            with eng.Fori(0, (NSEQ - 2) // 2) as j:
                for k in range(2):
                    if chain:
                        chain.round(2 * j + k)
                    body(1 + 2 * j + k, (1 + k) % 2)
            if chain:
                chain.round(NSEQ - 2)
            body(NSEQ - 1, (NSEQ - 1) % 2)

        def pairs(eng, n, body):
            for k in range(2):
                body(k, k, True)
            with eng.Fori(1, n // 2) as j:
                for k in range(2):
                    body(2 * j + k, k, False)

        def first_of(i):
            return isinstance(i, int) and i == 0

        def last_of(i, n):
            return isinstance(i, int) and i == n - 1

        def experts(eng, body, after_loop=1):
            body(0, 0)
            with eng.Fori(0, (E - 1 - after_loop) // 2) as j:
                for k in range(2):
                    body(1 + 2 * j + k, (1 + k) % 2)
            for e in range(E - after_loop, E):
                body(e, e % 2)

        block = ctx.enter_context(nc.Block())

        @block.sync
        def _(sp):
            x_t = x.rearrange("(g t p) c -> g p t c", g=GROUPS, p=P)
            sp.dma_start(cst[:, :], const).then_inc(const_in, 16)
            sp.dma_start(prm[:, :, :], params).then_inc(const_in, 16)
            part = NT * C // GROUPS
            for g in range(GROUPS):
                sp.dma_start(xall[:, g * part:(g + 1) * part].rearrange("p (t c) -> p t c", c=C), x_t[g]).then_inc(x_in[g], 16)
            sp.dma_start(rw[:, :, :], router_w).then_inc(router_in, 16)
            sp.dma_start(rb[:, :], router_b).then_inc(router_in, 16)
            sp.dma_start(bit_i[:, :], bits_i).then_inc(router_in, 16)
            sp.dma_start(bit_f[:, :], bits_f).then_inc(router_in, 16)
            sp.dma_start(raw_proj, w_proj).then_inc(proj_in, 16)
            z_rows = rows.rearrange("(b j p) r -> b p j r", b=NSEQ, p=P)
            for k in range(2):
                sp.wait_ge(z_ready[k], 2)
                sp.dma_start(z_rows[k, :, :, 0:C], zst[k]).then_inc(z_stored[k], 16)
            sp.dma_start(raw_fk, w_fk).then_inc(fk_in, 16)
            sp.dma_start(raw_fv, w_fv).then_inc(fv_in, 16)
            with sp.Fori(1, NSEQ // 2) as j:
                for k in range(2):
                    sp.wait_ge(z_ready[k], 2 * j + 2)
                    sp.dma_start(z_rows[bass.ds(2 * j + k, 1), :, :, 0:C].rearrange("b p j r -> (b p) j r"), zst[k]).then_inc(z_stored[k], 16)
            for k in range(2):
                sp.wait_ge(lg_stored[k], 16 * NSEQ // 2)
                sp.wait_ge(z_stored[k], 16 * NSEQ // 2)
            sp.dma_start(xsel[:, :], logit_rows.rearrange("b e t -> (b e) t")).then_inc(xsel_in, 16)
            x_b = x.rearrange("(b j p) c -> b p j c", b=NSEQ, p=P)
            out_b = out.rearrange("(b j p) c -> b p j c", b=NSEQ, p=P)
            sp.wait_ge(arena_b, 1)
            sp.dma_start(xres, x_b[0]).then_inc(xres_in, 16)
            with sp.Fori(0, NSEQ - 1) as b:
                sp.wait_ge(out_ready, b + 1)
                sp.dma_start(out_b[bass.ds(b, 1), :, :, :].rearrange("b p j c -> (b p) j c"), obuf).then_inc(out_stored, 16)
                sp.wait_ge(out_stored, 16 * (b + 1))
                sp.dma_start(xres, x_b[bass.ds(b + 1, 1), :, :, :].rearrange("b p j c -> (b p) j c")).then_inc(xres_in, 16)
            sp.wait_ge(gates_ready, 1)
            gate_rows = rows.rearrange("(s q p) r -> p q s r", s=SEG, p=P)
            for q in range(TT):
                sp.dma_start(gate_rows[:, q, :, C:ROW],
                             gates[:, q * SEG * E:(q + 1) * SEG * E].rearrange("p (s e) -> p s e", e=E)).then_inc(gates_stored, 16)
            sp.wait_ge(ids_ready, 1)
            ids_v = index_rows.rearrange("(g e) (h l) -> h e g l", g=2, l=16)
            for g in range(2):
                sp.dma_start(ids_v[:, :, g, :], idf[:, g, :]).then_inc(ids_stored, 16)
            sp.wait_ge(ids_stored, 32)
            sp.dma_start(idr, index_rows.rearrange("e (h n) -> (e h) n", n=P)).then_inc(idr_in, 16)
            sp.dma_start(w1[0], fc1[0]).then_inc(w1_in[0], 16)
            sp.dma_start(w2[0], fc2[0]).then_inc(w2_in[0], 16)
            sp.wait_ge(idx_ready, 1)
            sp.dma_start(b1, fc1_b).then_inc(b1_in, 16)
            sp.wait_ge(rows_in[0], 16 * HALVES)
            sp.dma_start(w1[1], fc1[1]).then_inc(w1_in[1], 16)
            sp.dma_start(w2[1], fc2[1]).then_inc(w2_in[1], 16)
            for k in range(2):
                sp.dma_start(b2[k], fc2_b[k:k + 1, :].to_broadcast([P, C])).then_inc(b2_in[k], 16)
            sp.wait_ge(out_ready, NSEQ)
            sp.dma_start(out_b[NSEQ - 1], obuf).then_inc(out_stored, 16)
            with sp.Fori(1, E // 2) as j:
                for k in range(2):
                    e = 2 * j + k
                    sp.wait_ge(w1l_ready, e - 1)
                    sp.dma_start(w1[k], fc1[bass.ds(e, 1), :, :, :].rearrange("e p c f -> (e p) c f")).then_inc(w1_in[k], 16)
                    sp.wait_ge(w2l_ready, e - 1)
                    sp.dma_start(w2[k], fc2[bass.ds(e, 1), :, :, :].rearrange("e p f d -> (e p) f d")).then_inc(w2_in[k], 16)
                    sp.wait_ge(ye_ready, e - 1)
                    sp.dma_start(b2[k], fc2_b[bass.ds(e, 1), :].to_broadcast([P, C])).then_inc(b2_in[k], 16)

        @block.gpsimd
        def _(pool):
            G = nc.gpsimd
            pool.wait_ge(zero_done, 1)

            def power1(g):
                tiles = slice(g * NT // GROUPS, (g + 1) * NT // GROUPS)
                pool.wait_ge(var_ready, g + 1)
                G.tensor_tensor(stat[:, 4, tiles], stat[:, 3, tiles], negh[:, tiles], ALU.pow).then_inc(rstd_ready, 1)

            def power2(g):
                tiles = slice(g * NT // GROUPS, (g + 1) * NT // GROUPS)
                pool.wait_ge(var2_ready, g + 1)
                G.tensor_tensor(stat[:, 6, tiles], stat[:, 5, tiles], negh[:, tiles], ALU.pow).then_inc(rstd2_ready, 1)

            def normalise(b):
                pool.wait_ge(scales_ready, b // 2 + 1)
                if b >= 2:
                    pool.wait_ge(z_stored[1], 8 * (b - 1))
                    pool.wait_ge(zT_psum, b - 1)
                for j in range(TT):
                    t = b * TT + j
                    ins = G.tensor_scalar(zst[1][:, j, :], xall[:, t * C:(t + 1) * C], stat[:, 8, t:t + 1],
                                          stat[:, 9, t:t + 1], ALU.mult, ALU.add)
                ins.then_inc(z_ready[1], 2)

            power1(0)
            power2(0)
            for g in range(GROUPS):
                if g + 1 < GROUPS:
                    power1(g + 1)
                normalise(2 * g + 1)
                if g + 1 < GROUPS:
                    power2(g + 1)
            for w in range(5):
                pool.wait_ge(proj_high, w + 1)
                G.tensor_tensor(wproj_l[:, w, :, :], raw_proj[:, w, :, :], wproj_h[:, w, :, :].bitcast(F32), ALU.subtract).then_inc(weights_low, 1)

            def low(lo, v, hi, ready, value, done):
                pool.wait_ge(ready, value)
                G.tensor_tensor(lo, v, hi.bitcast(F32), ALU.subtract).then_inc(done, 1)

            def xm1_low(b):
                for c in range(CC):
                    low(xm1_l[:, c, :], xm[:, c, :], xm1_h[:, c, :], xm1_ready, CC * b + c + 1, xm1_lo)

            def xm2_low(b):
                for c in range(CC):
                    low(xm2_l[:, c, :], xm[:, c, :], xm2_h[:, c, :], xm2_ready, CC * b + c + 1, xm2_lo)

            def y_low(b):
                low(y_l[:, :, :], kv, y_h[:, :, :], y_ready, b + 1, y_lo)

            def hidden_low(b, start, stop):
                for f in range(start, stop):
                    low(h_l[f % 3], h32[f % 2][:, :], h_h[f % 3], hh_ready, b * HF + f + 1, hl_ready)

            def residual2(b):
                pool.wait_ge(x4_part, b + 1)
                G.tensor_tensor(x4T, x4T, x3p[:, :, 1:T + 1], ALU.add).then_inc(x4_ready, 1)

            def rstd2(b):
                pool.wait_ge(v2_ready, b + 1)
                G.tensor_tensor(sm[:, 5, :], sm[:, 4, :], negh[:, 0:TT], ALU.pow).then_inc(r2_ready, 1)

            xm1_low(0)
            y_low(0)
            xm1_low(1)
            rstd2(0)
            xm2_low(0)

            def one(b, k):
                hidden_low(b - 1, 0, HF - 2)
                y_low(b)
                hidden_low(b - 1, HF - 2, HF)
                if not last_of(b, NSEQ):
                    xm1_low(b + 1)
                rstd2(b)
                residual2(b - 1)
                xm2_low(b)

            passes(pool, one)
            hidden_low(NSEQ - 1, 0, HF)
            pool.wait_ge(gates_stored, 16 * TT)
            pool.wait_ge(idx_ready, 1)

            def gather(e, k):
                early = isinstance(e, int) and e < 2
                after(pool, xel_ready, 0 if early else e - 1)
                G.tensor_copy(idx_g[:, k, :], idx[:, bass.ds(2 * e, 2)]).then_inc(idx_g_early if early else idx_g_ready, 1)
                pool.wait_ge(idx_ready, 1)
                pool.wait_ge(*((idx_g_early, e + 1) if early else (idx_g_ready, e - 1)))
                for h in range(HALVES):
                    G.indirect_dma_start(out=xe[k][:, h, :], out_offset=None, in_=rows,
                                         in_offset=bass.IndirectOffsetOnAxis(ap=idx_g[:, k, h:h + 1], axis=0)).then_inc(rows_in[k], 16)

            def scatter(e, k):
                pool.wait_ge(yg_ready, e + 1)
                if first_of(e):
                    pool.wait_ge(out_stored, 16 * NSEQ)
                after(pool, added, 2 * 16 * e)
                G.tensor_copy(idx_s[:, k, :], idx[:, bass.ds(2 * e, 2)]).then_inc(idx_s_ready, 1)
                pool.wait_ge(idx_ready, 1)
                pool.wait_ge(idx_s_ready, e + 2)
                for h in range(HALVES):
                    G.indirect_dma_start(out=out, out_offset=bass.IndirectOffsetOnAxis(ap=idx_s[:, k, h:h + 1], axis=0),
                                         in_=yg[k][:, h, :], in_offset=None, compute_op=ALU.add).then_inc(added, 16)

            def w1_low(e, k):
                pool.wait_ge(w1h_ready, e + 1)
                G.tensor_tensor(w1_l[k], w1[k], w1_h[k].bitcast(F32), ALU.subtract).then_inc(w1l_ready, 1)

            def slot(e, k):
                if not (isinstance(e, int) and e + 2 >= E):
                    gather(e + 2, k)
                if not last_of(e, E):
                    w1_low(e + 1, 1 - k)
                if not first_of(e):
                    scatter(e - 1, 1 - k)

            G.tensor_copy(idx_s[:, 0, :], idx[:, 0:2]).then_inc(idx_s_ready, 1)
            gather(0, 0)
            residual2(NSEQ - 1)
            gather(1, 1)
            experts(pool, slot, after_loop=3)
            scatter(E - 1, 1)
            pool.wait_ge(added, 2 * 16 * E)

        @block.scalar
        def _(act):
            ch = Chain(act, act_done)
            A = nc.scalar
            act.wait_ge(const_in, 32)
            ch.link(A.activation(decay[:, :], prm[:, DECAY, :], ACT.Exp))
            ch.link(A.activation(decay[:, :], decay[:, :], ACT.Exp, scale=-1.0))
            A.activation(first[:, :], prm[:, FIRST, :], ACT.Exp).then_inc(mixing_ready, 1)
            act.wait_ge(router_in, 64)

            def channels(b):
                act.wait_ge(zT_psum, b + 1)
                A.activation(zT_c[:, :, b * T:(b + 1) * T], (K_, V_)[b % 2][:, :, :], ACT.Copy).then_inc(zT_ready, 1)

            def logits(b):
                k = b % 2
                act.wait_ge(lg_psum, b + 1)
                if b >= 2:
                    act.wait_ge(lg_stored[k], 8 * (b - k))
                A.activation(lgs[k], R_[0:E, k, :], ACT.Identity, bias=rb[:, 0:1]).then_inc(lg_ready, 1)

            def store_logits(b):
                act.wait_ge(lg_ready, b + 1)
                A.dma_start(logit_rows[b], lgs[b % 2]).then_inc(lg_stored[b % 2], 16)

            def weights_high(i):
                if i < 5:
                    act.wait_ge(proj_in, 16)
                    A.activation(wproj_h[:, i, :, :], raw_proj[:, i, :, :], ACT.Copy).then_inc(proj_high, 1)
                elif i < 9:
                    act.wait_ge(fk_in, 16)
                    c, o = (i - 5) // 2, slice((i - 5) % 2 * H // 2, ((i - 5) % 2 + 1) * H // 2)
                    A.activation(wfk_h[:, c, o], raw_fk[:, c, o], ACT.Copy).then_inc(fk_high, 1)
                else:
                    act.wait_ge(fv_halved, 1)
                    f = slice(2 * (i - 9), 2 * (i - 9) + 2)
                    A.activation(wfv_h[:, f, :], raw_fv[:, f, :], ACT.Copy).then_inc(fv_high, 1)

            PIECES = 13
            for b in range(NSEQ + 1):
                if b < NSEQ:
                    channels(b)
                if b > 0:
                    logits(b - 1)
                if b > 1:
                    for i in range(2 * (b - 2), min(2 * (b - 1), PIECES)):
                        weights_high(i)
                if b > 0:
                    store_logits(b - 1)

            def mix_in(b, k, i):
                c, z = i // 2, zT_c[:, i // 2, bass.ds(b * T, T)]
                if i % 2 == 0:
                    A.activation(x1p[k][:, c, 1:T + 1], z, ACT.Identity, scale=prm[:, LN1_G, c:c + 1], bias=prm[:, LN1_B, c:c + 1])
                else:
                    A.activation(u[:, c, :], z, ACT.Identity, scale=gain1[:, c:c + 1], bias=bias1[:, c:c + 1]).then_inc(u1_ready, 1)

            def keys(b):
                act.wait_ge(clamp_ready, b + 1)
                A.activation(ek, ek, ACT.Exp).then_inc(ek_ready, 1)

            def receptance(b):
                act.wait_ge(r_done, b + 1)
                after(act, y_ready, b)
                A.activation(th, R_[:, :, :], ACT.Tanh, scale=0.5).then_inc(th_ready, 1)

            def ffn(b, between):
                act.wait_ge(fr_done, b + 1)
                A.activation(thf, R_[:, :, :], ACT.Tanh, scale=0.5).then_inc(thf_ready, 1)
                for f in range(HF):
                    if f >= 2:
                        act.wait_ge(hh_ready, b * HF + f - 1)
                    act.wait_ge(fk_done, b * HF + f + 1)
                    A.activation(hr[f % 2][:, :], K_[:, f % 2, :], ACT.Relu).then_inc(relu_done, 1)
                    if f >= 2:
                        act.wait_ge(hl_ready, b * HF + f - 1)
                    if f >= 3:
                        act.wait_ge(h_used, b * HF + f - 2)
                    act.wait_ge(relu_done, b * HF + f + 1)
                    A.activation(h32[f % 2][:, :], hr[f % 2][:, :], ACT.Square)
                    A.activation(h_h[f % 3], hr[f % 2][:, :], ACT.Square).then_inc(hh_ready, 1)
                    between(f)

            def norm2(b, next_keys):
                act.wait_ge(ln2_ready, b + 1)
                for j in range(TT):
                    last = A.activation(z2[:, j, :], V_[:, j // 2, (j % 2) * C:(j % 2 + 1) * C], ACT.Identity,
                                        scale=sm[:, 5, j:j + 1], bias=sm[:, 6, j:j + 1])
                last.then_inc(z2_ready, 1)
                if next_keys is not None:
                    keys(next_keys)
                act.wait_ge(z2T_done, b + 1)
                after(act, x4_ready, b)
                act.wait_ge(xm1_ready, CC * (b + (1 if last_of(b, NSEQ) else 2)))
                A.activation(x3p[:, 0, 1:T + 1], V_[:, 0, :], ACT.Identity, scale=prm[:, LN2_G, 0:1], bias=prm[:, LN2_B, 0:1])
                A.activation(u[:, 0, :], V_[:, 0, :], ACT.Identity, scale=gain2[:, 0:1], bias=bias2[:, 0:1]).then_inc(x3_ready, 1)
                act.wait_ge(u2_high, b + 1)
                A.activation(x3p[:, 1, 1:T + 1], V_[:, 1, :], ACT.Identity, scale=prm[:, LN2_G, 1:2],
                             bias=prm[:, LN2_B, 1:2]).then_inc(x3_ready, 1)

            act.wait_ge(arena_b, 1)
            for i in range(2 * CC):
                mix_in(0, 0, i)
            keys(0)
            receptance(0)
            for k in range(2):
                act.wait_ge(lg_stored[k], 8 * NSEQ)
            act.wait_ge(xm1_ready, CC)
            for i in range(2 * CC):
                mix_in(1, 1, i)
            norm2(0, 1)
            receptance(1)

            def one(b, k):
                more = not last_of(b, NSEQ)

                def between(f):
                    if more and 3 <= f < 3 + 2 * CC:
                        if f == 3:
                            act.wait_ge(xm2_ready, CC * b)
                        mix_in(b + 1, 1 - k, f - 3)

                ffn(b - 1, between)
                norm2(b, b + 1 if more else None)
                if more:
                    receptance(b + 1)

            passes(act, one)
            act.wait_ge(sub_ready, 1)
            A.activation(ex, lt, ACT.Exp).then_inc(exp_ready, 1)
            ffn(NSEQ - 1, lambda f: None)
            def w_high(e, k, w, w_h, w_in, used, ready):
                act.wait_ge(w_in[k], 8 * (e - k) + 16)
                after(act, used, 4 * (e - 1))
                A.activation(w_h[k], w[k], ACT.Copy).then_inc(ready, 1)

            def w1_high(e, k):
                w_high(e, k, w1, w1_h, w1_in, fc1_done, w1h_ready)

            def w2_high(e, k):
                w_high(e, k, w2, w2_h, w2_in, fc2_done, w2h_ready)

            def rows_to_channels(e, k):
                act.wait_ge(xeT_psum, e + 1)
                after(act, xel_ready, e - 1)
                for c in range(CC):
                    last = A.activation(xeT[k][:, c, :], K_[:, k, c * CAP:(c + 1) * CAP], ACT.Copy,
                                        scale=prm[:, NORM_W, c:c + 1])
                last.then_inc(xeT_ready, 1)

            def gelu(e, fp):
                act.wait_ge(fc1_done, 4 * e + fp + 1)
                if not (first_of(e) and fp < 2):
                    act.wait_ge(hel_ready, 4 * e + fp - 1)
                for i in range(2):
                    last = A.activation(he[fp % 2][:, i, :], V_[:, fp % 2, i * CAP:(i + 1) * CAP], ACT.Gelu,
                                        bias=b1f[:, bass.ds(e * FF + 2 * fp + i, 1)])
                last.then_inc(gelu_done, 1)

            def slot(e, k):
                more = not last_of(e, E)
                gelu(e, 0)
                if more:
                    w1_high(e + 1, 1 - k)
                gelu(e, 1)
                if more:
                    rows_to_channels(e + 1, 1 - k)
                gelu(e, 2)
                if more:
                    w2_high(e + 1, 1 - k)
                gelu(e, 3)

            act.wait_ge(h_used, HF * NSEQ)
            w1_high(0, 0)
            w2_high(0, 0)
            rows_to_channels(0, 0)
            A.activation(warm[:, :], prm[:, NORM_W, 0:1], ACT.Gelu)
            act.wait_ge(b1_in, 16)
            experts(act, slot)

        @block.tensor
        def _(pe):
            M = nc.tensor
            pe.wait_ge(const_in, 32)

            def stage_a(b, k, early):
                pair = (K_, V_)[k]
                pe.wait_ge(z_ready[k], b - k + 2)
                if not early:
                    pe.wait_ge(zT_ready, b - 1)
                for j in range(TT):
                    for c in range(CC):
                        last = M.transpose(pair[:, c, j * P:(j + 1) * P], zst[k][:, j, c * P:(c + 1) * P], ident)
                last.then_inc(zT_psum, 1)
                if early and k == 0:
                    pe.wait_ge(rwn_ready, 1)
                else:
                    logits(b - 1, 1 - k)

            def logits(b, k):
                pe.wait_ge(zT_ready, b + 1)
                for c in range(CC):
                    last = M.matmul(R_[0:E, k, :], rwn[:, c, :], zT_c[:, c, bass.ds(b * T, T)], start=(c == 0), stop=(c == CC - 1))
                last.then_inc(lg_psum, 1)

            pairs(pe, NSEQ, stage_a)
            logits(NSEQ - 1, 1)

            def total(o):
                return M.matmul(o, cst[:, BLOCK:BLOCK + P], cnt[:, 0:1], start=True, stop=True)

            def project(w, x_h, x_l, pair, ready, lo_ready, count, sig, per_chunk=True):
                for m in range(CC):
                    o = slice(m * P, (m + 1) * P)
                    for c in range(CC):
                        if m == 0:
                            pe.wait_ge(ready, count - (CC - 1 - c if per_chunk else 0))
                        M.matmul(pair[:, m, :], wproj_h[:, w, c, o], x_h[:, c, :], start=(c == 0), stop=False)
                        M.matmul(pair[:, m, :], wproj_l[:, w, c, o], x_h[:, c, :], start=False, stop=False)
                pe.wait_ge(lo_ready, count)
                for m in range(CC):
                    for c in range(CC):
                        last = M.matmul(pair[:, m, :], wproj_h[:, w, c, m * P:(m + 1) * P], x_l[:, c, :], start=False, stop=(c == CC - 1))
                last.then_inc(sig, 1)

            def key(b):
                after(pe, relu_done, HF * (b - 1))
                project(0, xm1_h, xm1_l, K_, xm1_ready, xm1_lo, CC * (b + 1), k_done)

            def receptance(b):
                after(pe, thf_ready, b - 1)
                project(2, xm1_h, xm1_l, R_, xm1_ready, xm1_lo, CC * (b + 1), r_done)

            def value(b):
                after(pe, out_ready, b - 1)
                project(1, xm1_h, xm1_l, O_, xm1_ready, xm1_lo, CC * (b + 1), v_done)

            def hidden_out(b, f):
                pe.wait_ge(hl_ready, b * HF + f + 1)
                for m in range(CC):
                    o = slice(m * P, (m + 1) * P)
                    last = product3(O_[:, m, :], wfv_h[:, f, o], wfv_l[:, f, o], h_h[f % 3], h_l[f % 3],
                                    start=(f == 0), stop=(f == HF - 1))
                last.then_inc(h_used, 1)

            def ffn(b, search):
                if search:
                    pe.wait_ge(th_ready, b + 2)
                project(4, xm2_h, xm2_l, R_, xm2_ready, xm2_lo, CC * (b + 1), fr_done)
                if not search:
                    pe.wait_ge(tail_read, 2)
                for f in range(HF):
                    if f >= 2:
                        pe.wait_ge(relu_done, b * HF + f - 1)
                    elif search and f == 0:
                        pe.wait_ge(clamp_ready, b + 2)
                    elif search:
                        pe.wait_ge(total_read, 2 * b + 1)
                    for c in range(CC):
                        o = slice(f * P, (f + 1) * P)
                        last = product3(K_[:, f % 2, :], wfk_h[:, c, o], wfk_l[:, c, o], xm2_h[:, c, :], xm2_l[:, c, :],
                                        start=(c == 0), stop=(c == CC - 1))
                    last.then_inc(fk_done, 1)
                    if f >= 2:
                        hidden_out(b, f - 2)
                    if not search:
                        if f == 4:
                            tail_ids()
                    elif last_of(b + 1, NSEQ):
                        if f == 1:
                            step_total(b, 0)
                        elif f == 3:
                            tail_at_threshold()
                        elif f == 6:
                            tail_before()
                    elif f in TOTALS:
                        step_total(b, TOTALS.index(f))
                if not search:
                    pe.wait_ge(idr_in, 16)
                    M.transpose(V_[:, 0, 0:2 * E], idr, cst[0:2 * E, IDENT:IDENT + 2 * E]).then_inc(idT_psum, 1)
                    hidden_out(b, HF - 2)
                    hidden_out(b, HF - 1)

            def step_total(b, i):
                pe.wait_ge(cnt_ready, b * STEPS + i + 2)
                total(V_[:, 0, 0:1]).then_inc(total_done, 1)

            def attention_out(b):
                project(3, y_h, y_l, V_, y_ready, y_lo, b + 1, wo_done, per_chunk=False)

            def to_tokens(pair, src, sig):
                for j in range(TT):
                    for c in range(CC):
                        last = M.transpose(pair[:, j // 2, (j % 2) * C + c * P:(j % 2) * C + (c + 1) * P],
                                           src[:, c, j * P:(j + 1) * P], ident)
                last.then_inc(sig, 1)

            def x4_tokens(b, pair):
                pe.wait_ge(x4_ready, b + 1)
                to_tokens(pair, x4T, x4tok)

            def x2_tokens(b):
                pe.wait_ge(x2_ready, b + 1)
                to_tokens(V_, x2T, x2tok)

            def z2_channels(b):
                pe.wait_ge(z2_ready, b + 1)
                for c in range(CC):
                    for j in range(TT):
                        last = M.transpose(V_[:, c, j * P:(j + 1) * P], z2[:, j, c * P:(c + 1) * P], ident)
                last.then_inc(z2T_done, 1)

            def tail_at_threshold():
                pe.wait_ge(tail_cnt, 1)
                M.matmul(V_[:, 1, 0:2], cst[:, BLOCK:BLOCK + P], cnt[:, 0:2], start=True, stop=True)
                M.matmul(V_[:, 1, 4:6], cst[:, TRI:TRI + P], cnt[:, 0:2], start=True, stop=True).then_inc(tail_psum, 1)

            def tail_before():
                pe.wait_ge(tail_cnt, 2)
                M.matmul(V_[:, 1, 0:1], cst[:, TRI:TRI + P], cnt[:, 0:1], start=True, stop=True).then_inc(tail_psum, 1)

            def tail_tokens():
                pe.wait_ge(relu_done, HF * (NSEQ - 1))
                for q in range(TT):
                    last = M.transpose(K_[:, 1, q * P:(q + 1) * P], xsel[:, q * P:(q + 1) * P], ident)
                last.then_inc(tok_psum, 1)
                pe.wait_ge(tail_cnt, 3)
                for q in range(TT):
                    last = M.transpose(K_[:, 0, q * P:(q + 1) * P], pos[:, q * P:(q + 1) * P], ident)
                last.then_inc(tail_psum, 1)

            def tail_ids():
                pe.wait_ge(onehots_ready, 1)
                for n in range(NT):
                    for g in range(2):
                        e8 = slice(g * 8, g * 8 + 8)
                        last = M.matmul(V_[:, g, 0:256], onehot[:, n, g, :, :].rearrange("p k e -> p (k e)"), place[:, :, n, e8],
                                        start=(n == 0), stop=(n == NT - 1))
                last.then_inc(ids_psum, 1)

            key(0)
            value(0)
            receptance(0)
            attention_out(0)
            pe.wait_ge(clamp_ready, 1)
            key(1)
            x2_tokens(0)
            pe.wait_ge(th_ready, 1)
            receptance(1)
            pe.wait_ge(cnt_ready, 1)
            total(O_[:, 0, 0:1]).then_inc(total_done, 1)
            z2_channels(0)
            pe.wait_ge(total_read, 1)
            value(1)

            def one(b, k):
                more = not last_of(b, NSEQ)
                ffn(b - 1, True)
                pe.wait_ge(total_read, 2 * b)
                attention_out(b)
                hidden_out(b - 1, HF - 2)
                x2_tokens(b)
                hidden_out(b - 1, HF - 1)
                if more:
                    key(b + 1)
                    receptance(b + 1)
                else:
                    tail_tokens()
                x4_tokens(b - 1, O_)
                z2_channels(b)
                if more:
                    pe.wait_ge(clamp_ready, b + 2)
                    pe.wait_ge(cnt_ready, b * STEPS + 1)
                    total(K_[:, 1, 0:1]).then_inc(total_done, 1)
                if more:
                    value(b + 1)

            passes(pe, one)
            ffn(NSEQ - 1, False)
            def rows_to_channels(e, k):
                pe.wait_ge(rows_in[k], 16 * (e - k) + 32)
                after(pe, xeT_ready, e - 1)
                for c in range(CC):
                    for h in range(HALVES):
                        last = M.transpose(K_[:, k, c * CAP + h * P:c * CAP + (h + 1) * P], xe[k][:, h, c * P:(c + 1) * P], ident)
                last.then_inc(xeT_psum, 1)

            def fc1_pair(e, k, fp):
                if fp == 0:
                    pe.wait_ge(w1l_ready, e + 1)
                    pe.wait_ge(xel_ready, e + 1)
                if not (first_of(e) and fp < 2):
                    pe.wait_ge(gelu_done, 4 * e + fp - 1)
                for i in range(2):
                    f = slice((2 * fp + i) * P, (2 * fp + i + 1) * P)
                    for c in range(CC):
                        last = product3(V_[:, fp % 2, i * CAP:(i + 1) * CAP], w1_h[k][:, c, f], w1_l[k][:, c, f],
                                        xe_h[k][:, c, :], xe_l[k][:, c, :], start=(c == 0), stop=(c == CC - 1))
                last.then_inc(fc1_done, 1)

            def fc2_pair(e, k, fp):
                if fp == 0:
                    pe.wait_ge(w2l_ready, e + 1)
                pe.wait_ge(hel_ready, 4 * e + fp + 1)
                for i in range(2):
                    for h in range(HALVES):
                        t = slice(h * P, (h + 1) * P)
                        last = product3((R_, O_)[k][:, h, 0:C], he_h[fp][:, i, t], he_l[fp][:, i, t],
                                        w2_h[k][:, 2 * fp + i, :], w2_l[k][:, 2 * fp + i, :],
                                        start=(fp == 0 and i == 0), stop=(fp == 3 and i == 1))
                last.then_inc(fc2_done, 1)

            def slot(e, k):
                fc1_pair(e, k, 0)
                if not first_of(e):
                    fc2_pair(e - 1, 1 - k, 2)
                fc1_pair(e, k, 1)
                if not first_of(e):
                    fc2_pair(e - 1, 1 - k, 3)
                if not last_of(e, E):
                    rows_to_channels(e + 1, 1 - k)
                fc1_pair(e, k, 2)
                fc2_pair(e, k, 0)
                fc1_pair(e, k, 3)
                fc2_pair(e, k, 1)

            rows_to_channels(0, 0)
            x4_tokens(NSEQ - 1, R_)
            experts(pe, slot)
            fc2_pair(E - 1, 1, 2)
            fc2_pair(E - 1, 1, 3)

        @block.vector
        def _(dve):
            ch = Chain(dve, dve_done, DVE_PASS)
            V = nc.vector
            V.memset(negh[:, :], -0.5).then_inc(zero_done, 1)
            def bn(lo, hi):
                for t in range(lo, hi):
                    ins = V.bn_stats(st[:, t, :], xall[:, t * C:(t + 1) * C])
                ch.link(ins)

            def moments(s, mean, dif, m2, var, tmp):
                ch.step(V.tensor_tensor(mean, s[:, :, 1], s[:, :, 4], ALU.add))
                ch.step(V.tensor_tensor(dif, s[:, :, 1], s[:, :, 4], ALU.subtract))
                ch.link(V.tensor_tensor(m2, s[:, :, 2], s[:, :, 5], ALU.add))
                ch.step(V.tensor_scalar(mean, mean, 0.5, None, ALU.mult))
                ch.link(V.scalar_tensor_tensor(tmp, dif, 0.25, dif, ALU.mult, ALU.mult))
                ch.link(V.scalar_tensor_tensor(var, m2, 1.0 / C, tmp, ALU.mult, ALU.add))

            def mixing_weights():
                dve.wait_ge(const_in, 32)
                for sh, tm, cm in ((shift1, TM1, CM1), (shift2, TM2, CM2)):
                    ch.link(V.tensor_scalar(sh[:, :], prm[:, tm, :], -1.0, 1.0, ALU.mult, ALU.add))
                    ch.link(V.tensor_tensor(sh[:, 0:1], sh[:, 0:1], prm[:, cm, 0:1], ALU.add))
                for product, norm, tm in ((gain1, LN1_G, TM1), (bias1, LN1_B, TM1), (gain2, LN2_G, TM2), (bias2, LN2_B, TM2)):
                    ch.step(V.tensor_tensor(product[:, :], prm[:, norm, :], prm[:, tm, :], ALU.mult))

            def router_weights():
                dve.wait_ge(router_in, 64)
                for c in range(CC):
                    ins = V.tensor_scalar(rwn[:, c, :], rw[:, c, :], prm[:, NORM_W, c:c + 1], None, ALU.mult)
                ins.then_inc(rwn_ready, 1)

            PER = NT // GROUPS

            def first_variance(g):
                s = slice(g * PER, (g + 1) * PER)
                moments(st[:, s, :], stat[:, 0, s], stat[:, 1, s], stat[:, 2, s], stat[:, 7, s], stat[:, 8, s])
                V.tensor_scalar(stat[:, 3, s], stat[:, 7, s], EPS, None, ALU.add).then_inc(var_ready, 1)

            def second_variance(g):
                s = slice(g * PER, (g + 1) * PER)
                dve.wait_ge(rstd_ready, g + 1)
                ch.link(V.tensor_tensor(stat[:, 8, s], stat[:, 7, s], stat[:, 4, s], ALU.mult))
                ch.link(V.tensor_tensor(stat[:, 8, s], stat[:, 8, s], stat[:, 4, s], ALU.mult))
                V.tensor_scalar(stat[:, 5, s], stat[:, 8, s], EPS, None, ALU.add).then_inc(var2_ready, 1)

            def scales(g):
                s = slice(g * PER, (g + 1) * PER)
                dve.wait_ge(rstd2_ready, g + 1)
                ch.link(V.tensor_tensor(stat[:, 8, s], stat[:, 4, s], stat[:, 6, s], ALU.mult))
                tell(dve, V.scalar_tensor_tensor(stat[:, 9, s], stat[:, 0, s], -1.0, stat[:, 8, s], ALU.mult, ALU.mult), scales_ready, g + 1)

            def normalise(b):
                if b >= 2:
                    dve.wait_ge(z_stored[0], 8 * b)
                    dve.wait_ge(zT_psum, b - 1)
                for j in range(TT):
                    t = b * TT + j
                    ins = V.tensor_scalar(zst[0][:, j, :], xall[:, t * C:(t + 1) * C], stat[:, 8, t:t + 1],
                                          stat[:, 9, t:t + 1], ALU.mult, ALU.add)
                ins.then_inc(z_ready[0], 2)

            dve.wait_ge(x_in[0], 16)
            bn(0, PER)
            first_variance(0)
            for g in range(GROUPS):
                if g + 1 < GROUPS:
                    dve.wait_ge(x_in[g + 1], 16)
                    bn((g + 1) * PER, (g + 1) * PER + PER // 2)
                second_variance(g)
                if g + 1 < GROUPS:
                    bn((g + 1) * PER + PER // 2, (g + 2) * PER)
                    first_variance(g + 1)
                else:
                    mixing_weights()
                scales(g)
                if g == 0:
                    router_weights()
                normalise(2 * g)
                if g == GROUPS - 2:
                    dve.wait_ge(fv_in, 16)
                    V.tensor_scalar(raw_fv, raw_fv, 0.5, None, ALU.mult).then_inc(fv_halved, 1)

            for i in range(4):
                c, o = i // 2, slice(i % 2 * H // 2, (i % 2 + 1) * H // 2)
                dve.wait_ge(fk_high, i + 1)
                ch.step(V.tensor_tensor(wfk_l[:, c, o], raw_fk[:, c, o], wfk_h[:, c, o].bitcast(F32), ALU.subtract))
            for i in range(2):
                f = slice(i * HF // 2, (i + 1) * HF // 2)
                dve.wait_ge(fv_high, 2 * i + 2)
                ch.step(V.tensor_tensor(wfv_l[:, f, :], raw_fv[:, f, :], wfv_h[:, f, :].bitcast(F32), ALU.subtract))
            dve.wait_ge(weights_low, 5)
            dve.wait_ge(zT_psum, NSEQ)
            for k in range(2):
                dve.wait_ge(z_stored[k], 8 * NSEQ)
            ch.join()
            for v in (*x1p, x3p):
                V.memset(v[:, :, 0:1], 0.0)
                V.memset(v[:, :, T + 1:T + 2], 0.0)
            V.memset(ap[:, :, 0:1], 0.0)
            tell(dve, V.memset(bp[:, :, 0:1], 0.0), arena_b, 1)

            def sign():
                dve.wait_ge(xsel_in, 16)
                V.tensor_scalar(junk[:, :], xsel[:, :], 0.0, None, ALU.is_ge, ALU.add, accum_out=cnt[:, 0:1]).then_inc(cnt_ready, 1)
                dve.wait_ge(total_done, 1)
                tell(dve, V.tensor_scalar(sgn[:, 0:1], O_[:, 0, 0:1], float(CAP), None, ALU.is_ge), total_read, 1)
                ch.step(V.tensor_scalar(sgn[:, 1:2], sgn[:, 0:1], 2.0, -1.0, ALU.mult, ALU.add))
                ch.link(V.tensor_scalar(sgn[:, 2:3], sgn[:, 0:1], float(CAP - (N - CAP + 1)), float(N - CAP + 1), ALU.mult, ALU.add))
                ch.step(V.tensor_scalar(xs[:, :], xsel[:, :], sgn[:, 1:2], None, ALU.mult))
                ch.link(V.tensor_copy(cand[:, 0:1], bit_i[:, 0:1]))

            def count():
                V.tensor_scalar(junk[:, :], xs[:, :], cand[:, 0:1].bitcast(F32), None, ALU.is_ge, ALU.add,
                                accum_out=cnt[:, 0:1]).then_inc(cnt_ready, 1)

            def decide(b, i):
                s = (b - 1) * STEPS + i
                dve.wait_ge(total_done, s + 2)
                o = K_[:, 1, 0:1] if i == STEPS - 1 else V_[:, 0, 0:1]
                ins = V.tensor_scalar(rej[:, :], o, sgn[:, 2:3], bit_f[:, bass.ds(s, 1)], ALU.is_lt, ALU.mult)
                if i >= STEPS - 2:
                    tell(dve, ins, total_read, 2 * b + i - (STEPS - 2))
                else:
                    ch.link(ins)
                ch.link(V.scalar_tensor_tensor(cand[:, 0:1], rej[:, :], bit_i[:, bass.ds(s + 1, 1)], cand[:, 0:1],
                                               ALU.bitwise_xor, ALU.bitwise_xor))

            def mix(b, src, src_ready, shift, cm, hi, ready):
                dve.wait_ge(src_ready, CC * b + 1)
                ch.link(V.scalar_tensor_tensor(xm[:, 0, :], src[:, 0, 0:T], shift[:, 0:1], u[:, 0, :], ALU.mult, ALU.add))
                V.tensor_copy(hi[:, 0, :], xm[:, 0, :]).then_inc(ready, 1)
                dve.wait_ge(src_ready, CC * b + 2)
                ch.link(V.scalar_tensor_tensor(xm[:, 1, :], src[:, 1, 0:T], shift[:, 1:2], u[:, 1, :], ALU.mult, ALU.add))
                ch.link(V.scalar_tensor_tensor(xm[:, 1, :], src[:, 1, 2:T + 2], prm[:, cm, 1:2], xm[:, 1, :], ALU.mult, ALU.add))
                V.tensor_copy(hi[:, 1, :], xm[:, 1, :]).then_inc(ready, 1)

            def clamp(b):
                dve.wait_ge(k_done, b + 1)
                V.tensor_scalar(ek, K_[:, :, :], K_CLAMP, None, ALU.min).then_inc(clamp_ready, 1)

            def scan(state, c, v):
                ch.step(V.tensor_tensor_scan(state[:, c, 1:T + 1], decay[:, c:c + 1].to_broadcast([P, T]), v[:, c, :], 0.0, ALU.mult, ALU.add))

            def scan_keys(b):
                dve.wait_ge(ek_ready, b + 1)
                for c in range(CC):
                    scan(bp, c, ek)

            def wkv(b, search):
                tail = last_of(b, NSEQ)
                dve.wait_ge(v_done, b + 1)
                ch.link(V.tensor_tensor(kv, ek, O_[:, :, :], ALU.mult))
                if search:
                    count()
                for c in range(CC):
                    scan(ap, c, kv)
                for c in range(CC):
                    ch.step(V.scalar_tensor_tensor(den[:, c, :], ek[:, c, :], first[:, c:c + 1], bp[:, c, 0:T], ALU.mult, ALU.add))
                if search:
                    decide(b, 0)
                    if tail:
                        threshold()
                    else:
                        count()
                ch.join()
                for c in range(CC):
                    ch.step(V.scalar_tensor_tensor(num[:, c, :], kv[:, c, :], first[:, c:c + 1], ap[:, c, 0:T], ALU.mult, ALU.add))
                if search and not tail:
                    decide(b, 1)
                    count()
                ch.join()
                ch.step(V.reciprocal(den, den))
                dve.wait_ge(th_ready, b + 1)
                ch.step(V.scalar_tensor_tensor(num, th, 1.0, num, ALU.add, ALU.mult))
                if tail:
                    choose()
                elif search:
                    decide(b, 2)
                    count()
                ch.join()
                ch.link(V.scalar_tensor_tensor(kv, num, 0.5, den, ALU.mult, ALU.mult))
                V.tensor_copy(y_h[:, :, :], kv).then_inc(y_ready, 1)
                if tail:
                    positions()
                elif search:
                    decide(b, 3)

            def choose():
                dve.wait_ge(tail_psum, 1)
                ch.step(V.tensor_scalar(sgn[:, 4:5], V_[:, 1, 0:1], -1.0, float(CAP), ALU.mult, ALU.add))
                ch.link(V.tensor_copy(sgn[:, 5:6], V_[:, 1, 5:6]))
                ch.link(V.tensor_tensor_scan(eqpre, ones, eq, sgn[:, 5:6], ALU.mult, ALU.add))
                ch.link(V.scalar_tensor_tensor(mt, eqpre, sgn[:, 4:5], eq, ALU.is_le, ALU.mult))
                ch.link(V.tensor_tensor(mask, mt, gt, ALU.add))
                tell(dve, V.tensor_scalar(pre, mask, 1.0, None, ALU.mult, ALU.add, accum_out=cnt[:, 0:1]), tail_cnt, 2)

            def positions():
                dve.wait_ge(tail_psum, 2)
                tell(dve, V.tensor_copy(sgn[:, 6:7], V_[:, 1, 0:1]), total_read, 2 * (NSEQ - 1))
                ch.link(V.tensor_tensor_scan(pre, ones, mask, sgn[:, 6:7], ALU.mult, ALU.add))
                ch.link(V.tensor_tensor(pos, pre, mask, ALU.mult))
                tell(dve, V.tensor_scalar(pos, pos, -1.0, None, ALU.add), tail_cnt, 3)

            def mix1(b, k):
                after(dve, xm2_lo, CC * (b - 1))
                mix(b, x1p[k], u1_ready, shift1, CM1, xm1_h, xm1_ready)

            def ffn_end(b):
                dve.wait_ge(h_used, HF * (b + 1))
                dve.wait_ge(thf_ready, b + 1)
                V.scalar_tensor_tensor(x4T, thf, 1.0, O_[:, :, :], ALU.add, ALU.mult).then_inc(x4_part, 1)

            def ffn_out(b, pair):
                dve.wait_ge(x4tok, b + 1)
                dve.wait_ge(xres_in, 16 * b + 16)
                tell(dve, V.tensor_tensor(obuf.rearrange("p (a j) c -> p a (j c)", a=2), pair[:, :, :],
                                        xres.rearrange("p (a j) c -> p a (j c)", a=2), ALU.add), out_ready, b + 1)

            def residual1(b, k):
                dve.wait_ge(wo_done, b + 1)
                tell(dve, V.tensor_tensor(x2T, V_[:, :, :], x1p[k][:, :, 1:T + 1], ALU.add), x2_ready, b + 1)

            def norm2(b, ffn_before):
                dve.wait_ge(x2tok, b + 1)
                after(dve, z2_ready, b)
                for j in range(TT):
                    ins = V.bn_stats(st2[:, j, :], V_[:, j // 2, (j % 2) * C:(j % 2 + 1) * C])
                ch.link(ins)
                moments(st2, sm[:, 0, :], sm[:, 1, :], sm[:, 2, :], sm[:, 3, :], sm[:, 7, :])
                V.tensor_scalar(sm[:, 4, :], sm[:, 3, :], EPS, None, ALU.add).then_inc(v2_ready, 1)
                if ffn_before:
                    ffn_end(b - 1)
                dve.wait_ge(r2_ready, b + 1)
                tell(dve, V.scalar_tensor_tensor(sm[:, 6, :], sm[:, 0, :], -1.0, sm[:, 5, :], ALU.mult, ALU.mult), ln2_ready, b + 1)

            def threshold():
                ch.link(V.tensor_scalar(sgn[:, 3:4], cand[:, 0:1].bitcast(F32), sgn[:, 1:2], None, ALU.mult))
                ch.step(V.memset(sgn[:, 7:8], 1.0))
                ch.step(V.tensor_scalar(gt, xsel[:, :], sgn[:, 3:4], None, ALU.is_gt, ALU.add, accum_out=cnt[:, 0:1]))
                tell(dve, V.tensor_scalar(eq, xsel[:, :], sgn[:, 3:4], None, ALU.is_equal, ALU.add, accum_out=cnt[:, 1:2]), tail_cnt, 1)

            def mix2(b):
                dve.wait_ge(z2T_done, b + 1)
                tell(dve, V.tensor_scalar(u[:, 1, :], V_[:, 1, :], gain2[:, 1:2], bias2[:, 1:2], ALU.mult, ALU.add), u2_high, b + 1)
                dve.wait_ge(xm1_lo, CC * (b + (1 if last_of(b, NSEQ) else 2)))
                mix(b, x3p, x3_ready, shift2, CM2, xm2_h, xm2_ready)

            def per_token(v):
                return v.rearrange("p (n e) -> p n e", e=E)

            def over_experts(v):
                return v.unsqueeze(2).to_broadcast([P, NT, E])

            ones = sgn[:, 7:8].to_broadcast([P, T])

            def tokens():
                dve.wait_ge(tok_psum, 1)
                ch.link(V.tensor_reduce(smx[:, 0, :], per_token(K_[:, 1, :]), AX.X, ALU.max))
                tell(dve, V.tensor_tensor(per_token(lt), per_token(K_[:, 1, :]), over_experts(smx[:, 0, :]), ALU.subtract), sub_ready, 1)
                dve.wait_ge(tail_psum, 3)
                V.tensor_scalar(mt, K_[:, 0, :], 0.0, None, ALU.is_ge).then_inc(tail_read, 1)
                tell(dve, V.tensor_copy(ph_i, K_[:, 0, :]), tail_read, 2)

            dve.wait_ge(mixing_ready, 1)
            mix1(0, 0)
            clamp(0)
            scan_keys(0)
            wkv(0, False)
            dve.wait_ge(xm1_lo, CC)
            mix1(1, 1)
            residual1(0, 0)
            norm2(0, False)
            clamp(1)
            sign()
            mix2(0)
            scan_keys(1)

            def one(b, k):
                more = not last_of(b, NSEQ)
                wkv(b, True)
                if more:
                    mix1(b + 1, 1 - k)
                residual1(b, k)
                norm2(b, True)
                if more:
                    clamp(b + 1)
                    count()
                else:
                    tokens()
                ffn_out(b - 1, O_)
                mix2(b)
                if more:
                    decide(b, 4)
                    scan_keys(b + 1)

            passes(dve, one, ch)

            ch.step(V.tensor_scalar(pl_i, ph_i, 15, None, ALU.bitwise_and))
            ch.step(V.tensor_copy(per_token(tile_b), over_experts(cst[:, TILE:TILE + NT])))
            ch.link(V.tensor_scalar(ph_i, ph_i, 4, None, ALU.arith_shift_right))
            ch.step(V.tensor_copy(pl, pl_i))
            ch.link(V.tensor_copy(ph, ph_i))
            dve.wait_ge(xm2_lo, CC * NSEQ)
            for l in range(16):
                ch.step(V.tensor_scalar(place[:, 16 + l, :, :], per_token(pl), float(l), None, ALU.is_equal))
            ch.join()
            tiles = tile_b.unsqueeze(1).to_broadcast([P, 16, NT * E])
            tile_place = place[:, 16:32, :, :].rearrange("p k n e -> p k (n e)")
            ch.step(V.tensor_tensor(tile_place, tile_place, tiles, ALU.mult))
            for l in range(16):
                ch.step(V.tensor_scalar(place[:, l, :, :], per_token(pl), float(l), cst[:, PCOL:PCOL + 1], ALU.is_equal, ALU.mult))
                ins = V.tensor_scalar(onehot[:, :, :, l, :], ph.rearrange("p (n g e) -> p n g e", g=2, e=8), float(l), None, ALU.is_equal)
            ins.then_inc(onehots_ready, 1)
            dve.wait_ge(exp_ready, 1)
            ch.link(V.tensor_reduce(smx[:, 1, :], per_token(ex), AX.X, ALU.add))
            ch.link(V.reciprocal(smx[:, 1, :], smx[:, 1, :]))
            ch.link(V.tensor_tensor(per_token(pt), per_token(ex), over_experts(smx[:, 1, :]), ALU.mult))
            ch.link(V.tensor_tensor(pm, pt, mt, ALU.mult))
            ch.link(V.tensor_reduce(smx[:, 2, :], per_token(pm), AX.X, ALU.add))
            ch.link(V.scalar_tensor_tensor(smx[:, 3, :], smx[:, 2, :], 0.0, smx[:, 2, :], ALU.is_equal, ALU.add))
            ch.link(V.reciprocal(smx[:, 3, :], smx[:, 3, :]))
            tell(dve, V.tensor_tensor(per_token(gates[:, :]), per_token(pm), over_experts(smx[:, 3, :]), ALU.mult), gates_ready, 1)
            dve.wait_ge(ids_psum, 1)
            for g in range(2):
                ch.link(V.tensor_tensor(diag, V_[:, g, 0:256].rearrange("p (k e) -> p k e", e=8),
                                        cst[:, DIAG:DIAG + 8].unsqueeze(1).to_broadcast([P, 32, 8]), ALU.mult))
                ch.link(V.tensor_reduce(ids[:, g, :], diag, AX.X, ALU.add))
            tell(dve, V.scalar_tensor_tensor(idf, ids[:, :, 16:32], float(P), ids[:, :, 0:16], ALU.mult, ALU.add), ids_ready, 1)
            dve.wait_ge(idT_psum, 1)
            V.tensor_copy(idx[:, :], V_[:, 0, 0:2 * E]).then_inc(idx_ready, 1)
            ffn_end(NSEQ - 1)

            def split_rows(e, k):
                dve.wait_ge(xeT_ready, e + 1)
                V.tensor_copy(gate[:, k, :], xe[k][:, :, bass.ds(e + C, 1)].rearrange("p h o -> p (h o)"))
                after(dve, fc1_done, 4 * (e - 1))
                tell(dve, V.tensor_copy(xe_h[k], xeT[k]), xeh_ready, e + 1)
                V.tensor_tensor(xe_l[k], xeT[k], xe_h[k].bitcast(F32), ALU.subtract).then_inc(xel_ready, 1)

            def split_hidden(e, fp):
                dve.wait_ge(gelu_done, 4 * e + fp + 1)
                if not first_of(e):
                    dve.wait_ge(fc2_done, 4 * e + fp - 3)
                tell(dve, V.tensor_copy(he_h[fp], he[fp % 2]), heh_ready, 4 * e + fp + 1)
                V.tensor_tensor(he_l[fp], he[fp % 2], he_h[fp].bitcast(F32), ALU.subtract).then_inc(hel_ready, 1)

            def w2_low(e, k):
                dve.wait_ge(w2h_ready, e + 1)
                V.tensor_tensor(w2_l[k], w2[k], w2_h[k].bitcast(F32), ALU.subtract).then_inc(w2l_ready, 1)

            def result(e, k):
                dve.wait_ge(fc2_done, 4 * e + 4)
                dve.wait_ge(b2_in[k], 8 * (e - k) + 16)
                dve.wait_ge(idx_s_ready, e + 1)
                tell(dve, V.tensor_tensor(ye, (R_, O_)[k][:, :, 0:C], b2[k].unsqueeze(1).to_broadcast([P, HALVES, C]), ALU.add),
                     ye_ready, e + 1)
                for h in range(HALVES):
                    ins = V.tensor_scalar(yg[k][:, h, :], ye[:, h, :], gate[:, k, h:h + 1], None, ALU.mult)
                tell(dve, ins, yg_ready, e + 1)

            def slot(e, k):
                more = not last_of(e, E)
                split_hidden(e, 0)
                split_hidden(e, 1)
                if not first_of(e):
                    result(e - 1, 1 - k)
                if more:
                    split_rows(e + 1, 1 - k)
                split_hidden(e, 2)
                if more:
                    w2_low(e + 1, 1 - k)
                split_hidden(e, 3)

            dve.wait_ge(w1h_ready, 1)
            V.tensor_tensor(w1_l[0], w1[0], w1_h[0].bitcast(F32), ALU.subtract).then_inc(w1l_ready, 1)
            split_rows(0, 0)
            w2_low(0, 0)
            ffn_out(NSEQ - 1, R_)
            experts(dve, slot)
            result(E - 1, 1)


def kernel(**inputs):
    import concourse.bacc as bacc
    from concourse.bass_utils import run_bass_kernel_spmd
    A = {k: np.asarray(v) for k, v in inputs.items()}
    a = {k[len("L0_attn_"):]: v for k, v in A.items() if k.startswith("L0_attn_")}
    m = {k[len("L0_ffn_"):]: v for k, v in A.items() if k.startswith("L0_ffn_")}

    def chans(v):
        return v.reshape(CC, P).T

    def stationary(w):
        return w.T.reshape(w.shape[1] // P, P, w.shape[0]).transpose(1, 0, 2)

    params = np.stack([chans(v) for v in (
        a["ln1_g"], a["ln1_b"], a["ln2_g"], a["ln2_b"], a["att_time_mix"], a["att_combined_mix"], a["ffn_time_mix"],
        a["ffn_combined_mix"], a["time_decay"], a["time_first"], m["norm_weight"])], axis=1)
    const = np.zeros((P, NCONST), np.float32)
    r = np.arange(P)
    const[:, IDENT:IDENT + P] = np.eye(P)
    const[:, BLOCK:BLOCK + P] = r[:, None] % E == r[None, :] % E
    const[:, TRI:TRI + P] = (r[:, None] % E == r[None, :] % E) & (r[:, None] // E < r[None, :] // E)
    const[:, PCOL] = r
    n = np.arange(NT)
    const[:, TILE:TILE + NT] = (n % SEG) * TT + n // SEG
    const[:, DIAG:DIAG + 8] = r[:, None] % 8 == np.arange(8)[None, :]
    bits = np.zeros(48, np.int64)
    bits[:MAG_BITS] = 1 << (MAG_BITS - 1 - np.arange(MAG_BITS))
    arrays = {
        "x": A["L0_attn_x"].reshape(N, C),
        "params": params,
        "w_proj": np.stack([stationary(a[k]) for k in ("Wk", "Wv", "Wr", "Wo", "Fr")], axis=1),
        "w_fk": stationary(a["Fk"]),
        "w_fv": stationary(a["Fv"]),
        "router_w": stationary(m["router_weight"]),
        "router_b": m["router_bias"].reshape(E, 1),
        "fc1": m["fc1_weight"].transpose(0, 2, 1).reshape(E, CC, P, F).transpose(0, 2, 1, 3),
        "fc1_b": m["fc1_bias"].reshape(E, FF, P).transpose(2, 0, 1),
        "fc2": m["fc2_weight"].transpose(0, 2, 1).reshape(E, FF, P, C).transpose(0, 2, 1, 3),
        "fc2_b": m["fc2_bias"],
        "const": const,
        "bits_i": np.broadcast_to(bits.astype(np.int32), (P, 48)),
        "bits_f": np.broadcast_to(bits.astype(np.float32), (P, 48)),
    }
    nc = bacc.Bacc("TRN2", target_bir_lowering=False, num_devices=1)
    given, aps = {}, []
    for name, v in arrays.items():
        given[f"in_{name}"] = np.ascontiguousarray(v)
        aps.append(nc.dram_tensor(f"in_{name}", v.shape, mybir.dt.from_np(v.dtype), kind="ExternalInput").ap())
    aps.append(nc.dram_tensor("y", (N, C), F32, kind="ExternalOutput").ap())
    build(nc, *aps)
    got = run_bass_kernel_spmd(nc, [given], core_ids=[0])
    return got.results[0]["y"].reshape(NSEQ, T, C)
```
